# Optimizing a Trainium2 kernel written in Bass

```python
import numpy as np
import jax
import jax.numpy as jnp

def _softmax(x, axis=-1):
    return jax.nn.softmax(x, axis=axis)

def _gelu(x):
    return jax.nn.gelu(x, approximate=True)

def _silu(x):
    return jax.nn.silu(x)

def _sigmoid(x):
    return jax.nn.sigmoid(x)

def _layernorm(x, axis=-1, eps=1e-05):
    m = jnp.mean(x, axis=axis, keepdims=True)
    v = jnp.var(x, axis=axis, keepdims=True)
    return (x - m) / jnp.sqrt(v + eps)

def _scatter_add(tgt, idx, src, axis=0):
    return tgt.at[idx].add(src)

def _segment_sum(src, seg, n):
    return jax.ops.segment_sum(src, seg, n)
kernel_name = 'mk_gnn_ffn_d2_gnn_r8_bfb73e'

def setup_inputs(seed: int=0):
    np.random.seed(seed)
    _w = jnp.asarray

    def _rec_inputs():
        import jax
        import jax.numpy as jnp
        _gk = jax.random.key(seed)
        x = -0.0003713 + 1 * jax.random.normal(jax.random.fold_in(_gk, 1), (6250, 256), jnp.float32)
        src = jax.random.randint(jax.random.fold_in(_gk, 2), (100000,), 0, 6250, jnp.int32)
        dst = jax.random.randint(jax.random.fold_in(_gk, 3), (100000,), 0, 6250, jnp.int32)
        _o = jnp.argsort(dst, stable=True)
        src = src[_o]
        dst = dst[_o]
        edge_attr_64 = 0.000189758 + 1.00013 * jax.random.normal(jax.random.fold_in(_gk, 13), (100000, 64), jnp.float32)
        edge_weight = jax.random.uniform(jax.random.fold_in(_gk, 15), (100000,), jnp.float32, 0.0, 1)
        return (x, src, dst, edge_attr_64, edge_weight)
    x, src, dst, edge_attr_64, edge_weight = _rec_inputs()

    def _L0_gnn_setup():
        import jax, jax.numpy as jnp
        import numpy as np
        N_NODES = 6250
        N_EDGES = 100000
        NODE_IN = 256
        EDGE_OUT = 64
        GLOBAL_IN = 128
        NODE_OUT = 256
        HIDDEN = 512
        N_GRAPHS = 64
        key = jax.random.key(seed)
        ks = jax.random.split(key, 8)
        x = jax.random.normal(ks[0], (N_NODES, NODE_IN), dtype=jnp.float32)
        edge_index = jax.random.randint(ks[1], (2, N_EDGES), 0, N_NODES, dtype=jnp.int64)
        edge_attr = jax.random.normal(ks[2], (N_EDGES, EDGE_OUT), dtype=jnp.float32)
        u = jax.random.normal(ks[3], (N_GRAPHS, GLOBAL_IN), dtype=jnp.float32)
        batch = jnp.sort(jax.random.randint(ks[4], (N_NODES,), 0, N_GRAPHS, dtype=jnp.int64))
        in_dim = NODE_IN + EDGE_OUT + GLOBAL_IN
        b1s = 1.0 / np.sqrt(in_dim)
        b2s = 1.0 / np.sqrt(HIDDEN)
        W1 = jax.random.uniform(ks[5], (in_dim, HIDDEN), dtype=jnp.float32, minval=-b1s, maxval=b1s)
        b1 = jnp.zeros((HIDDEN,), dtype=jnp.float32)
        W2 = jax.random.uniform(ks[6], (HIDDEN, NODE_OUT), dtype=jnp.float32, minval=-b2s, maxval=b2s)
        b2 = jnp.zeros((NODE_OUT,), dtype=jnp.float32)
        return {'x': x, 'edge_index': edge_index, 'edge_attr': edge_attr, 'u': u, 'batch': batch, 'W1': W1, 'b1': b1, 'W2': W2, 'b2': b2}
    _L0_gnn_all = _L0_gnn_setup()
    _L0_gnn_in = {k: v for k, v in _L0_gnn_all.items() if k in ('u', 'W1', 'b1', 'W2', 'b2')}
    del _L0_gnn_all

    def _L0_ffn_setup():
        import jax, jax.numpy as jnp
        import numpy as np
        BN_EPS = 0.001

        def _bn(h, g, b, m, v):
            return g * (h - m) * jax.lax.rsqrt(v + BN_EPS) + b
        key = jax.random.key(seed)
        ks = jax.random.split(key, 8)
        B, F, Df = (256, 64, 256)
        E, H, D = (8, 256, 256)
        s1 = 1.0 / np.sqrt(Df)
        s2 = 1.0 / np.sqrt(H)
        return {'x': jax.random.normal(ks[0], (B, F, Df), jnp.float32), 'Wr': jax.random.normal(ks[1], (Df, E), jnp.float32) * s1, 'br': jnp.zeros((E,), jnp.float32), 'W1': jax.random.normal(ks[2], (E, Df, H), jnp.float32) * s1, 'b1': jnp.zeros((E, H), jnp.float32), 'g1': jnp.ones((E, H), jnp.float32), 'be1': jnp.zeros((E, H), jnp.float32), 'm1': jnp.zeros((E, H), jnp.float32), 'v1': jnp.ones((E, H), jnp.float32), 'W2': jax.random.normal(ks[3], (E, H, H), jnp.float32) * s2, 'b2': jnp.zeros((E, H), jnp.float32), 'g2': jnp.ones((E, H), jnp.float32), 'be2': jnp.zeros((E, H), jnp.float32), 'm2': jnp.zeros((E, H), jnp.float32), 'v2': jnp.ones((E, H), jnp.float32), 'Wo': jax.random.normal(ks[4], (E, H, D), jnp.float32) * s2, 'bo': jnp.zeros((E, D), jnp.float32)}
    _L0_ffn_all = _L0_ffn_setup()
    _L0_ffn_in = {k: v for k, v in _L0_ffn_all.items() if k in ('Wr', 'br', 'W1', 'b1', 'g1', 'be1', 'm1', 'v1', 'W2', 'b2', 'g2', 'be2', 'm2', 'v2', 'Wo', 'bo')}
    del _L0_ffn_all

    def _L1_gnn_setup():
        import jax, jax.numpy as jnp
        import numpy as np
        BN_EPS = 1e-05
        IDX = np.array([[0, 1, 2, 3, 4, 5, 6, 7], [1, 0, 3, 2, 5, 4, 7, 6], [2, 3, 0, 1, 6, 7, 4, 5], [3, 2, 1, 0, 7, 6, 5, 4], [4, 5, 6, 7, 0, 1, 2, 3], [5, 4, 7, 6, 1, 0, 3, 2], [6, 7, 4, 5, 2, 3, 0, 1], [7, 6, 5, 4, 3, 2, 1, 0]], dtype=np.int32)
        SIGN = np.array([[1, 1, 1, 1, 1, 1, 1, 1], [1, -1, 1, -1, 1, -1, -1, 1], [1, -1, -1, 1, 1, 1, -1, -1], [1, 1, -1, -1, 1, -1, 1, -1], [1, -1, -1, -1, -1, 1, 1, 1], [1, 1, -1, 1, -1, -1, -1, 1], [1, 1, 1, -1, -1, 1, -1, -1], [1, -1, 1, 1, -1, -1, 1, -1]], dtype=np.float32)

        def make_octonion_mul(kernel):
            in8, out = kernel.shape
            out8 = out // 8
            a = kernel.reshape(in8, 8, out8).transpose(1, 0, 2)
            blocks = jnp.asarray(SIGN)[:, :, None, None] * a[jnp.asarray(IDX)]
            return jnp.transpose(blocks, (1, 2, 0, 3)).reshape(8 * in8, out)
        key = jax.random.key(seed)
        ks = jax.random.split(key, 5)
        N, E, D_IN, D_OUT = (12500, 400000, 256, 256)
        stdv = float(np.sqrt(6.0 / (D_IN // 8 + D_OUT)))
        return {'x': jax.random.normal(ks[0], (N, D_IN), dtype=jnp.float32), 'weight': jax.random.uniform(ks[1], (D_IN // 8, D_OUT), dtype=jnp.float32, minval=-stdv, maxval=stdv), 'gamma': jnp.ones((D_OUT,), dtype=jnp.float32), 'beta': jnp.zeros((D_OUT,), dtype=jnp.float32), 'edge_weight': jax.random.uniform(ks[2], (E,), dtype=jnp.float32), 'edge_src': jax.random.randint(ks[3], (E,), 0, N, dtype=jnp.int32), 'edge_dst': jax.random.randint(ks[4], (E,), 0, N, dtype=jnp.int32)}
    _L1_gnn_all = _L1_gnn_setup()
    _L1_gnn_in = {k: v for k, v in _L1_gnn_all.items() if k in ('weight', 'gamma', 'beta')}
    del _L1_gnn_all

    def _L1_ffn_setup():
        import jax, jax.numpy as jnp
        import numpy as np
        B, N, D = (16, 512, 256)
        NUM_EXPERTS, TOP_K, HEADS = (4, 2, 4)
        N_EDGES = 131072
        LN_EPS = 1e-05

        def _layernorm(x, g, b):
            mu = x.mean(-1, keepdims=True)
            var = ((x - mu) ** 2).mean(-1, keepdims=True)
            return (x - mu) * jax.lax.rsqrt(var + LN_EPS) * g + b

        def _forward(x, edge_index, W_gat, att_src, att_dst, b_gat, ln_gamma, ln_beta, W1, b1, W2, b2):
            Bc, Nc, Dc = x.shape
            M = Bc * Nc
            x_flat = x.reshape(M, Dc)
            h = (x_flat @ W_gat).reshape(M, HEADS, NUM_EXPERTS)
            loops = jnp.arange(M, dtype=edge_index.dtype)
            src = jnp.concatenate([edge_index[0], loops])
            dst = jnp.concatenate([edge_index[1], loops])
            a_src = (h * att_src).sum(-1)
            a_dst = (h * att_dst).sum(-1)
            e = jax.nn.leaky_relu(a_src[src] + a_dst[dst], negative_slope=0.2)
            e_max = jax.ops.segment_max(e, dst, num_segments=M)
            ee = jnp.exp(e - e_max[dst])
            denom = jax.ops.segment_sum(ee, dst, num_segments=M)
            alpha = ee / (denom[dst] + 1e-16)
            msg = h[src] * alpha[:, :, None]
            agg = jax.ops.segment_sum(msg, dst, num_segments=M).reshape(M, HEADS * NUM_EXPERTS) + b_gat
            scores = _layernorm(agg, ln_gamma, ln_beta).reshape(M, HEADS, NUM_EXPERTS).mean(1)
            scores = scores.reshape(Bc, Nc, NUM_EXPERTS)
            topk_s, topk_i = jax.lax.top_k(scores, TOP_K)
            w = jax.nn.softmax(topk_s, axis=-1)
            out = jnp.zeros_like(x)
            for ei in range(NUM_EXPERTS):
                g = jnp.where(topk_i == ei, w, 0.0).sum(-1)
                hh = jax.nn.gelu(x @ W1[ei] + b1[ei], approximate=False)
                out = out + g[..., None] * (hh @ W2[ei] + b2[ei])
            return out
        key = jax.random.key(seed)
        ks = jax.random.split(key, 8)
        s = 0.05
        return {'x': jax.random.normal(ks[0], (B, N, D), jnp.float32), 'W_gat': jax.random.normal(ks[1], (D, HEADS * NUM_EXPERTS), jnp.float32) * s, 'att_src': jax.random.normal(ks[2], (HEADS, NUM_EXPERTS), jnp.float32) * s, 'att_dst': jax.random.normal(ks[3], (HEADS, NUM_EXPERTS), jnp.float32) * s, 'b_gat': jnp.zeros((HEADS * NUM_EXPERTS,), jnp.float32), 'ln_gamma': jnp.ones((HEADS * NUM_EXPERTS,), jnp.float32), 'ln_beta': jnp.zeros((HEADS * NUM_EXPERTS,), jnp.float32), 'W1': jax.random.normal(ks[4], (NUM_EXPERTS, D, 2 * D), jnp.float32) * s, 'b1': jnp.zeros((NUM_EXPERTS, 2 * D), jnp.float32), 'W2': jax.random.normal(ks[5], (NUM_EXPERTS, 2 * D, D), jnp.float32) * s, 'b2': jnp.zeros((NUM_EXPERTS, D), jnp.float32), 'edge_index': jax.random.randint(ks[6], (2, N_EDGES), 0, B * N, jnp.int32)}
    _L1_ffn_all = _L1_ffn_setup()
    _L1_ffn_in = {k: v for k, v in _L1_ffn_all.items() if k in ('W_gat', 'att_src', 'att_dst', 'b_gat', 'ln_gamma', 'ln_beta', 'W1', 'b1', 'W2', 'b2', 'edge_index')}
    del _L1_ffn_all
    return {'x': x, 'src': src, 'dst': dst, 'edge_attr_64': edge_attr_64, 'edge_weight': edge_weight, 'L0_gnn_u': _L0_gnn_in['u'], 'L0_gnn_W1': _L0_gnn_in['W1'], 'L0_gnn_b1': _L0_gnn_in['b1'], 'L0_gnn_W2': _L0_gnn_in['W2'], 'L0_gnn_b2': _L0_gnn_in['b2'], 'L0_ffn_Wr': _L0_ffn_in['Wr'], 'L0_ffn_br': _L0_ffn_in['br'], 'L0_ffn_W1': _L0_ffn_in['W1'], 'L0_ffn_b1': _L0_ffn_in['b1'], 'L0_ffn_g1': _L0_ffn_in['g1'], 'L0_ffn_be1': _L0_ffn_in['be1'], 'L0_ffn_m1': _L0_ffn_in['m1'], 'L0_ffn_v1': _L0_ffn_in['v1'], 'L0_ffn_W2': _L0_ffn_in['W2'], 'L0_ffn_b2': _L0_ffn_in['b2'], 'L0_ffn_g2': _L0_ffn_in['g2'], 'L0_ffn_be2': _L0_ffn_in['be2'], 'L0_ffn_m2': _L0_ffn_in['m2'], 'L0_ffn_v2': _L0_ffn_in['v2'], 'L0_ffn_Wo': _L0_ffn_in['Wo'], 'L0_ffn_bo': _L0_ffn_in['bo'], 'L1_gnn_weight': _L1_gnn_in['weight'], 'L1_gnn_gamma': _L1_gnn_in['gamma'], 'L1_gnn_beta': _L1_gnn_in['beta'], 'L1_ffn_W_gat': _L1_ffn_in['W_gat'], 'L1_ffn_att_src': _L1_ffn_in['att_src'], 'L1_ffn_att_dst': _L1_ffn_in['att_dst'], 'L1_ffn_b_gat': _L1_ffn_in['b_gat'], 'L1_ffn_ln_gamma': _L1_ffn_in['ln_gamma'], 'L1_ffn_ln_beta': _L1_ffn_in['ln_beta'], 'L1_ffn_W1': _L1_ffn_in['W1'], 'L1_ffn_b1': _L1_ffn_in['b1'], 'L1_ffn_W2': _L1_ffn_in['W2'], 'L1_ffn_b2': _L1_ffn_in['b2'], 'L1_ffn_edge_index': _L1_ffn_in['edge_index']}

def reference(x, src, dst, edge_attr_64, edge_weight, L0_gnn_u, L0_gnn_W1, L0_gnn_b1, L0_gnn_W2, L0_gnn_b2, L0_ffn_Wr, L0_ffn_br, L0_ffn_W1, L0_ffn_b1, L0_ffn_g1, L0_ffn_be1, L0_ffn_m1, L0_ffn_v1, L0_ffn_W2, L0_ffn_b2, L0_ffn_g2, L0_ffn_be2, L0_ffn_m2, L0_ffn_v2, L0_ffn_Wo, L0_ffn_bo, L1_gnn_weight, L1_gnn_gamma, L1_gnn_beta, L1_ffn_W_gat, L1_ffn_att_src, L1_ffn_att_dst, L1_ffn_b_gat, L1_ffn_ln_gamma, L1_ffn_ln_beta, L1_ffn_W1, L1_ffn_b1, L1_ffn_W2, L1_ffn_b2, L1_ffn_edge_index):
    import jax
    import jax.numpy as jnp

    def _L0_gnn_ref(x, edge_index, edge_attr, u, batch, W1, b1, W2, b2):
        import jax, jax.numpy as jnp
        import numpy as np
        N_NODES = 6250
        N_EDGES = 100000
        NODE_IN = 256
        EDGE_OUT = 64
        GLOBAL_IN = 128
        NODE_OUT = 256
        HIDDEN = 512
        N_GRAPHS = 64
        n = x.shape[0]
        src = edge_index[0]
        sums = jax.ops.segment_sum(edge_attr, src, num_segments=n)
        counts = jax.ops.segment_sum(jnp.ones((edge_attr.shape[0],), edge_attr.dtype), src, num_segments=n)
        edge_attr_agg = sums / jnp.maximum(counts, 1.0)[:, None]
        u_expanded = u[batch]
        combined = jnp.concatenate([x, edge_attr_agg, u_expanded], axis=1)
        h = jax.nn.relu(combined @ W1 + b1)
        return h @ W2 + b2

    def _L0_ffn_ref(x, Wr, br, W1, b1, g1, be1, m1, v1, W2, b2, g2, be2, m2, v2, Wo, bo):
        import jax, jax.numpy as jnp
        import numpy as np
        BN_EPS = 0.001

        def _bn(h, g, b, m, v):
            return g * (h - m) * jax.lax.rsqrt(v + BN_EPS) + b
        feat = jnp.mean(x, axis=0)
        w = jax.nn.softmax(feat @ Wr + br, axis=-1)
        h = jnp.einsum('bfd,edh->bfeh', x, W1) + b1
        h = jax.nn.relu(_bn(h, g1, be1, m1, v1))
        h = jnp.einsum('bfeh,ehk->bfek', h, W2) + b2
        h = jax.nn.relu(_bn(h, g2, be2, m2, v2))
        y = jnp.einsum('bfeh,ehd->bfed', h, Wo) + bo
        return jnp.einsum('bfed,fe->bfd', y, w)

    def _L1_gnn_ref(x, weight, gamma, beta, edge_weight, edge_src, edge_dst):
        import jax, jax.numpy as jnp
        import numpy as np
        BN_EPS = 1e-05
        IDX = np.array([[0, 1, 2, 3, 4, 5, 6, 7], [1, 0, 3, 2, 5, 4, 7, 6], [2, 3, 0, 1, 6, 7, 4, 5], [3, 2, 1, 0, 7, 6, 5, 4], [4, 5, 6, 7, 0, 1, 2, 3], [5, 4, 7, 6, 1, 0, 3, 2], [6, 7, 4, 5, 2, 3, 0, 1], [7, 6, 5, 4, 3, 2, 1, 0]], dtype=np.int32)
        SIGN = np.array([[1, 1, 1, 1, 1, 1, 1, 1], [1, -1, 1, -1, 1, -1, -1, 1], [1, -1, -1, 1, 1, 1, -1, -1], [1, 1, -1, -1, 1, -1, 1, -1], [1, -1, -1, -1, -1, 1, 1, 1], [1, 1, -1, 1, -1, -1, -1, 1], [1, 1, 1, -1, -1, 1, -1, -1], [1, -1, 1, 1, -1, -1, 1, -1]], dtype=np.float32)

        def make_octonion_mul(kernel):
            in8, out = kernel.shape
            out8 = out // 8
            a = kernel.reshape(in8, 8, out8).transpose(1, 0, 2)
            blocks = jnp.asarray(SIGN)[:, :, None, None] * a[jnp.asarray(IDX)]
            return jnp.transpose(blocks, (1, 2, 0, 3)).reshape(8 * in8, out)
        N = x.shape[0]
        hamilton = make_octonion_mul(weight)
        support = x @ hamilton
        msgs = edge_weight[:, None] * support[edge_src]
        out = jax.ops.segment_sum(msgs, edge_dst, num_segments=N)
        mean = jnp.mean(out, axis=0)
        var = jnp.var(out, axis=0)
        out = (out - mean) * jax.lax.rsqrt(var + BN_EPS) * gamma + beta
        return jnp.tanh(out)

    def _L1_ffn_ref(x, W_gat, att_src, att_dst, b_gat, ln_gamma, ln_beta, W1, b1, W2, b2, edge_index):
        import jax, jax.numpy as jnp
        import numpy as np
        B, N, D = (16, 512, 256)
        NUM_EXPERTS, TOP_K, HEADS = (4, 2, 4)
        N_EDGES = 131072
        LN_EPS = 1e-05

        def _layernorm(x, g, b):
            mu = x.mean(-1, keepdims=True)
            var = ((x - mu) ** 2).mean(-1, keepdims=True)
            return (x - mu) * jax.lax.rsqrt(var + LN_EPS) * g + b

        def _forward(x, edge_index, W_gat, att_src, att_dst, b_gat, ln_gamma, ln_beta, W1, b1, W2, b2):
            Bc, Nc, Dc = x.shape
            M = Bc * Nc
            x_flat = x.reshape(M, Dc)
            h = (x_flat @ W_gat).reshape(M, HEADS, NUM_EXPERTS)
            loops = jnp.arange(M, dtype=edge_index.dtype)
            src = jnp.concatenate([edge_index[0], loops])
            dst = jnp.concatenate([edge_index[1], loops])
            a_src = (h * att_src).sum(-1)
            a_dst = (h * att_dst).sum(-1)
            e = jax.nn.leaky_relu(a_src[src] + a_dst[dst], negative_slope=0.2)
            e_max = jax.ops.segment_max(e, dst, num_segments=M)
            ee = jnp.exp(e - e_max[dst])
            denom = jax.ops.segment_sum(ee, dst, num_segments=M)
            alpha = ee / (denom[dst] + 1e-16)
            msg = h[src] * alpha[:, :, None]
            agg = jax.ops.segment_sum(msg, dst, num_segments=M).reshape(M, HEADS * NUM_EXPERTS) + b_gat
            scores = _layernorm(agg, ln_gamma, ln_beta).reshape(M, HEADS, NUM_EXPERTS).mean(1)
            scores = scores.reshape(Bc, Nc, NUM_EXPERTS)
            topk_s, topk_i = jax.lax.top_k(scores, TOP_K)
            w = jax.nn.softmax(topk_s, axis=-1)
            out = jnp.zeros_like(x)
            for ei in range(NUM_EXPERTS):
                g = jnp.where(topk_i == ei, w, 0.0).sum(-1)
                hh = jax.nn.gelu(x @ W1[ei] + b1[ei], approximate=False)
                out = out + g[..., None] * (hh @ W2[ei] + b2[ei])
            return out
        return _forward(x, edge_index, W_gat, att_src, att_dst, b_gat, ln_gamma, ln_beta, W1, b1, W2, b2)
    edge_index = jnp.stack([src, dst])
    batch0 = jnp.zeros((6250,), jnp.int32)
    x = x + _L0_gnn_ref(_layernorm(x, axis=-1), edge_index, edge_attr_64, L0_gnn_u, batch0, L0_gnn_W1, L0_gnn_b1, L0_gnn_W2, L0_gnn_b2)
    x = x + _L0_ffn_ref(_layernorm(x, axis=-1)[None], L0_ffn_Wr, L0_ffn_br, L0_ffn_W1, L0_ffn_b1, L0_ffn_g1, L0_ffn_be1, L0_ffn_m1, L0_ffn_v1, L0_ffn_W2, L0_ffn_b2, L0_ffn_g2, L0_ffn_be2, L0_ffn_m2, L0_ffn_v2, L0_ffn_Wo, L0_ffn_bo)[0]
    x = x + _L1_gnn_ref(_layernorm(x, axis=-1), L1_gnn_weight, L1_gnn_gamma, L1_gnn_beta, edge_weight, src, dst)
    x = x + _L1_ffn_ref(_layernorm(x, axis=-1)[None], L1_ffn_W_gat, L1_ffn_att_src, L1_ffn_att_dst, L1_ffn_b_gat, L1_ffn_ln_gamma, L1_ffn_ln_beta, L1_ffn_W1, L1_ffn_b1, L1_ffn_W2, L1_ffn_b2, L1_ffn_edge_index)[0]
    return x

_drawn_inputs = setup_inputs


def setup_inputs(seed=0):
    import zlib

    import numpy as np

    out = dict(_drawn_inputs(seed))
    spreads = {'L0_gnn_b1': (0.0, 0.1),
     'L0_gnn_b2': (0.0, 0.1),
     'L0_ffn_br': (0.0, 0.1),
     'L0_ffn_b1': (0.0, 0.272),
     'L0_ffn_g1': (1.0, 0.2),
     'L0_ffn_be1': (0.0, 0.283),
     'L0_ffn_m1': (0.0, 0.1),
     'L0_ffn_v1': (1.0, 0.2),
     'L0_ffn_b2': (0.0, 0.1),
     'L0_ffn_g2': (1.0, 0.2),
     'L0_ffn_be2': (0.0, 0.1),
     'L0_ffn_m2': (0.0, 0.1),
     'L0_ffn_v2': (1.0, 0.2),
     'L0_ffn_bo': (0.0, 0.1),
     'L1_gnn_gamma': (1.0, 0.2),
     'L1_gnn_beta': (0.0, 0.1),
     'L1_ffn_b_gat': (0.0, 0.1),
     'L1_ffn_ln_gamma': (1.0, 0.2),
     'L1_ffn_ln_beta': (0.0, 0.1),
     'L1_ffn_b1': (0.0, 0.1),
     'L1_ffn_b2': (0.0, 0.1)}
    factors = {'L1_ffn_att_dst': 4.587}
    for name, (base, spread) in spreads.items():
        noise = np.random.default_rng([zlib.crc32(name.encode()), seed]).standard_normal(out[name].shape)
        drawn = base * np.exp(spread * noise) if base else spread * noise
        out[name] = jnp.asarray(drawn.astype(out[name].dtype))
    for name, factor in factors.items():
        out[name] = (out[name] * factor).astype(out[name].dtype)
    return out
```

```python
from contextlib import ExitStack

import concourse.bass as bass
from concourse import mybir

F32 = mybir.dt.float32
I32 = mybir.dt.int32
ALU = mybir.AluOpType
ACT = mybir.ActivationFunctionType
AX = mybir.AxisListType.X
DVE_ONLY = (mybir.EngineType.DVE,)
PE_ONLY = (mybir.EngineType.PE,)

P = 128
LN_EPS = 1e-5
BN_EPS_EXPERTS = 1e-3
BN_EPS_GRAPH = 1e-5
SIGN = [[1, 1, 1, 1, 1, 1, 1, 1], [1, -1, 1, -1, 1, -1, -1, 1], [1, -1, -1, 1, 1, 1, -1, -1],
        [1, 1, -1, -1, 1, -1, 1, -1], [1, -1, -1, -1, -1, 1, 1, 1], [1, 1, -1, 1, -1, -1, -1, 1],
        [1, 1, 1, -1, -1, 1, -1, -1], [1, -1, 1, 1, -1, -1, 1, -1]]
SELF_REACH = 80.0


def most(n):
    return max(p for p in range(1, P + 1) if n % p == 0)


class Graph:

    def __init__(self, edges, keys, unroll):
        self.parts = most(edges)
        self.cols = edges // self.parts
        self.buckets = -(-keys // P)
        chunks = (edges + self.buckets * (P - 1)) // P
        self.chunks = -(-chunks // unroll) * unroll


class Count:

    def __init__(self, sem):
        self.sem, self.base, self.k, self.turn, self.per = sem, 0, 0, None, 0

    def add(self, instruction, n=1):
        instruction.then_inc(self.sem, n)
        self.k += n

    @property
    def value(self):
        v = self.base + self.k
        return v if self.turn is None else self.turn * self.per + v

    def enter(self, turn, per):
        self.base, self.k, self.turn, self.per = self.base + self.k, 0, turn, per

    def leave(self, turns):
        assert self.k == self.per, (self.k, self.per)
        self.base, self.k, self.turn = self.base + turns * self.per, 0, None


def build(nc, t, out):
    N, D = t["x"].shape
    E0 = t["src"].shape[0]
    E2 = t["L1_ffn_edge_index"].shape[1]
    EA = t["edge_attr_64"].shape[1]
    NX, _, H1 = t["L0_ffn_W1"].shape
    GH = t["L0_gnn_W1"].shape[1]
    NE, _, H2 = t["L1_ffn_W1"].shape
    HEADS = t["L1_ffn_att_src"].shape[0]
    HK = t["L1_ffn_W_gat"].shape[1]
    TG = 4
    TILES = -(-N // P)
    GROUPS = -(-TILES // TG)
    TPAD = GROUPS * TG
    W = TG * P
    TAIL = N - (TILES - 1) * P
    KD, KG, KF = D // P, GH // P, H2 // P
    A0 = EA + 2
    GW = HEADS + HK
    PB = 512 // GW
    SC = 8
    SS = 16
    R1, R2 = 3, 2
    g0 = Graph(E0, N, 2 * SC)
    g1 = Graph(E0, N, 2 * SC)
    g2 = Graph(E2, 8192, 2 * SC)
    graphs = (g0, g1, g2)
    TMAX = max(g.cols for g in graphs)
    CMAX = max(g.chunks for g in graphs)
    ITERS = [g.cols // (2 * SS) for g in graphs]
    C0, C1, C2 = (g.chunks // (2 * SC) for g in graphs)
    FILL = [2 * SC, 64, 64]
    FILLS = [g.chunks // f for g, f in zip(graphs, FILL)]
    for g, n, f, fs in zip(graphs, ITERS, FILL, FILLS):
        assert n * 2 * SS == g.cols and f * fs == g.chunks
    Q = NX * KD
    HP, YP = KG + NX * 2 * KD, 4 + 2 * NX

    ctx = ExitStack()
    with ctx:
        def sb(name, shape, dt=F32):
            return ctx.enter_context(nc.sbuf_tensor(name, shape, dt))

        def sem(name):
            return ctx.enter_context(nc.semaphore(name))

        def pair(name):
            return [sem(f"{name}_a"), sem(f"{name}_b")]

        rec0 = nc.dram_tensor("rec0", [P * g0.chunks, A0], F32)
        rec1 = nc.dram_tensor("rec1", [P * g1.chunks, R1], I32)
        rec2 = nc.dram_tensor("rec2", [P * g2.chunks, R2], I32)
        slot_d = [nc.dram_tensor(f"slots{n}", [g.parts, g.cols], I32) for n, g in enumerate(graphs)]
        pay_d = [None, nc.dram_tensor("pay1", [g1.parts, g1.cols * R1], I32),
                 nc.dram_tensor("pay2", [g2.parts, g2.cols * R2], I32)]
        xl_d = nc.dram_tensor("xl", [TPAD * P, D], F32)
        gat_d = nc.dram_tensor("gat", [TPAD * P, GW], F32)

        class Region:
            def __init__(self, name, size):
                self.ap, self.size, self.at = sb(name, [P, size])[:], size, 0

            def restart(self, at=0):
                self.at = at

            def take(self, *shape, rows=P, dt=F32):
                n = 1
                for k in shape:
                    n *= k
                a = self.ap[0:rows, self.at:self.at + n]
                self.at += n
                assert self.at <= self.size
                if dt is not F32:
                    a = a.bitcast(dt)
                if len(shape) == 2:
                    a = a.rearrange("p (a b) -> p a b", a=shape[0])
                if len(shape) == 3:
                    a = a.rearrange("p (a b c) -> p a b c", a=shape[0], b=shape[1])
                return a

        rX = Region("rX", TPAD * D)
        X = rX.take(TPAD, D)
        rX.restart()
        key = [rX.take(TMAX, dt=I32) for _ in graphs]
        sloti = [rX.take(TMAX, dt=I32) for _ in graphs]
        hi, mask = rX.take(TMAX, dt=I32), rX.take(TMAX, dt=I32)
        lo, cum, slotf, zeros = (rX.take(TMAX) for _ in range(4))
        rB = Region("rB", KD * TPAD * P)
        big = rB.take(KD, TPAD * P)
        rB.restart()
        EW1, EW2, EWo = (rB.take(NX, KD, H1) for _ in range(3))
        attr = rB.take(TG, EA)
        bo = rB.take(D, rows=NX)
        gb2r = rB.take(D, rows=1)
        brr = rB.take(NX, rows=1)
        wr = rB.take(KD, NX)
        rS = Region("rS", NE * KD * H2 + NE * KF * D)
        ew, srcs = rS.take(TMAX), rS.take(TMAX, dt=I32)
        ends = rS.take(CMAX)
        py1, py2 = rS.take(g1.cols, R1), rS.take(g2.cols, R2)
        rS.restart()
        acc0 = rS.take(TPAD, A0)
        oring = rS.take(2 * SC, A0)
        rS.restart()
        FW1, FW2 = rS.take(NE, KD, H2), rS.take(NE, KF, D)
        rH = Region("rH", 8 * W)
        HB = rH.take(8, W)
        rH.restart()
        iota_c, brow, brow2 = rH.take(CMAX), rH.take(CMAX), rH.take(CMAX)
        gw1u = rH.take(GH)
        empty1, empty2 = rH.take(FILL[1], R1), rH.take(FILL[2], R2)
        rH.restart()
        rows1 = rH.take(2 * SC, D)
        rG = Region("rG", 3328)
        gw1, gw2, gw1e = rG.take(KD, GH), rG.take(KG, D), rG.take(GH, rows=EA)
        rG.restart()
        G, nd = rG.take(TPAD, GW), rG.take(g2.buckets, 2 * HEADS)
        sums, t16 = rG.take(TILES, GW), rG.take(TILES, HK)
        rD = Region("rD", 3 * TG * D)
        aring = rD.take(2, SS, A0)
        rD.restart()
        xln, xl3, xT = rD.take(TG, D), rD.take(TG, D), rD.take(KD, W)
        rD.restart()
        ohT = rD.take(2 * SC, P)
        r2, v2, ev = rD.take(2, SC * GW), rD.take(2, SC * GW), rD.take(2, SC * HEADS)
        rO = Region("rO", 2 * SC * P)
        oh = rO.take(2 * SC, P)
        rO.restart()
        lo0, prow, wrep = rO.take(g0.cols), rO.take(3, P), rO.take(D)
        rA = Region("rA", 2 * W)
        attrT, gateT = rA.take(W, rows=EA), rA.take(W, rows=NX)
        rA.restart()
        fb2r = rA.take(NE, D, rows=1)
        rE = Region("rE", (3 * HEADS + NE) * TPAD)
        before, upto = rE.take(P), rE.take(P)
        nrep, cnt, base = rE.take(P), rE.take(64), rE.take(64)
        rE.restart()
        tmp, gates = [rE.take(TPAD, HEADS) for _ in range(3)], rE.take(TPAD, NE)
        iota = sb("iota", [P, P])
        zero = rO.ap[:, 2 * SC * P - 512:2 * SC * P]
        ident = sb("ident", [P, P])
        ones = sb("ones", [P, P])
        nch = sb("nch", [64, 3])
        nchi = sb("nchi", [64, 1], I32)
        offs = sb("offs", [P, CMAX], I32)
        off0, off1, off2n, off2s = (offs[32 * q:32 * q + 1, 0:g.chunks] for q, g in enumerate((g0, g1, g2, g2)))
        pcol = sb("pcol", [P, 3, P])
        bnf = sb("bnf", [P, 2, 2, Q])
        gb1 = sb("gb1", [P, KG])
        ham = sb("ham", [P, KD, D])
        wg = sb("wg", [P, KD, HK])
        att = sb("att", [P, 5, HK])
        root_in = sb("root_in", [P, Q])
        root_part = sb("root_part", [P, Q])
        lnst = sb("lnst", [P, TG, 6])
        lnmv = sb("lnmv", [P, TG, 2])
        rstd = sb("rstd", [P, TG])
        cmx = sb("cmx", [P, TG])
        gate = sb("gate", [P, TG, NX])
        gmx = sb("gmx", [P, TG])
        gsm = sb("gsm", [P, TG])
        iring = sb("iring", [P, 2, SS], I32)
        pring = sb("pring", [P, 2, SS * R1], I32)
        mring = sb("mring", [P, 2, SC * R1], I32)
        bst = sb("bst", [P, KD, GROUPS, 6])
        bmv = sb("bmv", [P, KD, 2])
        bsc = sb("bsc", [P, KD, 2])
        roots = sb("roots", [P, 3, TPAD])
        hat = sb("hat", [P, TG, HK])
        gmax = sb("gmax", [P, HEADS])
        gm4 = sb("gm4", [HEADS, 1 + HEADS])
        es = sb("es", [P, TPAD, HEADS])

        bank = [ctx.enter_context(nc.psum_tensor(f"bank{n}", [P, 512], F32))[:] for n in range(6)]
        sumbank = ctx.enter_context(nc.psum_tensor("sumbank", [P, 2 * 512], F32))[:]
        bank += [sumbank[:, 512 * n:512 * (n + 1)] for n in range(2)]
        assert TILES < 2 * PB

        def tiles(i, j=0, n=TG):
            return bass.ds(i * TG + j, n)

        def tile(x, i, j):
            return x[:, tiles(i, j, 1), :].rearrange("p a d -> p (a d)")

        empty0 = rB.ap[:, 0:FILL[0] * A0].rearrange("p (c w) -> p c w", w=A0)
        empty0f = rB.ap[:, 0:FILL[0] * A0]
        zero_l, zero_r = zero[:, 0:P], zero[:]

        by_k = lambda a: a.rearrange("(k p) n -> p k n", p=P)
        row = lambda a: a.rearrange("(a n) -> a n", a=1)
        experts = lambda a: a.rearrange("e (k p) n -> p e k n", p=P)
        gW1 = t["L0_gnn_W1"]
        weights = [(gw1u, gW1[D + EA:, :]), (wrep[0:32, :], t["L1_gnn_weight"]), (wrep[32:64, :], t["L1_gnn_weight"]),
                   (wrep[64:96, :], t["L1_gnn_weight"]), (wrep[96:128, :], t["L1_gnn_weight"]),
                   (gw1, by_k(gW1[0:D, :])), (gw1e, gW1[D:D + EA, :]), (gw2, by_k(t["L0_gnn_W2"])), (gb2r, row(t["L0_gnn_b2"])),
                   (brr, row(t["L0_ffn_br"])), (wr, by_k(t["L0_ffn_Wr"])), (bo, t["L0_ffn_bo"]), (wg[:], by_k(t["L1_ffn_W_gat"]))]
        for q, name in enumerate(("att_src", "att_dst", "b_gat", "ln_gamma", "ln_beta")):
            vector = t["L1_ffn_" + name]
            vector = vector.rearrange("(a h) k -> a (h k)", a=1) if q < 2 else row(vector)
            weights.append((att[:, q, :], vector.broadcast_to([P, HK])))
        param_rows = []
        for c, names in enumerate((("b1", "g1", "be1", "m1", "v1"), ("b2", "g2", "be2", "m2", "v2"))):
            for q, name in enumerate(names):
                param_rows.append((prow[q * Q:(q + 1) * Q, c, :], t["L0_ffn_" + name].rearrange("e (m p) -> (e m) p", p=P)))
        at = 0
        for a in (t["L0_gnn_b1"].rearrange("(m p) -> m p", p=P), t["L0_gnn_u"][0:1, :], t["L1_gnn_gamma"].rearrange("(m p) -> m p", p=P),
                  t["L1_gnn_beta"].rearrange("(m p) -> m p", p=P), t["L1_ffn_b1"].rearrange("e (m p) -> (e m) p", p=P)):
            param_rows.append((prow[at:at + a.shape[0], 2, :], a))
            at += a.shape[0]
        late_weights = [(EW1, experts(t["L0_ffn_W1"])), (EW2, experts(t["L0_ffn_W2"])), (EWo, experts(t["L0_ffn_Wo"]))]
        weight_loads = len(weights) + len(param_rows) + len(late_weights)

        s_const = sem("constants")
        s_dve = sem("dve_own")
        s_key = sem("keys_in")
        s_fillv = sem("empty_records")
        s_fill = [sem(f"records{n}_emptied") for n in range(3)]
        s_cnt = sem("bucket_counts")
        s_tot = sem("bucket_totals")
        s_nch = sem("bucket_chunks")
        s_base = sem("bucket_starts")
        s_cmp = sem("bucket_ends_compared")
        s_brow = sem("buckets_by_chunk")
        s_slot = sem("slots_ready")
        s_sd = sem("slots_stored")
        s_idx = pair("scatter_indices_in")
        s_prg = pair("scatter_payload_in")
        s_loc = pair("scatter_nodes_in")
        s_sc = pair("scattered")
        s_pass = sem("pool_passed")
        s_vpass = sem("dve_passed")
        s_ppass = sem("pe_passed")
        s_spass = sem("sp_passed")
        s_w = sem("weights_in")
        s_w4 = sem("weights4_in")
        s_xin = sem("x_in")
        s_pre = sem("preset")
        s_bld = pair("records0_back")
        s_oh = pair("onehots0")
        s_mm = pair("chunk_sums0")
        s_add = pair("added0")
        s_pT = sem("parameters_turned")
        s_par = sem("parameters_ready")
        s_ub = sem("u_bias")
        s_xln = sem("tokens_normed")
        s_tr = sem("tokens_turned")
        s_xTa = sem("turned_in_sbuf_act")
        s_xTv = sem("turned_in_sbuf_dve")
        s_at = sem("edge_means")
        s_atr = sem("edge_means_turned")
        s_atT = sem("edge_means_in_sbuf")
        s_hp = sem("hidden_psum")
        s_hr = sem("hidden_sbuf")
        s_yp = sem("outputs_psum")
        s_yr = sem("outputs_added")
        s_lg = sem("router_logits")
        s_sh = sem("router_shifted")
        s_ex = sem("router_exp")
        s_gt = sem("router_gates")
        s_gtp = sem("gates_turned")
        s_gT = sem("gates_in_sbuf")
        s_xl3 = sem("tokens3_normed")
        s_xst = sem("tokens3_stored")
        s_m1 = pair("records1_back")
        s_g1 = pair("rows1_gathered")
        s_oh1 = pair("onehots1")
        s_mm1 = pair("chunk_sums1")
        s_ad1 = pair("added1")
        s_hm = sem("octonion_psum")
        s_hc = sem("octonion_sbuf")
        s_hb = sem("octonion_stats")
        s_bn = sem("batch_norm_ready")
        s_th = sem("tanh_done")
        s_nt = sem("tanh_turned")
        s_nx = sem("tokens4_normed")
        s_nr = sem("tokens4_turned")
        s_nca = sem("tokens4_sbuf_act")
        s_nh = sem("projected")
        s_nhr = sem("projected_taken")
        s_gs = sem("rows2_ready")
        s_gst = sem("rows2_stored")
        s_mxa = sem("max_asked")
        s_mxp = sem("max_turned")
        s_nd = sem("node_table_ready")
        s_m2 = pair("records2_back")
        s_g2 = pair("rows2_gathered")
        s_oh2 = pair("onehots2")
        s_t2 = pair("onehots2_turned")
        s_c2 = pair("onehots2_sbuf")
        s_d2 = pair("destination_values")
        s_e2 = pair("scores_shifted")
        s_x2 = pair("scores_exp")
        s_v2 = pair("messages")
        s_a2 = pair("messages_summed")
        s_z2 = sem("sums2_zeroed")
        s_fe = sem("final_asked")
        s_fx = sem("final_exp")
        s_fhp = sem("hidden4_psum")
        s_fhr = sem("hidden4_sbuf")
        s_fyp = sem("outputs4_psum")
        s_fyr = sem("outputs4_added")
        s_out = sem("stored")

        def halves(a, n):
            return a.rearrange("(p c) -> p c", p=n)

        r0v = rec0[:].rearrange("(p c) w -> p (c w)", p=P)
        r1v = rec1[:].rearrange("(p c) w -> p (c w)", p=P)
        r2v = rec2[:].rearrange("(p c) w -> p (c w)", p=P)
        flat = lambda a: a.rearrange("p a b -> p (a b)")
        whole_tiles = N // P

        block = ctx.enter_context(nc.Block())

        @block.sync
        def _(sp):
            sp.dma_start(key[0][0:g0.parts, 0:g0.cols], halves(t["src"], g0.parts)).then_inc(s_key, 16)
            sp.dma_start(key[1][0:g1.parts, 0:g1.cols], halves(t["dst"], g1.parts)).then_inc(s_key, 16)
            sp.dma_start(key[2][0:g2.parts, 0:g2.cols], halves(t["L1_ffn_edge_index"][1], g2.parts)).then_inc(s_key, 16)
            sp.dma_start(ew[0:g1.parts, 0:g1.cols], halves(t["edge_weight"], g1.parts)).then_inc(s_key, 16)
            sp.dma_start(srcs[0:g2.parts, 0:g2.cols], halves(t["L1_ffn_edge_index"][0], g2.parts)).then_inc(s_key, 16)
            sp.wait_ge(s_fillv, 3)
            with sp.Fori(0, FILLS[0]) as i:
                sp.dma_start(r0v[:, bass.ds(i * FILL[0] * A0, FILL[0] * A0)], empty0f).then_inc(s_fill[0], 16)
            with sp.Fori(0, FILLS[1]) as i:
                sp.dma_start(r1v[:, bass.ds(i * FILL[1] * R1, FILL[1] * R1)], flat(empty1).bitcast(I32)).then_inc(s_fill[1], 16)
            with sp.Fori(0, FILLS[2]) as i:
                sp.dma_start(r2v[:, bass.ds(i * FILL[2] * R2, FILL[2] * R2)], flat(empty2).bitcast(I32)).then_inc(s_fill[2], 16)

            attr_v = t["edge_attr_64"].rearrange("(p c) w -> p c w", p=g0.parts)

            def store_slots(n, g):
                sp.wait_ge(s_slot, n + 1)
                sp.dma_start(slot_d[n][:], sloti[n][0:g.parts, 0:g.cols]).then_inc(s_sd, 16)
                if n:
                    py = (None, py1, py2)[n]
                    sp.dma_start(pay_d[n][:], flat(py[0:g.parts]).bitcast(I32)).then_inc(s_sd, 16)

            scattered = 0
            for n, g in enumerate(graphs):
                if n == 0:
                    store_slots(0, g0)
                    sp.wait_ge(s_sd, 16)
                if n == 1:
                    store_slots(1, g1)
                    store_slots(2, g2)
                    sp.wait_ge(s_sd, 16 * 5)
                    sp.wait_ge(s_pre, 1)
                    sp.dma_start(X[:, 0:whole_tiles, :], t["x"][0:whole_tiles * P, :].rearrange("(t p) d -> p t d", p=P)).then_inc(s_xin, 16)
                    sp.dma_start(X[0:TAIL, whole_tiles, :], t["x"][whole_tiles * P:N, :]).then_inc(s_xin, 16)
                with sp.Fori(0, ITERS[n]) as i:
                    for s in range(2):
                        at = i * (2 * SS) + s * SS
                        sp.wait_ge(s_sc[s], i * (16 * SS) + scattered)
                        sp.sem_inc(s_spass, 1)
                        sp.dma_start(iring[0:g.parts, s, :], slot_d[n][:, bass.ds(at, SS)]).then_inc(s_idx[s], 16)
                        if n == 0:
                            sp.dma_start(aring[0:g.parts, s, :, 0:EA], attr_v[:, bass.ds(at, SS), :]).then_inc(s_prg[s], 16)
                        else:
                            rw = (0, R1, R2)[n]
                            sp.dma_start(pring[0:g.parts, s, 0:SS * rw], pay_d[n][:, bass.ds(at * rw, SS * rw)]).then_inc(s_prg[s], 16)
                scattered += 16 * SS * ITERS[n]

            for s in range(2):
                sp.wait_ge(s_sc[s], scattered)
            with sp.Fori(0, C1) as i:
                for s in range(2):
                    sp.wait_ge(s_g1[s], i * (16 * SC))
                    sp.sem_inc(s_spass, 1)
                    sp.wait_ge(s_oh1[s], i * SC)
                    sp.sem_inc(s_spass, 1)
                    sp.dma_start(mring[:, s, 0:SC * R1], r1v[:, bass.ds((i * 2 + s) * (SC * R1), SC * R1)]).then_inc(s_m1[s], 16)
            sp.dma_start(FW1, t["L1_ffn_W1"].rearrange("e (k p) n -> p e k n", p=P)).then_inc(s_w4, 16)
            sp.dma_start(FW2, t["L1_ffn_W2"].rearrange("e (k p) n -> p e k n", p=P)).then_inc(s_w4, 16)
            sp.dma_start(flat(fb2r), t["L1_ffn_b2"].rearrange("(a e) d -> a (e d)", a=1)).then_inc(s_w4, 16)
            sp.wait_ge(s_gs, 1)
            sp.dma_start(gat_d[:].rearrange("(t p) w -> p t w", p=P), G).then_inc(s_gst, 16)
            for s in range(2):
                sp.wait_ge(s_g1[s], C1 * 16 * SC)
            with sp.Fori(0, C2) as i:
                for s in range(2):
                    sp.wait_ge(s_g2[s], i * (16 * SC))
                    sp.sem_inc(s_spass, 1)
                    sp.wait_ge(s_oh2[s], i * SC)
                    sp.sem_inc(s_spass, 1)
                    sp.dma_start(mring[:, s, 0:SC * R2], r2v[:, bass.ds((i * 2 + s) * (SC * R2), SC * R2)]).then_inc(s_m2[s], 16)
            with sp.Fori(0, GROUPS - 1) as i:
                sp.wait_ge(s_fyr, i * (2 * NE) + 2 * NE)
                sp.sem_inc(s_spass, 1)
                sp.dma_start(out[bass.ds(i * W, W), :].rearrange("(t p) d -> p t d", p=P), X[:, tiles(i), :]).then_inc(s_out, 16)
            sp.wait_ge(s_fyr, GROUPS * 2 * NE)
            last = (GROUPS - 1) * TG
            stores = GROUPS
            if last < whole_tiles:
                sp.dma_start(out[last * P:whole_tiles * P, :].rearrange("(t p) d -> p t d", p=P), X[:, last:whole_tiles, :]).then_inc(s_out, 16)
                stores += 1
            sp.dma_start(out[whole_tiles * P:N, :], X[0:TAIL, whole_tiles, :]).then_inc(s_out, 16)
            sp.wait_ge(s_out, 16 * stores)

        @block.gpsimd
        def _(pool):
            pool.iota(iota_c, [[1, CMAX]], base=0, channel_multiplier=0, allow_small_or_imprecise_dtypes=True).then_inc(s_const, 1)
            pool.iota(iota[:], [[1, P]], base=0, channel_multiplier=0, allow_small_or_imprecise_dtypes=True).then_inc(s_const, 1)
            pool.memset(ones[:], 1.0).then_inc(s_const, 1)
            pool.memset(ident[:], 0.0).then_inc(s_const, 1)
            pool.memset(before, 1.0).then_inc(s_const, 1)
            pool.memset(upto, 1.0).then_inc(s_const, 1)
            pool.wait_ge(s_const, 6)
            pool.affine_select(out=ident[:], in_=ident[:], compare_op=ALU.not_equal, fill=1.0, base=0, pattern=[[-1, P]], channel_multiplier=1).then_inc(s_const, 1)
            pool.affine_select(out=before, in_=before, compare_op=ALU.is_gt, fill=0.0, base=0, pattern=[[1, P]], channel_multiplier=-1).then_inc(s_const, 1)
            pool.affine_select(out=upto, in_=upto, compare_op=ALU.is_ge, fill=0.0, base=0, pattern=[[1, P]], channel_multiplier=-1).then_inc(s_const, 1)

            records = [rec0[:], rec1[:], rec2[:]]
            staged = 0
            for n, g in enumerate(graphs):
                pool.wait_ge(s_fill[n], 16 * FILLS[n])
                with pool.Fori(0, ITERS[n]) as i:
                    for s in range(2):
                        pool.wait_ge(s_idx[s], i * 16 + (staged + 16))
                        pool.wait_ge(s_prg[s], i * 16 + (staged + 16))
                        if n == 0:
                            pool.wait_ge(s_loc[s], i + 1)
                        pool.sem_inc(s_pass, 1)
                        for c in range(SS):
                            if n == 0:
                                record = aring[0:g.parts, s, c, :]
                            else:
                                rw = (0, R1, R2)[n]
                                record = pring[0:g.parts, s, c * rw:(c + 1) * rw]
                            pool.indirect_dma_start(records[n], bass.IndirectOffsetOnAxis(ap=iring[0:g.parts, s, c:c + 1], axis=0), record, None).then_inc(s_sc[s], 16)
                staged += 16 * ITERS[n]
            pool.wait_ge(s_xst, 16 * GROUPS)
            with pool.Fori(0, C1) as i:
                for s in range(2):
                    pool.wait_ge(s_m1[s], i * 16 + 16)
                    pool.wait_ge(s_mm1[s], i * SC)
                    pool.sem_inc(s_pass, 1)
                    for c in range(SC):
                        pool.indirect_dma_start(rows1[:, s * SC + c, :], None, xl_d[:], bass.IndirectOffsetOnAxis(ap=mring[:, s, c * R1:c * R1 + 1], axis=0)).then_inc(s_g1[s], 16)
            pool.wait_ge(s_gst, 16)
            with pool.Fori(0, C2) as i:
                for s in range(2):
                    pool.wait_ge(s_m2[s], i * 16 + 16)
                    pool.wait_ge(s_v2[s], i)
                    pool.sem_inc(s_pass, 1)
                    for c in range(SC):
                        pool.indirect_dma_start(r2[:, s, c * GW:(c + 1) * GW], None, gat_d[:], bass.IndirectOffsetOnAxis(ap=mring[:, s, c * R2:c * R2 + 1], axis=0)).then_inc(s_g2[s], 16)

        @block.vector
        def _(v):
            d = Count(s_dve)

            def own():
                v.wait_ge(s_dve, d.value)

            def signal(s):
                own()
                v.sem_inc(s, 1)

            def inverse_root(y, x_, part):
                d.add(v.tensor_scalar(y.bitcast(I32), x_.bitcast(I32), 1, None, ALU.arith_shift_right))
                own()
                d.add(v.tensor_scalar(y.bitcast(I32), y.bitcast(I32), -1.0, float(0x5F3759DF), ALU.mult, ALU.add))
                own()
                for _ in range(3):
                    d.add(v.scalar_tensor_tensor(out=part, in0=y, scalar=-0.5, in1=y, op0=ALU.mult, op1=ALU.mult))
                    own()
                    d.add(v.tensor_tensor(part, part, x_, ALU.mult))
                    own()
                    d.add(v.scalar_tensor_tensor(out=y, in0=part, scalar=1.5, in1=y, op0=ALU.add, op1=ALU.mult))
                    own()
            ROOT = 11

            d.add(v.memset(empty0, 0.0))
            d.add(v.memset(empty1, 0.0))
            d.add(v.memset(empty2, 0.0))
            d.add(v.memset(zeros, 0.0))
            d.add(v.memset(prow, 0.0))
            d.add(v.memset(aring[:, :, :, EA + 1:EA + 2], 1.0))
            own()
            v.memset(empty0[:, :, EA:EA + 1], -1.0).then_inc(s_fillv, 1)
            v.memset(empty1[:, :, 1:2], -1.0).then_inc(s_fillv, 1)
            v.memset(empty2[:, :, 1:2], -1.0).then_inc(s_fillv, 1)
            v.wait_ge(s_const, 9)
            v.wait_ge(s_key, 16 * 5)

            def group_edges(n, g):
                pp, T, NB = g.parts, g.cols, g.buckets
                k_, si, hi_, m_, c_, s_ = (a[0:pp, 0:T] for a in (key[n], sloti[n], hi, mask, cum, slotf))
                lo_ = (lo0 if n == 0 else lo)[0:pp, 0:T]
                d.add(v.tensor_scalar(hi_, k_, 7, None, ALU.arith_shift_right))
                d.add(v.tensor_scalar(m_, k_, P - 1, None, ALU.bitwise_and))
                d.add(v.memset(s_, 0.0))
                own()
                d.add(v.tensor_copy(lo_, m_))
                start = d.value
                d.base, d.k = start, 0
                with v.Fori(0, NB) as h:
                    d.enter(h, 1)
                    own()
                    d.add(v.tensor_scalar(m_, hi_, iota[0:pp, bass.ds(h, 1)], 0.0, ALU.is_equal, ALU.add, accum_out=cnt[0:pp, bass.ds(h, 1)]))
                d.leave(NB)
                signal(s_cnt)
                v.wait_ge(s_tot, n + 1)
                d.add(v.tensor_scalar(nch[0:NB, 0:1], bank[0][0:NB, 0:1], float(P - 1), None, ALU.add))
                own()
                d.add(v.tensor_copy(nchi[0:NB, :], nch[0:NB, 0:1]))
                own()
                d.add(v.tensor_scalar(nchi[0:NB, :], nchi[0:NB, :], 7, None, ALU.arith_shift_right))
                own()
                d.add(v.tensor_copy(nch[0:NB, 1:2], nchi[0:NB, :]))
                own()
                d.add(v.tensor_scalar(nrep[0:NB, :], ones[0:NB, :], nch[0:NB, 1:2], float(P), ALU.mult, ALU.mult))
                signal(s_nch)
                v.wait_ge(s_base, n + 1)
                d.add(v.tensor_scalar(base[0:pp, 0:NB], bank[1][0:pp, 0:NB], 1.0, None, ALU.subtract))
                d.add(v.tensor_copy(nch[0:NB, 2:3], bank[2][0:NB, 0:1]))
                own()
                d.add(v.tensor_scalar(ends[0:NB, 0:g.chunks], iota_c[0:NB, 0:g.chunks], nch[0:NB, 2:3], None, ALU.is_ge))
                signal(s_cmp)
                with v.Fori(0, NB) as h:
                    d.enter(h, 4)
                    own()
                    d.add(v.tensor_scalar(m_, hi_, iota[0:pp, bass.ds(h, 1)], None, ALU.is_equal))
                    own()
                    d.add(v.tensor_tensor_scan(c_, m_, zeros[0:pp, 0:T], base[0:pp, bass.ds(h, 1)], ALU.add, ALU.add))
                    own()
                    d.add(v.tensor_tensor(c_, c_, m_, ALU.mult))
                    own()
                    d.add(v.tensor_tensor(s_, s_, c_, ALU.add))
                d.leave(NB)
                own()
                d.add(v.tensor_copy(hi_, s_))
                own()
                d.add(v.tensor_scalar(m_, hi_, P - 1, None, ALU.bitwise_and))
                own()
                d.add(v.tensor_scalar(hi_, hi_, 7, None, ALU.arith_shift_right))
                own()
                d.add(v.scalar_tensor_tensor(out=si, in0=m_, scalar=float(g.chunks), in1=hi_, op0=ALU.mult, op1=ALU.add))

            def buckets_by_chunk(n, g):
                v.wait_ge(s_brow, n + 1)
                for a in range(0, g.chunks, 512):
                    b = min(a + 512, g.chunks)
                    d.add(v.tensor_scalar(brow[0:1, a:b], bank[3 + a // 512][0:1, 0:b - a], float(g.buckets - 1), None, ALU.min))
                own()
                return brow[0:1, 0:g.chunks], brow2[0:1, 0:g.chunks]

            group_edges(0, g0)
            signal(s_slot)
            b, _ = buckets_by_chunk(0, g0)
            d.add(v.tensor_scalar(off0, b, float(A0), None, ALU.mult))
            group_edges(1, g1)
            d.add(v.tensor_copy(py1[0:g1.parts].bitcast(I32)[:, :, 0], key[0][0:g1.parts, 0:g1.cols]))
            d.add(v.tensor_copy(py1[0:g1.parts, :, 1], lo[0:g1.parts, 0:g1.cols]))
            d.add(v.tensor_copy(py1[0:g1.parts, :, 2], ew[0:g1.parts, 0:g1.cols]))
            signal(s_slot)
            b, _ = buckets_by_chunk(1, g1)
            d.add(v.tensor_scalar(off1, b, float(P), None, ALU.mult))
            group_edges(2, g2)
            d.add(v.tensor_scalar(py2[0:g2.parts].bitcast(I32)[:, :, 0], srcs[0:g2.parts, 0:g2.cols], float(N - 1), None, ALU.min))
            d.add(v.tensor_copy(py2[0:g2.parts, :, 1], lo[0:g2.parts, 0:g2.cols]))
            signal(s_slot)
            b, b2 = buckets_by_chunk(2, g2)
            d.add(v.tensor_scalar(off2n, b, float(2 * HEADS), None, ALU.mult))
            own()
            d.add(v.tensor_scalar(b, b, float(TILES), None, ALU.min))
            own()
            d.add(v.tensor_scalar(b2, b, float(PB), float(512 - PB * GW), ALU.is_ge, ALU.mult))
            own()
            d.add(v.tensor_scalar(b, b, float(GW), None, ALU.mult))
            own()
            d.add(v.tensor_tensor(off2s, b, b2, ALU.add))
            own()

            v.wait_ge(s_pT, 1)
            d.add(v.tensor_copy(flat(pcol[:]), bank[6][:, 0:3 * P]))
            own()
            for c in range(2):
                b1c, gc, bec, mc, vc = (pcol[:, c, a * Q:(a + 1) * Q] for a in range(5))
                scale, shift = bnf[:, c, 0, :], bnf[:, c, 1, :]
                d.add(v.tensor_scalar(root_in[:], vc, BN_EPS_EXPERTS, None, ALU.add))
                own()
                inverse_root(scale, root_in[:], root_part[:])
                d.add(v.tensor_tensor(shift, b1c, mc, ALU.subtract))
                own()
                d.add(v.tensor_tensor(scale, scale, gc, ALU.mult))
                own()
                d.add(v.tensor_tensor(shift, shift, scale, ALU.mult))
                own()
                d.add(v.tensor_tensor(shift, shift, bec, ALU.add))
            signal(s_par)
            v.wait_ge(s_ub, 1)
            d.add(v.tensor_tensor(gb1[:], pcol[:, 2, 0:KG], bank[7][:, 0:KG], ALU.add))
            v.wait_ge(s_w, 16 * weight_loads)
            for c in range(8):
                rows, k = slice(32 * (c % 4), 32 * (c % 4) + 32), c // 4
                for r in range(8):
                    part = r ^ c
                    d.add(v.tensor_scalar(ham[rows, k, 32 * r:32 * r + 32], wrep[rows, 32 * part:32 * part + 32], float(SIGN[r][c]), None, ALU.mult))
            signal(s_par)

            v.wait_ge(s_sd, 16 * 5)
            v.memset(X[:, whole_tiles:TPAD, :], 0.0).then_inc(s_pre, 1)
            d.add(v.memset(acc0, 0.0))

            acc0f = flat(acc0)
            with v.Fori(0, C0) as i:
                d.enter(i, 2 * SC)
                for s in range(2):
                    v.wait_ge(s_bld[s], i * 16 + 16)
                    v.wait_ge(s_mm[s], i * SC)
                    for c in range(SC):
                        v.tensor_scalar(oh[:, s * SC + c, :], iota[:], oring[:, s * SC + c, EA:EA + 1], None, ALU.is_equal).then_inc(s_oh[s], 1)
                for s in range(2):
                    _, at = nc.values_load_multi_w_load_instructions(off0[:, bass.ds(i * (2 * SC) + s * SC, SC)], engines=DVE_ONLY, min_val=0, max_val=(TILES - 1) * A0)
                    for c in range(SC):
                        if c % 4 == 0:
                            v.wait_ge(s_mm[s], i * SC + (c + 4))
                        own()
                        a = acc0f[:, bass.ds(at[c], A0)]
                        d.add(v.tensor_tensor(a, a, bank[2 * s + c // 4][:, (c % 4) * A0:(c % 4 + 1) * A0], ALU.add))
                    signal(s_add[s])
            d.leave(C0)

            def norm(source, into, done, eps=LN_EPS):
                v.sem_inc(s_vpass, 1)
                for j in range(TG):
                    d.add(v.bn_stats(lnst[:, j, :], source(j)))
                own()
                v.sem_inc(s_vpass, 1)
                for j in range(TG):
                    d.add(v.bn_aggr(lnmv[:, j, :], lnst[:, j, :]))
                own()
                d.add(v.tensor_scalar(root_in[:, 0:TG], lnmv[:, :, 1], eps, None, ALU.add))
                own()
                inverse_root(rstd[:], root_in[:, 0:TG], root_part[:, 0:TG])
                for j in range(TG):
                    d.add(v.tensor_scalar(into[:, j, :], source(j), lnmv[:, j, 0:1], rstd[:, j:j + 1], ALU.subtract, ALU.mult))
                signal(done)
            NORM = 3 * TG + 1 + ROOT

            v.wait_ge(s_xin, 32)
            with v.Fori(0, GROUPS) as i:
                d.enter(i, 3 * NORM + 2 + TG + 3)
                two = lambda b: X[:, tiles(i, 2 * b, 2), :]
                xt = lambda j: tile(X, i, j)
                norm(xt, xln, s_xln)
                d.add(v.tensor_scalar(cmx[:], acc0[:, tiles(i), EA + 1], 1.0, None, ALU.max))
                own()
                d.add(v.reciprocal(cmx[:], cmx[:]))
                own()
                for j in range(TG):
                    d.add(v.tensor_scalar(attr[:, j, :], acc0[:, tiles(i, j, 1), 0:EA].rearrange("p a d -> p (a d)"), cmx[:, j:j + 1], None, ALU.mult))
                signal(s_at)
                v.wait_ge(s_tr, i * 2 + 1)
                v.tensor_copy(xT[:, 1, :], bank[1]).then_inc(s_xTv, 1)
                v.wait_ge(s_atr, i + 1)
                v.tensor_copy(attrT, bank[2][0:EA, :]).then_inc(s_atT, 1)
                for b in range(2):
                    v.wait_ge(s_yp, i * YP + (b + 1))
                    v.tensor_tensor(two(b), two(b), bank[6 + b].rearrange("p (t d) -> p t d", d=D), ALU.add).then_inc(s_yr, 1)
                v.wait_ge(s_yr, i * YP + 2)
                norm(xt, xln, s_xln)
                v.wait_ge(s_tr, i * 2 + 2)
                v.tensor_copy(xT[:, 1, :], bank[1]).then_inc(s_xTv, 1)
                v.wait_ge(s_lg, i + 1)
                lg = bank[3][:, 0:TG * NX].rearrange("p (t e) -> p t e", e=NX)
                d.add(v.tensor_reduce(gmx[:], lg, AX, ALU.max))
                own()
                v.tensor_tensor(gate[:], lg, gmx[:].unsqueeze(2).broadcast_to([P, TG, NX]), ALU.subtract).then_inc(s_sh, 1)
                v.wait_ge(s_ex, i + 1)
                d.add(v.tensor_reduce(gsm[:], gate[:], AX, ALU.add))
                own()
                d.add(v.reciprocal(gsm[:], gsm[:]))
                own()
                v.tensor_tensor(gate[:], gate[:], gsm[:].unsqueeze(2).broadcast_to([P, TG, NX]), ALU.mult).then_inc(s_gt, 1)
                v.wait_ge(s_gtp, i + 1)
                v.tensor_copy(gateT, bank[3][0:NX, :]).then_inc(s_gT, 1)
                v.wait_ge(s_gt, i + 1)
                for u in range(2, YP):
                    b, e = u % 2, u // 2 - 2
                    v.wait_ge(s_yp, i * YP + (u + 1))
                    v.wait_ge(s_yr, i * YP + (u - 1))
                    if e < 0:
                        ins = v.tensor_tensor(two(b), two(b), bank[6 + b].rearrange("p (t d) -> p t d", d=D), ALU.add)
                    else:
                        for j in range(2):
                            x_ = xt(2 * b + j)
                            ins = v.scalar_tensor_tensor(out=x_, in0=bank[6 + b][:, j * D:(j + 1) * D], scalar=gate[:, 2 * b + j, e:e + 1], in1=x_, op0=ALU.mult, op1=ALU.add)
                    ins.then_inc(s_yr, 1)
                v.wait_ge(s_yr, i * YP + YP)
                v.wait_ge(s_xst, i * 16)
                norm(xt, xl3, s_xl3)
            d.leave(GROUPS)
            own()

            d.add(v.memset(big, 0.0))
            with v.Fori(0, C1) as i:
                d.enter(i, 2 * SC)
                for s in range(2):
                    v.wait_ge(s_m1[s], i * 16 + 16)
                    v.wait_ge(s_mm1[s], i * SC)
                    record = mring[:, s, :].bitcast(F32)
                    for c in range(SC):
                        v.tensor_scalar(oh[:, s * SC + c, :], iota[:], record[:, c * R1 + 1:c * R1 + 2], record[:, c * R1 + 2:c * R1 + 3], ALU.is_equal, ALU.mult).then_inc(s_oh1[s], 1)
                for s in range(2):
                    _, at = nc.values_load_multi_w_load_instructions(off1[:, bass.ds(i * (2 * SC) + s * SC, SC)], engines=DVE_ONLY, min_val=0, max_val=(TILES - 1) * P)
                    for c in range(SC):
                        if c % 2 == 0:
                            v.wait_ge(s_mm1[s], i * SC + (c + 2))
                        own()
                        a = big[:, :, bass.ds(at[c], P)]
                        sums_ = bank[4 * s + c // 2][:, (c % 2) * KD * P:(c % 2 + 1) * KD * P].rearrange("p (k n) -> p k n", k=KD)
                        d.add(v.tensor_tensor(a, a, sums_, ALU.add))
                    signal(s_ad1[s])
            d.leave(C1)

            with v.Fori(0, GROUPS - 1) as i:
                for m in range(KD):
                    v.wait_ge(s_hc, i * KD + (m + 1))
                    v.sem_inc(s_vpass, 1)
                    v.bn_stats(bst[:, m, bass.ds(i, 1), :].rearrange("p a w -> p (a w)"), big[:, m, bass.ds(i * W, W)]).then_inc(s_hb, 1)
            for m in range(KD):
                v.wait_ge(s_hc, (GROUPS - 1) * KD + m + 1)
                v.bn_stats(bst[:, m, GROUPS - 1, :], big[:, m, (GROUPS - 1) * W:N]).then_inc(s_hb, 1)
            v.wait_ge(s_hb, GROUPS * KD)
            for m in range(KD):
                d.add(v.bn_aggr(bmv[:, m, :], bst[:, m, :, :].rearrange("p g w -> p (g w)")))
            own()
            gamma, beta = pcol[:, 2, KG + 1:KG + 1 + KD], pcol[:, 2, KG + 1 + KD:KG + 1 + 2 * KD]
            d.add(v.tensor_scalar(root_in[:, 0:KD], bmv[:, :, 1], BN_EPS_GRAPH, None, ALU.add))
            own()
            inverse_root(root_in[:, KD:2 * KD], root_in[:, 0:KD], root_part[:, 0:KD])
            d.add(v.tensor_copy(bsc[:, :, 0], root_in[:, KD:2 * KD]))
            own()
            d.add(v.tensor_tensor(bsc[:, :, 0], bsc[:, :, 0], gamma, ALU.mult))
            own()
            d.add(v.tensor_tensor(bsc[:, :, 1], bmv[:, :, 0], bsc[:, :, 0], ALU.mult))
            own()
            d.add(v.tensor_tensor(bsc[:, :, 1], beta, bsc[:, :, 1], ALU.subtract))
            signal(s_bn)

            d.add(v.memset(nd, 0.0))
            with v.Fori(0, GROUPS) as i:
                d.enter(i, 2 + NORM + 5)
                v.wait_ge(s_nt, i + 1)
                for b in range(2):
                    x_ = X[:, tiles(i, 2 * b, 2), :]
                    d.add(v.tensor_tensor(x_, x_, bank[2 + b].rearrange("p (t d) -> p t d", d=D), ALU.add))
                own()
                norm(lambda j: tile(X, i, j), xln, s_nx)
                for k in range(KD):
                    v.wait_ge(s_nca, i * KD + (k + 1))
                    v.tensor_copy(big[:, k, bass.ds(i * W, W)], xT[:, k, :])
                v.wait_ge(s_nh, i + 1)
                h = bank[6][:, 0:TG * HK].rearrange("p (t q) -> p t q", q=HK)
                d.add(v.tensor_copy(G[:, tiles(i), HEADS:GW], h))
                for a, scores in ((0, G), (1, nd)):
                    own()
                    d.add(v.tensor_tensor(hat[:], h, att[:, a, :].unsqueeze(1).broadcast_to([P, TG, HK]), ALU.mult))
                    own()
                    d.add(v.tensor_reduce(scores[:, tiles(i), 0:HEADS], hat[:].rearrange("p t (h k) -> p t h k", h=HEADS), AX, ALU.add))
                signal(s_nhr)
            d.leave(GROUPS)
            signal(s_gs)
            d.add(v.tensor_reduce(gmax[:], G[:, 0:TILES - 1, 0:HEADS].rearrange("p t h -> p h t"), AX, ALU.max))
            own()
            d.add(v.tensor_tensor(gmax[0:TAIL, :], gmax[0:TAIL, :], G[0:TAIL, TILES - 1, 0:HEADS], ALU.max))
            signal(s_mxa)
            v.wait_ge(s_mxp, 1)
            d.add(v.tensor_reduce(gm4[:, 0:1], bank[0][0:HEADS, 0:P], AX, ALU.max))
            own()
            d.add(v.tensor_scalar(gm4[:, 1:1 + HEADS], ident[0:HEADS, 0:HEADS], gm4[:, 0:1], None, ALU.mult))
            signal(s_mxa)
            v.wait_ge(s_mxp, 2)
            d.add(v.tensor_copy(gmax[:], bank[0][:, P:P + HEADS]))
            own()
            score, shift = nd[:, 0:TPAD, 0:HEADS], nd[:, 0:TPAD, HEADS:2 * HEADS]
            d.add(v.tensor_tensor(es[:], score, G[:, :, 0:HEADS], ALU.add))
            d.add(v.tensor_tensor(shift, score, gmax[:].unsqueeze(1).broadcast_to([P, TPAD, HEADS]), ALU.add))
            own()
            d.add(v.scalar_tensor_tensor(out=es[:], in0=es[:], scalar=0.2, in1=es[:], op0=ALU.mult, op1=ALU.max))
            d.add(v.scalar_tensor_tensor(out=shift, in0=shift, scalar=0.2, in1=shift, op0=ALU.mult, op1=ALU.max))
            own()
            d.add(v.tensor_scalar(tmp[0], es[:], SELF_REACH, None, ALU.add))
            own()
            d.add(v.tensor_tensor(shift, shift, tmp[0], ALU.min))
            own()
            d.add(v.tensor_tensor(es[:], es[:], shift, ALU.subtract))
            d.add(v.memset(zero, 0.0))
            signal(s_nd)
            v.wait_ge(s_z2, 2)

            with v.Fori(0, C2) as i:
                d.enter(i, 2 * 5)
                for s in range(2):
                    v.wait_ge(s_m2[s], i * 16 + 16)
                    v.wait_ge(s_a2[s], i * SC)
                    record = mring[:, s, :].bitcast(F32)
                    for c in range(SC):
                        v.tensor_scalar(oh[:, s * SC + c, :], iota[:], record[:, c * R2 + 1:c * R2 + 2], None, ALU.is_equal).then_inc(s_oh2[s], 1)
                for s in range(2):
                    at_dst = bank[(1, 5)[s]][:, 0:SC * 2 * HEADS].rearrange("p (c w) -> p c w", w=2 * HEADS)
                    row = r2[:, s, :].rearrange("p (c w) -> p c w", w=GW)
                    msg = v2[:, s, :].rearrange("p (c w) -> p c w", w=GW)
                    e = ev[:, s, :].rearrange("p (c h) -> p c h", h=HEADS)
                    v.wait_ge(s_g2[s], i * (16 * SC) + 16 * SC)
                    v.wait_ge(s_d2[s], i + 1)
                    d.add(v.tensor_tensor(e, row[:, :, 0:HEADS], at_dst[:, :, 0:HEADS], ALU.add))
                    own()
                    d.add(v.scalar_tensor_tensor(out=e, in0=e, scalar=0.2, in1=e, op0=ALU.mult, op1=ALU.max))
                    own()
                    d.add(v.tensor_tensor(e, e, at_dst[:, :, HEADS:2 * HEADS], ALU.subtract))
                    own()
                    d.add(v.tensor_scalar(e, e, SELF_REACH, None, ALU.min))
                    signal(s_e2[s])
                    v.wait_ge(s_x2[s], i + 1)
                    d.add(v.tensor_tensor(msg[:, :, HEADS:GW].rearrange("p c (h k) -> p c h k", h=HEADS), row[:, :, HEADS:GW].rearrange("p c (h k) -> p c h k", h=HEADS),
                                          msg[:, :, 0:HEADS].unsqueeze(3).broadcast_to([P, SC, HEADS, HK // HEADS]), ALU.mult))
                    signal(s_v2[s])
            d.leave(C2)

            for s in range(2):
                v.wait_ge(s_a2[s], C2 * SC)
            v.wait_ge(s_fx, 1)
            for b in range(-(-TILES // PB)):
                a, z = b * PB, min((b + 1) * PB, TILES)
                d.add(v.tensor_copy(sums[:, a:z, :], sumbank[:, 512 * b:512 * b + (z - a) * GW].rearrange("p (t w) -> p t w", w=GW)))
            den, num = sums[:, :, 0:HEADS], sums[:, :, HEADS:GW]
            by_head = lambda a: a.rearrange("p t (h k) -> p t h k", h=HEADS)
            wide = lambda a: a.unsqueeze(3).broadcast_to([P, TILES, HEADS, HK // HEADS])
            vec = lambda a: att[:, a, :].unsqueeze(1).broadcast_to([P, TILES, HK])
            over16 = lambda a: a.broadcast_to([P, TILES, HK])
            own_e = es[:, 0:TILES, :]
            d.add(v.tensor_tensor(by_head(t16), by_head(G[:, 0:TILES, HEADS:GW]), wide(own_e), ALU.mult))
            own()
            d.add(v.tensor_tensor(den, den, own_e, ALU.add))
            d.add(v.tensor_tensor(num, num, t16, ALU.add))
            own()
            d.add(v.reciprocal(den, den))
            own()
            d.add(v.tensor_tensor(by_head(num), by_head(num), wide(den), ALU.mult))
            own()
            d.add(v.tensor_tensor(num, num, vec(2), ALU.add))
            own()
            m1, m2 = tmp[0][:, 0:TILES, 0:1], tmp[1][:, 0:TILES, 0:1]
            m1s, m2s = tmp[0][:, 0:TILES, 0], tmp[1][:, 0:TILES, 0]
            d.add(v.tensor_reduce(m1s, num, AX, ALU.add))
            own()
            d.add(v.tensor_scalar(m1s, m1s, 1.0 / HK, None, ALU.mult))
            own()
            d.add(v.tensor_tensor(num, num, over16(m1), ALU.subtract))
            own()
            d.add(v.tensor_tensor(t16, num, num, ALU.mult))
            own()
            d.add(v.tensor_reduce(m2s, t16, AX, ALU.add))
            own()
            d.add(v.tensor_scalar(m2s, m2s, 1.0 / HK, LN_EPS, ALU.mult, ALU.add))
            own()
            d.add(v.tensor_copy(roots[:, 0, 0:TILES], m2s))
            own()
            inverse_root(roots[:, 1, 0:TILES], roots[:, 0, 0:TILES], roots[:, 2, 0:TILES])
            d.add(v.tensor_tensor(num, num, roots[:, 1, 0:TILES].unsqueeze(2).broadcast_to([P, TILES, HK]), ALU.mult))
            own()
            d.add(v.tensor_tensor(num, num, vec(3), ALU.mult))
            own()
            d.add(v.tensor_tensor(num, num, vec(4), ALU.add))
            own()
            score, rank, ahead = es[:, 0:TILES, :], tmp[0][:, 0:TILES, :], tmp[1][:, 0:TILES, :]
            d.add(v.tensor_reduce(score, num.rearrange("p t (h k) -> p t k h", h=HEADS), AX, ALU.add))
            own()
            d.add(v.tensor_scalar(score, score, 1.0 / HEADS, None, ALU.mult))
            d.add(v.memset(rank, 0.0))
            own()
            best = tmp[2][:, 0:TILES, 0:1]
            d.add(v.tensor_reduce(tmp[2][:, 0:TILES, 0], score, AX, ALU.max))
            for f in range(NE):
                for a, z, op in ((0, f + 1, ALU.is_gt), (f + 1, NE, ALU.is_ge)):
                    if a < z:
                        d.add(v.tensor_tensor(ahead[:, :, a:z], score[:, :, f:f + 1].broadcast_to([P, TILES, z - a]), score[:, :, a:z], op))
                own()
                d.add(v.tensor_tensor(rank, rank, ahead, ALU.add))
                own()
            d.add(v.tensor_scalar(rank, rank, 1.5, None, ALU.is_lt))
            d.add(v.tensor_tensor(score, score, best.broadcast_to([P, TILES, NE]), ALU.subtract))
            signal(s_fe)
            v.wait_ge(s_fx, 2)
            d.add(v.tensor_tensor(score, score, rank, ALU.mult))
            d.add(v.memset(gates, 0.0))
            own()
            d.add(v.tensor_reduce(tmp[2][:, 0:TILES, 0], score, AX, ALU.add))
            own()
            d.add(v.reciprocal(tmp[2][:, 0:TILES, 0], tmp[2][:, 0:TILES, 0]))
            own()
            d.add(v.tensor_tensor(gates[:, 0:TILES, :], score, best.broadcast_to([P, TILES, NE]), ALU.mult))
            own()
            with v.Fori(0, GROUPS) as i:
                for u in range(2 * NE):
                    b, e = u % 2, u // 2
                    v.wait_ge(s_fyp, i * (2 * NE) + (u + 1))
                    if u >= 2:
                        v.wait_ge(s_fyr, i * (2 * NE) + (u - 1))
                    for j in range(2):
                        x_ = tile(X, i, 2 * b + j)
                        ins = v.scalar_tensor_tensor(out=x_, in0=bank[2 + b][:, j * D:(j + 1) * D], scalar=gates[:, tiles(i, 2 * b + j, 1), e:e + 1].rearrange("p a e -> p (a e)"), in1=x_, op0=ALU.mult, op1=ALU.add)
                    ins.then_inc(s_fyr, 1)

        @block.scalar
        def _(a):
            load = lambda dst, src: a.dma_start(dst, src).then_inc(s_w, 16)
            for dst, src in weights:
                load(dst, src)
            a.wait_ge(s_fillv, 3)
            for dst, src in param_rows:
                load(dst, src)
            a.wait_ge(s_fill[0], 16 * FILLS[0])
            for dst, src in late_weights:
                load(dst, src)
            a.wait_ge(s_slot, 1)
            with a.Fori(0, ITERS[0]) as i:
                for s in range(2):
                    a.wait_ge(s_sc[s], i * (16 * SS))
                    a.activation(aring[0:g0.parts, s, :, EA], lo0[0:g0.parts, bass.ds(i * (2 * SS) + s * SS, SS)], ACT.Copy).then_inc(s_loc[s], 1)
            for s in range(2):
                a.wait_ge(s_sc[s], 16 * SS * ITERS[0])
            a.wait_ge(s_sd, 16 * 5)
            with a.Fori(0, C0) as i:
                for s in range(2):
                    a.wait_ge(s_mm[s], i * SC)
                    a.dma_start(flat(oring[:, s * SC:(s + 1) * SC, :]), r0v[:, bass.ds((i * 2 + s) * (SC * A0), SC * A0)]).then_inc(s_bld[s], 16)
            a.wait_ge(s_par, 2)
            with a.Fori(0, GROUPS) as i:
                hidden = 0

                def take_hidden(slot, func, bias, scale=1.0):
                    nonlocal hidden
                    a.wait_ge(s_hp, i * HP + (hidden + 1))
                    a.activation(HB[:, slot, :], bank[4 + hidden % 2], func, bias=bias, scale=scale).then_inc(s_hr, 1)
                    hidden += 1

                a.wait_ge(s_tr, i * 2 + 1)
                a.activation(xT[:, 0, :], bank[0], ACT.Copy).then_inc(s_xTa, 1)
                for m in range(KG):
                    take_hidden(m, ACT.Relu, gb1[:, m:m + 1])
                a.wait_ge(s_tr, i * 2 + 2)
                a.activation(xT[:, 0, :], bank[0], ACT.Copy).then_inc(s_xTa, 1)
                a.wait_ge(s_sh, i + 1)
                a.activation(gate[:], gate[:], ACT.Exp).then_inc(s_ex, 1)
                for e in range(NX):
                    for c in range(2):
                        for m in range(KD):
                            q = e * KD + m
                            take_hidden(4 * c + (e % 2) * KD + m, ACT.Relu, bnf[:, c, 1, q:q + 1], bnf[:, c, 0, q:q + 1])
                assert hidden == HP
                a.wait_ge(s_xl3, i + 1)
                a.dma_start(xl_d[bass.ds(i * W, W), :].rearrange("(t p) d -> p t d", p=P), xl3).then_inc(s_xst, 16)
            with a.Fori(0, GROUPS) as i:
                a.wait_ge(s_hm, i * KD + KD)
                for m in range(KD):
                    a.activation(big[:, m, bass.ds(i * W, W)], bank[m], ACT.Copy).then_inc(s_hc, 1)
            a.wait_ge(s_bn, 1)
            with a.Fori(0, GROUPS) as i:
                a.wait_ge(s_nt, i)
                a.wait_ge(s_hc, GROUPS * KD)
                for k in range(KD):
                    a.activation(HB[:, k, :], big[:, k, bass.ds(i * W, W)], ACT.Tanh, bias=bsc[:, k, 1:2], scale=bsc[:, k, 0:1]).then_inc(s_th, 1)
                a.wait_ge(s_nr, i + 1)
                for k in range(KD):
                    a.activation(xT[:, k, :], bank[4 + k], ACT.Copy).then_inc(s_nca, 1)
            with a.Fori(0, C2) as i:
                for s in range(2):
                    a.wait_ge(s_t2[s], i + 1)
                    for b in range(2):
                        c0 = s * SC + 4 * b
                        a.activation(flat(ohT[:, c0:c0 + 4, :]), bank[(0, 2, 3, 4)[2 * s + b]], ACT.Copy).then_inc(s_c2[s], 1)
                for s in range(2):
                    a.wait_ge(s_e2[s], i + 1)
                    a.wait_ge(s_a2[s], i * SC)
                    a.activation(v2[:, s, :].rearrange("p (c w) -> p c w", w=GW)[:, :, 0:HEADS], ev[:, s, :].rearrange("p (c h) -> p c h", h=HEADS), ACT.Exp).then_inc(s_x2[s], 1)
            a.wait_ge(s_nd, 1)
            a.activation(es[:], es[:], ACT.Exp).then_inc(s_fx, 1)
            a.wait_ge(s_fe, 1)
            a.activation(es[:, 0:TILES, :], es[:, 0:TILES, :], ACT.Exp).then_inc(s_fx, 1)
            bias4 = pcol[:, 2, KG + 1 + 2 * KD:KG + 1 + 2 * KD + NE * KF]
            with a.Fori(0, GROUPS) as i:
                for e in range(NE):
                    for m in range(KF):
                        u = e * KF + m
                        a.wait_ge(s_fhp, i * (NE * KF) + (u + 1))
                        a.activation(HB[:, (e % 2) * KF + m, :], bank[u % 2], ACT.Gelu, bias=bias4[:, u:u + 1]).then_inc(s_fhr, 1)

        @block.tensor
        def _(pe):
            pe.wait_ge(s_const, 9)
            for n, g in enumerate(graphs):
                pp, NB = g.parts, g.buckets
                pe.wait_ge(s_cnt, n + 1)
                pe.matmul(bank[0][0:NB, 0:1], cnt[0:pp, 0:NB], ones[0:pp, 0:1], start=True, stop=True).then_inc(s_tot, 1)
                pe.wait_ge(s_nch, n + 1)
                pe.matmul(bank[1][0:pp, 0:NB], before[0:pp, 0:pp], cnt[0:pp, 0:NB], start=True, stop=False)
                pe.matmul(bank[1][0:pp, 0:NB], nrep[0:NB, 0:pp], before[0:NB, 0:NB], start=False, stop=True)
                pe.matmul(bank[2][0:NB, 0:1], upto[0:NB, 0:NB], nch[0:NB, 1:2], start=True, stop=True).then_inc(s_base, 1)
                pe.wait_ge(s_cmp, n + 1)
                for c in range(0, g.chunks, 512):
                    z = min(c + 512, g.chunks)
                    mm = pe.matmul(bank[3 + c // 512][0:1, 0:z - c], ones[0:NB, 0:1], ends[0:NB, c:z], start=True, stop=True)
                mm.then_inc(s_brow, 1)
            pe.wait_ge(s_w, 16 * weight_loads)
            for c in range(3):
                mm = pe.transpose(bank[6][:, c * P:(c + 1) * P], prow[:, c, :], ident[:])
            mm.then_inc(s_pT, 1)
            pe.wait_ge(s_par, 1)
            for m in range(KG):
                mm = pe.matmul(bank[7][:, m:m + 1], gw1u[:, m * P:(m + 1) * P], pcol[:, 2, KG:KG + 1], start=True, stop=True)
            mm.then_inc(s_ub, 1)

            with pe.Fori(0, C0) as i:
                for s in range(2):
                    pe.wait_ge(s_bld[s], i * 16 + 16)
                    pe.wait_ge(s_add[s], i)
                    for c in range(SC):
                        pe.wait_ge(s_oh[s], i * SC + (c + 1))
                        pe.matmul(bank[2 * s + c // 4][:, (c % 4) * A0:(c % 4 + 1) * A0], oh[:, s * SC + c, :], oring[:, s * SC + c, :], start=True, stop=True).then_inc(s_mm[s], 1)

            def turn(source, banks, j0=0):
                for k in range(KD):
                    for j in range(TG):
                        mm = pe.transpose(banks[k][:, j * P:(j + 1) * P], source[:, j, k * P:(k + 1) * P], ident[:])
                return mm

            pe.wait_ge(s_par, 2)
            pe.wait_ge(s_add[0], C0)
            pe.wait_ge(s_add[1], C0)
            with pe.Fori(0, GROUPS) as i:
                hidden, outs = 0, 0

                def into_hidden(products):
                    nonlocal hidden
                    pe.wait_ge(s_hr, i * HP + max(hidden - 1, 0))
                    for n, (w_, x_) in enumerate(products):
                        mm = pe.matmul(bank[4 + hidden % 2], w_, x_, start=(n == 0), stop=(n == len(products) - 1))
                    mm.then_inc(s_hp, 1)
                    hidden += 1

                def into_outputs(products):
                    nonlocal outs
                    for b in range(2):
                        pe.wait_ge(s_yr, i * YP + max(outs - 1, 0))
                        for j in range(2):
                            ps = products(2 * b + j)
                            for n, (x_, w_) in enumerate(ps):
                                mm = pe.matmul(bank[6 + b][:, j * D:(j + 1) * D], x_, w_, start=(n == 0), stop=(n == len(ps) - 1))
                        mm.then_inc(s_yp, 1)
                        outs += 1

                cols = lambda j: slice(j * P, (j + 1) * P)
                pe.wait_ge(s_xln, i * 2 + 1)
                turn(xln, bank[0:2]).then_inc(s_tr, 1)
                pe.wait_ge(s_at, i + 1)
                pe.sem_inc(s_ppass, 1)
                for j in range(TG):
                    mm = pe.transpose(bank[2][0:EA, cols(j)], attr[:, j, :], ident[:])
                mm.then_inc(s_atr, 1)
                pe.wait_ge(s_xTa, i * 2 + 1)
                pe.wait_ge(s_xTv, i * 2 + 1)
                pe.wait_ge(s_atT, i + 1)
                for m in range(KG):
                    into_hidden([(gw1[:, k, cols(m)], xT[:, k, :]) for k in range(KD)] + [(gw1e[:, cols(m)], attrT)])
                pe.wait_ge(s_hr, i * HP + hidden)
                into_outputs(lambda j: [(ones[0:1, :], gb2r)] + [(HB[:, m, cols(j)], gw2[:, m, :]) for m in range(KG)])
                pe.wait_ge(s_xln, i * 2 + 2)
                turn(xln, bank[0:2]).then_inc(s_tr, 1)
                pe.wait_ge(s_xTa, i * 2 + 2)
                pe.wait_ge(s_xTv, i * 2 + 2)
                for j in range(TG):
                    for k in range(KD):
                        pe.matmul(bank[3][:, j * NX:(j + 1) * NX], xT[:, k, cols(j)], wr[:, k, :], start=(k == 0), stop=False)
                    mm = pe.matmul(bank[3][:, j * NX:(j + 1) * NX], ones[0:1, :], brr, start=False, stop=True)
                mm.then_inc(s_lg, 1)

                def first(e):
                    for m in range(KD):
                        into_hidden([(EW1[:, e, k, cols(m)], xT[:, k, :]) for k in range(KD)])

                def second(e, taken):
                    pe.wait_ge(s_hr, i * HP + taken)
                    for m in range(KD):
                        into_hidden([(EW2[:, e, k, cols(m)], HB[:, (e % 2) * KD + k, :]) for k in range(KD)])

                def third(e, taken):
                    pe.wait_ge(s_hr, i * HP + taken)
                    into_outputs(lambda j: [(HB[:, 4 + (e % 2) * KD + k, cols(j)], EWo[:, e, k, :]) for k in range(KD)])

                first(0)
                second(0, hidden)
                pe.wait_ge(s_gt, i + 1)
                for j in range(TG):
                    mm = pe.transpose(bank[3][0:NX, cols(j)], gate[:, j, :], ident[:])
                mm.then_inc(s_gtp, 1)
                pe.wait_ge(s_gT, i + 1)
                into_outputs(lambda j: [(gateT[:, cols(j)], bo)])
                for e in range(1, NX + 1):
                    done2 = hidden
                    if e < NX:
                        first(e)
                    third(e - 1, done2)
                    if e < NX:
                        second(e, hidden)
                assert (hidden, outs) == (HP, YP)

            pe.wait_ge(s_yr, GROUPS * YP)
            with pe.Fori(0, C1) as i:
                for s in range(2):
                    pe.wait_ge(s_g1[s], i * (16 * SC) + 16 * SC)
                    pe.wait_ge(s_ad1[s], i)
                    for c in range(SC):
                        pe.wait_ge(s_oh1[s], i * SC + (c + 1))
                        for k in range(KD):
                            at = (c % 2) * KD * P + k * P
                            mm = pe.matmul(bank[4 * s + c // 2][:, at:at + P], rows1[:, s * SC + c, k * P:(k + 1) * P], oh[:, s * SC + c, :], start=True, stop=True)
                        mm.then_inc(s_mm1[s], 1)
            for s in range(2):
                pe.wait_ge(s_ad1[s], C1)
            with pe.Fori(0, GROUPS) as i:
                pe.wait_ge(s_hc, i * KD)
                for m in range(KD):
                    for k in range(KD):
                        mm = pe.matmul(bank[m], ham[:, k, m * P:(m + 1) * P], big[:, k, bass.ds(i * W, W)], start=(k == 0), stop=(k == KD - 1))
                    mm.then_inc(s_hm, 1)
            with pe.Fori(0, GROUPS) as i:
                pe.wait_ge(s_th, i * KD + KD)
                for j in range(TG):
                    for k in range(KD):
                        mm = pe.transpose(bank[2 + j // 2][:, (j % 2) * D + k * P:(j % 2) * D + (k + 1) * P], HB[:, k, j * P:(j + 1) * P], ident[:])
                mm.then_inc(s_nt, 1)
                pe.wait_ge(s_nx, i + 1)
                turn(xln, bank[4:6]).then_inc(s_nr, 1)
                pe.wait_ge(s_nca, i * KD + KD)
                for j in range(TG):
                    for k in range(KD):
                        mm = pe.matmul(bank[6][:, j * HK:(j + 1) * HK], xT[:, k, j * P:(j + 1) * P], wg[:, k, :], start=(k == 0), stop=(k == KD - 1))
                mm.then_inc(s_nh, 1)
                pe.wait_ge(s_nhr, i + 1)
            pe.wait_ge(s_mxa, 1)
            pe.transpose(bank[0][0:HEADS, 0:P], gmax[:], ident[:]).then_inc(s_mxp, 1)
            pe.wait_ge(s_mxa, 2)
            pe.matmul(bank[0][:, P:P + HEADS], ones[0:HEADS, :], gm4[:, 1:1 + HEADS], start=True, stop=True).then_inc(s_mxp, 1)

            pe.wait_ge(s_nd, 1)
            for b in range(2):
                pe.matmul(bank[6 + b], zero_l, zero_r, start=True, stop=False, skip_group_check=True).then_inc(s_z2, 1)
            with pe.Fori(0, C2) as i:
                for s in range(2):
                    pe.wait_ge(s_c2[s], i * 2)
                    for c in range(SC):
                        pe.wait_ge(s_oh2[s], i * SC + (c + 1))
                        mm = pe.transpose(bank[(0, 2, 3, 4)[2 * s + c // 4]][:, (c % 4) * P:(c % 4 + 1) * P], oh[:, s * SC + c, :], ident[:])
                    mm.then_inc(s_t2[s], 1)
                for s in range(2):
                    _, at = nc.values_load_multi_w_load_instructions(off2n[:, bass.ds(i * (2 * SC) + s * SC, SC)], engines=PE_ONLY, min_val=0, max_val=(g2.buckets - 1) * 2 * HEADS)
                    pe.wait_ge(s_c2[s], i * 2 + 2)
                    pe.wait_ge(s_v2[s], i)
                    for c in range(SC):
                        mm = pe.matmul(bank[(1, 5)[s]][:, c * 2 * HEADS:(c + 1) * 2 * HEADS], ohT[:, s * SC + c, :], flat(nd)[:, bass.ds(at[c], 2 * HEADS)], start=True, stop=True)
                    mm.then_inc(s_d2[s], 1)
                for s in range(2):
                    _, at = nc.values_load_multi_w_load_instructions(off2s[:, bass.ds(i * (2 * SC) + s * SC, SC)], engines=PE_ONLY, min_val=0, max_val=2 * 512 - GW)
                    pe.wait_ge(s_v2[s], i + 1)
                    for c in range(SC):
                        pe.matmul(sumbank[:, bass.ds(at[c], GW)], oh[:, s * SC + c, :], v2[:, s, c * GW:(c + 1) * GW], start=False, stop=False, skip_group_check=True).then_inc(s_a2[s], 1)

            pe.wait_ge(s_w4, 48)
            pe.wait_ge(s_fe, 1)
            with pe.Fori(0, GROUPS) as i:
                def first4(e):
                    for m in range(KF):
                        u = e * KF + m
                        pe.wait_ge(s_fhr, i * (NE * KF) + max(u - 1, 0))
                        for k in range(KD):
                            mm = pe.matmul(bank[u % 2], FW1[:, e, k, m * P:(m + 1) * P], big[:, k, bass.ds(i * W, W)], start=(k == 0), stop=(k == KD - 1))
                        mm.then_inc(s_fhp, 1)

                def second4(e):
                    pe.wait_ge(s_fhr, i * (NE * KF) + (e + 1) * KF)
                    for b in range(2):
                        u = e * 2 + b
                        pe.wait_ge(s_fyr, i * (2 * NE) + max(u - 1, 0))
                        for j in range(2):
                            o = bank[2 + b][:, j * D:(j + 1) * D]
                            pe.matmul(o, ones[0:1, :], fb2r[:, e, :], start=True, stop=False)
                            for m in range(KF):
                                mm = pe.matmul(o, HB[:, (e % 2) * KF + m, (2 * b + j) * P:(2 * b + j + 1) * P], FW2[:, e, m, :], start=False, stop=(m == KF - 1))
                        mm.then_inc(s_fyp, 1)

                first4(0)
                for e in range(1, NE):
                    first4(e)
                    second4(e - 1)
                second4(NE - 1)


def kernel(**inputs):
    import numpy as _np
    import concourse.bacc as _bacc
    from concourse.bass_utils import run_bass_kernel_spmd as _run

    nc = _bacc.Bacc("TRN2", target_bir_lowering=False, num_devices=1)
    arrays, args = {}, {}
    for name, value in inputs.items():
        a = _np.ascontiguousarray(value)
        arrays[f"in_{name}"] = a
        args[name] = nc.dram_tensor(f"in_{name}", a.shape, mybir.dt.from_np(a.dtype), kind="ExternalInput").ap()
    shape = args["x"].shape
    result = nc.dram_tensor("out_x", shape, F32, kind="ExternalOutput").ap()
    build(nc, args, result)
    r = _run(nc, [arrays], core_ids=[0])
    return r.results[0]["out_x"]
```

```python
from contextlib import ExitStack

import concourse.bass as bass
from concourse import mybir

F32 = mybir.dt.float32
I32 = mybir.dt.int32
ALU = mybir.AluOpType
ACT = mybir.ActivationFunctionType
AX = mybir.AxisListType.X
DVE_ONLY = (mybir.EngineType.DVE,)
PE_ONLY = (mybir.EngineType.PE,)

P = 128
LN_EPS = 1e-5
BN_EPS_EXPERTS = 1e-3
BN_EPS_GRAPH = 1e-5
SIGN = [[1, 1, 1, 1, 1, 1, 1, 1], [1, -1, 1, -1, 1, -1, -1, 1], [1, -1, -1, 1, 1, 1, -1, -1],
        [1, 1, -1, -1, 1, -1, 1, -1], [1, -1, -1, -1, -1, 1, 1, 1], [1, 1, -1, 1, -1, -1, -1, 1],
        [1, 1, 1, -1, -1, 1, -1, -1], [1, -1, 1, 1, -1, -1, 1, -1]]
SELF_REACH = 80.0


def most(n):
    return max(p for p in range(1, P + 1) if n % p == 0)


class Graph:

    def __init__(self, edges, keys, unroll):
        self.parts = most(edges)
        self.cols = edges // self.parts
        self.buckets = -(-keys // P)
        chunks = (edges + self.buckets * (P - 1)) // P
        self.chunks = -(-chunks // unroll) * unroll


class Count:

    def __init__(self, sem):
        self.sem, self.base, self.k, self.turn, self.per = sem, 0, 0, None, 0

    def add(self, instruction, n=1):
        instruction.then_inc(self.sem, n)
        self.k += n

    @property
    def value(self):
        v = self.base + self.k
        return v if self.turn is None else self.turn * self.per + v

    def enter(self, turn, per):
        self.base, self.k, self.turn, self.per = self.base + self.k, 0, turn, per

    def leave(self, turns):
        assert self.k == self.per, (self.k, self.per)
        self.base, self.k, self.turn = self.base + turns * self.per, 0, None


def build(nc, t, out):
    N, D = t["x"].shape
    E0 = t["src"].shape[0]
    E2 = t["L1_ffn_edge_index"].shape[1]
    EA = t["edge_attr_64"].shape[1]
    NX, _, H1 = t["L0_ffn_W1"].shape
    GH = t["L0_gnn_W1"].shape[1]
    NE, _, H2 = t["L1_ffn_W1"].shape
    HEADS = t["L1_ffn_att_src"].shape[0]
    HK = t["L1_ffn_W_gat"].shape[1]
    TG = 4
    TILES = -(-N // P)
    GROUPS = -(-TILES // TG)
    TPAD = GROUPS * TG
    W = TG * P
    TAIL = N - (TILES - 1) * P
    KD, KG, KF = D // P, GH // P, H2 // P
    A0 = EA + 2
    GW = HEADS + HK
    PB = 512 // GW
    PB0 = 512 // A0
    SC = 8
    SS = 16
    R1, R2 = 3, 2
    g0 = Graph(E0, N, 2 * SC)
    g1 = Graph(E0, N, 2 * SC)
    g2 = Graph(E2, 8192, 2 * SC)
    graphs = (g0, g1, g2)
    TMAX = max(g.cols for g in graphs)
    CMAX = max(g.chunks for g in graphs)
    ITERS = [g.cols // (2 * SS) for g in graphs]
    C0, C1, C2 = (g.chunks // (2 * SC) for g in graphs)
    FILL = [2 * SC, 64, 64]
    FILLS = [g.chunks // f for g, f in zip(graphs, FILL)]
    for g, n, f, fs in zip(graphs, ITERS, FILL, FILLS):
        assert n * 2 * SS == g.cols and f * fs == g.chunks
    Q = NX * KD
    HP, YP = KG + NX * 2 * KD, 4 + 2 * NX

    ctx = ExitStack()
    with ctx:
        def sb(name, shape, dt=F32):
            return ctx.enter_context(nc.sbuf_tensor(name, shape, dt))

        def sem(name):
            return ctx.enter_context(nc.semaphore(name))

        def pair(name):
            return [sem(f"{name}_a"), sem(f"{name}_b")]

        rec0 = nc.dram_tensor("rec0", [P * g0.chunks, A0], F32)
        rec1 = nc.dram_tensor("rec1", [P * g1.chunks, R1], I32)
        rec2 = nc.dram_tensor("rec2", [P * g2.chunks, R2], I32)
        slot_d = [nc.dram_tensor(f"slots{n}", [g.parts, g.cols], I32) for n, g in enumerate(graphs)]
        pay_d = [None, nc.dram_tensor("pay1", [g1.parts, g1.cols * R1], I32),
                 nc.dram_tensor("pay2", [g2.parts, g2.cols * R2], I32)]
        xl_d = nc.dram_tensor("xl", [TPAD * P, D], F32)
        gat_d = nc.dram_tensor("gat", [TPAD * P, GW], F32)

        class Region:
            def __init__(self, name, size):
                self.ap, self.size, self.at = sb(name, [P, size])[:], size, 0

            def restart(self, at=0):
                self.at = at

            def take(self, *shape, rows=P, dt=F32):
                n = 1
                for k in shape:
                    n *= k
                a = self.ap[0:rows, self.at:self.at + n]
                self.at += n
                assert self.at <= self.size
                if dt is not F32:
                    a = a.bitcast(dt)
                if len(shape) == 2:
                    a = a.rearrange("p (a b) -> p a b", a=shape[0])
                if len(shape) == 3:
                    a = a.rearrange("p (a b c) -> p a b c", a=shape[0], b=shape[1])
                return a

        rX = Region("rX", TPAD * D)
        X = rX.take(TPAD, D)
        rX.restart()
        key = [rX.take(TMAX, dt=I32) for _ in graphs]
        sloti = [rX.take(TMAX, dt=I32) for _ in graphs]
        hi, mask = rX.take(TMAX, dt=I32), rX.take(TMAX, dt=I32)
        lo, cum, slotf, zeros = (rX.take(TMAX) for _ in range(4))
        rB = Region("rB", KD * TPAD * P)
        big = rB.take(KD, TPAD * P)
        rB.restart()
        EW1, EW2, EWo = (rB.take(NX, KD, H1) for _ in range(3))
        attr = rB.take(TG, EA)
        bo = rB.take(D, rows=NX)
        gb2r = rB.take(D, rows=1)
        brr = rB.take(NX, rows=1)
        wr = rB.take(KD, NX)
        rS = Region("rS", NE * KD * H2 + NE * KF * D)
        ew, srcs = rS.take(TMAX), rS.take(TMAX, dt=I32)
        ends = rS.take(CMAX)
        py1, py2 = rS.take(g1.cols, R1), rS.take(g2.cols, R2)
        rS.restart()
        acc0 = rS.take(TPAD, A0)
        oring = rS.take(2 * SC, A0)
        xTb, xl3 = rS.take(KD, W), rS.take(TG, D)
        rS.restart()
        FW1, FW2 = rS.take(NE, KD, H2), rS.take(NE, KF, D)
        rH = Region("rH", 8 * W)
        HB = rH.take(8, W)
        rH.restart()
        iota_c = rH.take(CMAX)
        brow = rH.take(CMAX, rows=1)
        brow2 = rH.take(CMAX, rows=1)
        gw1u = rH.take(GH)
        empty1, empty2 = rH.take(FILL[1], R1), rH.take(FILL[2], R2)
        rH.restart()
        rows1 = rH.take(2 * SC, D)
        rG = Region("rG", 3328)
        gw1, gw2, gw1e = rG.take(KD, GH), rG.take(KG, D), rG.take(GH, rows=EA)
        rG.restart()
        G, nd = rG.take(TPAD, GW), rG.take(g2.buckets, 2 * HEADS)
        sums, t16 = rG.take(TILES, GW), rG.take(TILES, HK)
        rD = Region("rD", 3 * TG * D)
        aring = rD.take(2, SS, A0)
        rD.restart()
        xln, xT = rD.take(TG, D), rD.take(KD, W)
        rD.restart()
        ohT = rD.take(2 * SC, P)
        r2, v2, ev = rD.take(2, SC * GW), rD.take(2, SC * GW), rD.take(2, SC * HEADS)
        rO = Region("rO", 2 * SC * P)
        oh = rO.take(2 * SC, P)
        rO.restart()
        HG = rO.take(KG, W)
        rO.restart()
        lo0, prow, wrep = rO.take(g0.cols), rO.take(3, P), rO.take(D)
        rA = Region("rA", 2 * W)
        attrT, gateT = rA.take(W, rows=EA), rA.take(W, rows=NX)
        rA.restart()
        fb2r = rA.take(NE, D, rows=1)
        rE = Region("rE", (3 * HEADS + NE) * TPAD)
        before, upto = rE.take(P), rE.take(P)
        nrep, cnt, base = rE.take(P), rE.take(64), rE.take(64)
        rE.restart()
        tmp, gates = [rE.take(TPAD, HEADS) for _ in range(3)], rE.take(TPAD, NE)
        iota = sb("iota", [P, P])
        zero = rO.ap[:, 2 * SC * P - 512:2 * SC * P]
        ident = sb("ident", [P, P])
        ones = sb("ones", [P, P])
        nch = sb("nch", [64, 3])
        nchi = sb("nchi", [64, 1], I32)
        offs = sb("offs", [P, CMAX], I32)
        off0, off1, off2n, off2s = (offs[32 * q:32 * q + 1, 0:g.chunks] for q, g in enumerate((g0, g1, g2, g2)))
        pcol = sb("pcol", [P, 3, P])
        bnf = sb("bnf", [P, 2, 2, Q])
        gb1 = sb("gb1", [P, KG])
        ham = sb("ham", [P, KD, D])
        wg = sb("wg", [P, KD, HK])
        att = sb("att", [P, 5, HK])
        root_in = sb("root_in", [P, Q])
        root_part = sb("root_part", [P, Q])
        lnst = sb("lnst", [P, TG, 6])
        lnmv = sb("lnmv", [P, TG, 2])
        rstd = sb("rstd", [P, TG])
        cmx = sb("cmx", [P, TG])
        gate = sb("gate", [P, TG, NX])
        gate_next = sb("gate_next", [P, TG, NX])
        gmx = sb("gmx", [P, TG])
        gsm = sb("gsm", [P, TG])
        iring = sb("iring", [P, 2, SS], I32)
        pring = sb("pring", [P, 2, SS * R1], I32)
        mring = sb("mring", [P, 2, SC * R1], I32)
        bst = sb("bst", [P, KD, GROUPS, 6])
        bmv = sb("bmv", [P, KD, 2])
        bsc = sb("bsc", [P, KD, 2])
        roots = sb("roots", [P, 3, TPAD])
        hat = sb("hat", [P, TG, HK])
        gmax = sb("gmax", [P, HEADS])
        gm4 = sb("gm4", [HEADS, 1 + HEADS])
        es = sb("es", [P, TPAD, HEADS])

        psum = ctx.enter_context(nc.psum_tensor("psum", [P, 8 * 512], F32))[:]
        bank = [psum[:, 512 * n:512 * (n + 1)] for n in range(8)]
        sumbank0, sumbank = psum[:, 512:], psum[:, 6 * 512:]
        assert TILES <= 7 * PB0 and TILES < 2 * PB

        def tiles(i, j=0, n=TG):
            return bass.ds(i * TG + j, n)

        def tile_at(x, g, j):
            return x[:, bass.ds(past(g, TG, j), 1), :].rearrange("p a d -> p (a d)")

        def tile(x, i, j):
            return x[:, tiles(i, j, 1), :].rearrange("p a d -> p (a d)")

        empty0 = rB.ap[:, 0:FILL[0] * A0].rearrange("p (c w) -> p c w", w=A0)
        empty0f = rB.ap[:, 0:FILL[0] * A0]
        zero_l, zero_r = zero[:, 0:P], zero[:]
        acc0f = acc0.rearrange("p t w -> p (t w)")
        zero_l0, zero_r0 = acc0f[:, 0:P], acc0f[:, 0:512]

        by_k = lambda a: a.rearrange("(k p) n -> p k n", p=P)
        row = lambda a: a.rearrange("(a n) -> a n", a=1)
        experts = lambda a: a.rearrange("e (k p) n -> p e k n", p=P)
        gW1 = t["L0_gnn_W1"]
        weights = [(gw1u, gW1[D + EA:, :]), (wrep[0:32, :], t["L1_gnn_weight"]), (wrep[32:64, :], t["L1_gnn_weight"]),
                   (wrep[64:96, :], t["L1_gnn_weight"]), (wrep[96:128, :], t["L1_gnn_weight"]),
                   (gw1, by_k(gW1[0:D, :])), (gw1e, gW1[D:D + EA, :]), (gw2, by_k(t["L0_gnn_W2"])), (gb2r, row(t["L0_gnn_b2"])),
                   (brr, row(t["L0_ffn_br"])), (wr, by_k(t["L0_ffn_Wr"])), (bo, t["L0_ffn_bo"]), (wg[:], by_k(t["L1_ffn_W_gat"]))]
        for q, name in enumerate(("att_src", "att_dst", "b_gat", "ln_gamma", "ln_beta")):
            vector = t["L1_ffn_" + name]
            vector = vector.rearrange("(a h) k -> a (h k)", a=1) if q < 2 else row(vector)
            weights.append((att[:, q, :], vector.broadcast_to([P, HK])))
        param_rows = []
        for c, names in enumerate((("b1", "g1", "be1", "m1", "v1"), ("b2", "g2", "be2", "m2", "v2"))):
            for q, name in enumerate(names):
                param_rows.append((prow[q * Q:(q + 1) * Q, c, :], t["L0_ffn_" + name].rearrange("e (m p) -> (e m) p", p=P)))
        at = 0
        for a in (t["L0_gnn_b1"].rearrange("(m p) -> m p", p=P), t["L0_gnn_u"][0:1, :], t["L1_gnn_gamma"].rearrange("(m p) -> m p", p=P),
                  t["L1_gnn_beta"].rearrange("(m p) -> m p", p=P), t["L1_ffn_b1"].rearrange("e (m p) -> (e m) p", p=P)):
            param_rows.append((prow[at:at + a.shape[0], 2, :], a))
            at += a.shape[0]
        late_weights = [(EW1, experts(t["L0_ffn_W1"])), (EW2, experts(t["L0_ffn_W2"])), (EWo, experts(t["L0_ffn_Wo"]))]
        weight_loads = len(weights) + len(param_rows) + len(late_weights)

        s_const = sem("constants")
        s_dve = sem("dve_own")
        s_key = sem("keys_in")
        s_fillv = sem("empty_records")
        s_fill = [sem(f"records{n}_emptied") for n in range(3)]
        s_cnt = sem("bucket_counts")
        s_tot = sem("bucket_totals")
        s_nch = sem("bucket_chunks")
        s_base = sem("bucket_starts")
        s_cmp = sem("bucket_ends_compared")
        s_brow = sem("buckets_by_chunk")
        s_slot = sem("slots_ready")
        s_sd = sem("slots_stored")
        s_idx = pair("scatter_indices_in")
        s_prg = pair("scatter_payload_in")
        s_loc = pair("scatter_nodes_in")
        s_sc = pair("scattered")
        s_pass = sem("pool_passed")
        s_vpass = sem("dve_passed")
        s_ppass = sem("pe_passed")
        s_spass = sem("sp_passed")
        s_w = sem("weights_in")
        s_w4 = sem("weights4_in")
        s_xin = sem("x_in")
        s_pre = sem("preset")
        s_bld = pair("records0_back")
        s_oh = pair("onehots0")
        s_mm = pair("chunk_sums0")
        s_add = sem("sums0_in_sbuf")
        s_pT = sem("parameters_turned")
        s_par = sem("parameters_ready")
        s_ub = sem("u_bias")
        s_xln = sem("tokens_normed")
        s_tr = sem("tokens_turned")
        s_xTa = sem("turned_in_sbuf_act")
        s_xTv = sem("turned_in_sbuf_dve")
        s_at = sem("edge_means")
        s_atr = sem("edge_means_turned")
        s_atT = sem("edge_means_in_sbuf")
        s_hp = sem("hidden_psum")
        s_hr = sem("hidden_sbuf")
        s_yp = sem("outputs_psum")
        s_yr = sem("outputs_added")
        s_lg = sem("router_logits")
        s_sh = sem("router_shifted")
        s_ex = sem("router_exp")
        s_gt = sem("router_gates")
        s_gtp = sem("gates_turned")
        s_gT = sem("gates_in_sbuf")
        s_xTb = sem("turned_handed_over")
        s_xl3 = sem("tokens3_normed")
        s_xst = sem("tokens3_stored")
        s_m1 = pair("records1_back")
        s_g1 = pair("rows1_gathered")
        s_oh1 = pair("onehots1")
        s_mm1 = pair("chunk_sums1")
        s_ad1 = pair("added1")
        s_hm = sem("octonion_psum")
        s_hc = sem("octonion_sbuf")
        s_hb = sem("octonion_stats")
        s_bn = sem("batch_norm_ready")
        s_th = sem("tanh_done")
        s_nt = sem("tanh_turned")
        s_nx = sem("tokens4_normed")
        s_nr = sem("tokens4_turned")
        s_nca = sem("tokens4_sbuf_act")
        s_nh = sem("projected")
        s_nhr = sem("projected_taken")
        s_gs = sem("rows2_ready")
        s_gst = sem("rows2_stored")
        s_mxa = sem("max_asked")
        s_mxp = sem("max_turned")
        s_nd = sem("node_table_ready")
        s_m2 = pair("records2_back")
        s_g2 = pair("rows2_gathered")
        s_oh2 = pair("onehots2")
        s_t2 = pair("onehots2_turned")
        s_c2 = pair("onehots2_sbuf")
        s_d2 = pair("destination_values")
        s_e2 = pair("scores_shifted")
        s_x2 = pair("scores_exp")
        s_v2 = pair("messages")
        s_a2 = pair("messages_summed")
        s_z2 = sem("sums2_zeroed")
        s_fe = sem("final_asked")
        s_fx = sem("final_exp")
        s_fhp = sem("hidden4_psum")
        s_fhr = sem("hidden4_sbuf")
        s_fyp = sem("outputs4_psum")
        s_fyr = sem("outputs4_added")
        s_out = sem("stored")

        FREE = 1
        free_again = [s_xst, s_nt, s_hc, s_hr, s_yr, s_fhr, s_fyr]
        for two in (s_mm, s_mm1, s_v2, s_a2, s_ad1, s_c2):
            free_again += two

        def halves(a, n):
            return a.rearrange("(p c) -> p c", p=n)

        r0v = rec0[:].rearrange("(p c) w -> p (c w)", p=P)
        r1v = rec1[:].rearrange("(p c) w -> p (c w)", p=P)
        r2v = rec2[:].rearrange("(p c) w -> p (c w)", p=P)
        flat = lambda a: a.rearrange("p a b -> p (a b)")
        whole_tiles = N // P

        BACK = ("first", "second", "third")
        order = [("second", 0), ("first", 1), ("turn1", 0), ("third", 0), ("second", 1), ("mlp1", 0), ("first", 2), ("third", 1),
                 ("second", 2), ("mlp2", 0), ("first", 3), ("third", 2), ("second", 3), ("first", 4), ("third", 3), ("turn2", 0),
                 ("second", 4), ("first", 5), ("third", 4), ("logits", 0), ("second", 5), ("first", 6), ("third", 5), ("gates", 0),
                 ("second", 6), ("first", 7), ("third", 6), ("bias", 0), ("hand", 0), ("second", 7), ("third", 7), ("first", 0)]
        assert [e for k, e in order if k == "third"] == list(range(NX))
        HIDDEN = {"first": KD, "second": KD, "mlp1": KG}
        OUTS = {"third": 2, "mlp2": 2, "bias": 2}
        FRONT_H, FRONT_Y = KG + KD, 4

        def steps(part):
            if part == "front":
                return [x for x in order if x[0] not in BACK or x == ("first", 0)]
            if part == "back":
                return [x for x in order if x[0] in BACK and x != ("first", 0)]
            return order

        def past(g, per, k):
            i, more = g
            return more * per + k if i is None else i * per + (more * per + k)

        def dense_turns(engine, turn):
            turn("front", (None, 0), None, lambda k: k, lambda k: k)
            with engine.Fori(0, GROUPS - 1) as i:
                turn("both", (i, 1), (i, 0), lambda k: i * HP + (FRONT_H + k), lambda k: i * YP + (FRONT_Y + k))
            turn("back", None, (None, GROUPS - 1), lambda k: (GROUPS - 1) * HP + FRONT_H + k, lambda k: (GROUPS - 1) * YP + FRONT_Y + k)

        block = ctx.enter_context(nc.Block())

        @block.sync
        def _(sp):
            sp.dma_start(key[0][0:g0.parts, 0:g0.cols], halves(t["src"], g0.parts)).then_inc(s_key, 16)
            sp.dma_start(key[1][0:g1.parts, 0:g1.cols], halves(t["dst"], g1.parts)).then_inc(s_key, 16)
            sp.dma_start(key[2][0:g2.parts, 0:g2.cols], halves(t["L1_ffn_edge_index"][1], g2.parts)).then_inc(s_key, 16)
            sp.dma_start(ew[0:g1.parts, 0:g1.cols], halves(t["edge_weight"], g1.parts)).then_inc(s_key, 16)
            sp.dma_start(srcs[0:g2.parts, 0:g2.cols], halves(t["L1_ffn_edge_index"][0], g2.parts)).then_inc(s_key, 16)
            sp.wait_ge(s_fillv, 3)
            with sp.Fori(0, FILLS[0]) as i:
                sp.dma_start(r0v[:, bass.ds(i * FILL[0] * A0, FILL[0] * A0)], empty0f).then_inc(s_fill[0], 16)
            with sp.Fori(0, FILLS[1]) as i:
                sp.dma_start(r1v[:, bass.ds(i * FILL[1] * R1, FILL[1] * R1)], flat(empty1).bitcast(I32)).then_inc(s_fill[1], 16)
            with sp.Fori(0, FILLS[2]) as i:
                sp.dma_start(r2v[:, bass.ds(i * FILL[2] * R2, FILL[2] * R2)], flat(empty2).bitcast(I32)).then_inc(s_fill[2], 16)

            attr_v = t["edge_attr_64"].rearrange("(p c) w -> p c w", p=g0.parts)

            def store_slots(n, g):
                sp.wait_ge(s_slot, n + 1)
                sp.dma_start(slot_d[n][:], sloti[n][0:g.parts, 0:g.cols]).then_inc(s_sd, 16)
                if n:
                    py = (None, py1, py2)[n]
                    sp.dma_start(pay_d[n][:], flat(py[0:g.parts]).bitcast(I32)).then_inc(s_sd, 16)

            scattered = 0
            for n, g in enumerate(graphs):
                if n == 0:
                    store_slots(0, g0)
                    sp.wait_ge(s_sd, 16)
                if n == 1:
                    store_slots(1, g1)
                    store_slots(2, g2)
                    sp.wait_ge(s_sd, 16 * 5)
                    sp.wait_ge(s_pre, 1)
                    sp.dma_start(X[:, 0:whole_tiles, :], t["x"][0:whole_tiles * P, :].rearrange("(t p) d -> p t d", p=P)).then_inc(s_xin, 16)
                    sp.dma_start(X[0:TAIL, whole_tiles, :], t["x"][whole_tiles * P:N, :]).then_inc(s_xin, 16)

                def stage(n, g, at, s):
                    sp.dma_start(iring[0:g.parts, s, :], slot_d[n][:, bass.ds(at, SS)]).then_inc(s_idx[s], 16)
                    if n == 0:
                        sp.dma_start(aring[0:g.parts, s, :, 0:EA], attr_v[:, bass.ds(at, SS), :]).then_inc(s_prg[s], 16)
                    else:
                        rw = (0, R1, R2)[n]
                        sp.dma_start(pring[0:g.parts, s, 0:SS * rw], pay_d[n][:, bass.ds(at * rw, SS * rw)]).then_inc(s_prg[s], 16)

                for s in range(2):
                    if n:
                        sp.wait_ge(s_sc[s], scattered)
                    stage(n, g, s * SS, s)
                with sp.Fori(0, ITERS[n] - 1) as i:
                    for s in range(2):
                        sp.wait_ge(s_sc[s], i * (16 * SS) + (scattered + 16 * SS))
                        sp.sem_inc(s_spass, 1)
                        stage(n, g, i * (2 * SS) + (2 + s) * SS, s)
                scattered += 16 * SS * ITERS[n]

            for s in range(2):
                sp.wait_ge(s_sc[s], scattered)
            for s in range(2):
                sp.dma_start(mring[:, s, 0:SC * R1], r1v[:, s * (SC * R1):(s + 1) * (SC * R1)]).then_inc(s_m1[s], 16)
            with sp.Fori(0, C1 - 1) as i:
                for s in range(2):
                    sp.wait_ge(s_g1[s], i * (16 * SC) + 16 * SC)
                    sp.sem_inc(s_spass, 1)
                    sp.wait_ge(s_oh1[s], i * SC + SC)
                    sp.sem_inc(s_spass, 1)
                    sp.dma_start(mring[:, s, 0:SC * R1], r1v[:, bass.ds(i * (2 * SC * R1) + (2 + s) * (SC * R1), SC * R1)]).then_inc(s_m1[s], 16)
            sp.dma_start(FW1, t["L1_ffn_W1"].rearrange("e (k p) n -> p e k n", p=P)).then_inc(s_w4, 16)
            sp.dma_start(FW2, t["L1_ffn_W2"].rearrange("e (k p) n -> p e k n", p=P)).then_inc(s_w4, 16)
            sp.dma_start(flat(fb2r), t["L1_ffn_b2"].rearrange("(a e) d -> a (e d)", a=1)).then_inc(s_w4, 16)
            sp.wait_ge(s_gs, 1)
            sp.dma_start(gat_d[:].rearrange("(t p) w -> p t w", p=P), G).then_inc(s_gst, 16)
            for s in range(2):
                sp.wait_ge(s_g1[s], C1 * 16 * SC)
                sp.wait_ge(s_oh1[s], C1 * SC)
            for s in range(2):
                sp.dma_start(mring[:, s, 0:SC * R2], r2v[:, s * (SC * R2):(s + 1) * (SC * R2)]).then_inc(s_m2[s], 16)
            with sp.Fori(0, C2 - 1) as i:
                for s in range(2):
                    sp.wait_ge(s_g2[s], i * (16 * SC) + 16 * SC)
                    sp.sem_inc(s_spass, 1)
                    sp.wait_ge(s_oh2[s], i * SC + SC)
                    sp.sem_inc(s_spass, 1)
                    sp.dma_start(mring[:, s, 0:SC * R2], r2v[:, bass.ds(i * (2 * SC * R2) + (2 + s) * (SC * R2), SC * R2)]).then_inc(s_m2[s], 16)
            with sp.Fori(0, GROUPS - 1) as i:
                sp.wait_ge(s_fyr, i * (2 * NE) + 2 * NE + FREE)
                sp.sem_inc(s_spass, 1)
                sp.dma_start(out[bass.ds(i * W, W), :].rearrange("(t p) d -> p t d", p=P), X[:, tiles(i), :]).then_inc(s_out, 16)
            sp.wait_ge(s_fyr, GROUPS * 2 * NE + FREE)
            last = (GROUPS - 1) * TG
            stores = GROUPS
            if last < whole_tiles:
                sp.dma_start(out[last * P:whole_tiles * P, :].rearrange("(t p) d -> p t d", p=P), X[:, last:whole_tiles, :]).then_inc(s_out, 16)
                stores += 1
            sp.dma_start(out[whole_tiles * P:N, :], X[0:TAIL, whole_tiles, :]).then_inc(s_out, 16)
            sp.wait_ge(s_out, 16 * stores)

        @block.gpsimd
        def _(pool):
            for s in free_again:
                pool.sem_inc(s, FREE)
            pool.iota(iota_c, [[1, CMAX]], base=0, channel_multiplier=0, allow_small_or_imprecise_dtypes=True).then_inc(s_const, 1)
            pool.iota(iota[:], [[1, P]], base=0, channel_multiplier=0, allow_small_or_imprecise_dtypes=True).then_inc(s_const, 1)
            pool.memset(ones[:], 1.0).then_inc(s_const, 1)
            pool.memset(ident[:], 0.0).then_inc(s_const, 1)
            pool.memset(before, 1.0).then_inc(s_const, 1)
            pool.memset(upto, 1.0).then_inc(s_const, 1)
            pool.wait_ge(s_const, 6)
            pool.affine_select(out=ident[:], in_=ident[:], compare_op=ALU.not_equal, fill=1.0, base=0, pattern=[[-1, P]], channel_multiplier=1).then_inc(s_const, 1)
            pool.affine_select(out=before, in_=before, compare_op=ALU.is_gt, fill=0.0, base=0, pattern=[[1, P]], channel_multiplier=-1).then_inc(s_const, 1)
            pool.affine_select(out=upto, in_=upto, compare_op=ALU.is_ge, fill=0.0, base=0, pattern=[[1, P]], channel_multiplier=-1).then_inc(s_const, 1)

            records = [rec0[:], rec1[:], rec2[:]]
            staged = 0
            for n, g in enumerate(graphs):
                pool.wait_ge(s_fill[n], 16 * FILLS[n])
                with pool.Fori(0, ITERS[n]) as i:
                    for s in range(2):
                        pool.wait_ge(s_idx[s], i * 16 + (staged + 16))
                        pool.wait_ge(s_prg[s], i * 16 + (staged + 16))
                        if n == 0:
                            pool.wait_ge(s_loc[s], i + 1)
                        pool.sem_inc(s_pass, 1)
                        for c in range(SS):
                            if n == 0:
                                record = aring[0:g.parts, s, c, :]
                            else:
                                rw = (0, R1, R2)[n]
                                record = pring[0:g.parts, s, c * rw:(c + 1) * rw]
                            pool.indirect_dma_start(records[n], bass.IndirectOffsetOnAxis(ap=iring[0:g.parts, s, c:c + 1], axis=0), record, None).then_inc(s_sc[s], 16)
                staged += 16 * ITERS[n]
            pool.wait_ge(s_xst, 16 * GROUPS + FREE)
            with pool.Fori(0, C1) as i:
                for s in range(2):
                    pool.wait_ge(s_m1[s], i * 16 + 16)
                    pool.wait_ge(s_mm1[s], i * SC + FREE)
                    pool.sem_inc(s_pass, 1)
                    for c in range(SC):
                        pool.indirect_dma_start(rows1[:, s * SC + c, :], None, xl_d[:], bass.IndirectOffsetOnAxis(ap=mring[:, s, c * R1:c * R1 + 1], axis=0)).then_inc(s_g1[s], 16)
            pool.wait_ge(s_gst, 16)
            with pool.Fori(0, C2) as i:
                for s in range(2):
                    pool.wait_ge(s_m2[s], i * 16 + 16)
                    pool.wait_ge(s_v2[s], i + FREE)
                    pool.sem_inc(s_pass, 1)
                    for c in range(SC):
                        pool.indirect_dma_start(r2[:, s, c * GW:(c + 1) * GW], None, gat_d[:], bass.IndirectOffsetOnAxis(ap=mring[:, s, c * R2:c * R2 + 1], axis=0)).then_inc(s_g2[s], 16)

        @block.vector
        def _(v):
            d = Count(s_dve)

            def own():
                v.wait_ge(s_dve, d.value)

            def signal(s):
                own()
                v.sem_inc(s, 1)

            def inverse_root(y, x_, part):
                d.add(v.tensor_scalar(y.bitcast(I32), x_.bitcast(I32), 1, None, ALU.arith_shift_right))
                own()
                d.add(v.tensor_scalar(y.bitcast(I32), y.bitcast(I32), -1.0, float(0x5F3759DF), ALU.mult, ALU.add))
                own()
                for _ in range(3):
                    d.add(v.scalar_tensor_tensor(out=part, in0=y, scalar=-0.5, in1=y, op0=ALU.mult, op1=ALU.mult))
                    own()
                    d.add(v.tensor_tensor(part, part, x_, ALU.mult))
                    own()
                    d.add(v.scalar_tensor_tensor(out=y, in0=part, scalar=1.5, in1=y, op0=ALU.add, op1=ALU.mult))
                    own()
            ROOT = 11

            d.add(v.memset(empty0, 0.0))
            d.add(v.memset(empty1, 0.0))
            d.add(v.memset(empty2, 0.0))
            d.add(v.memset(zeros, 0.0))
            d.add(v.memset(prow, 0.0))
            d.add(v.memset(aring[:, :, :, EA + 1:EA + 2], 1.0))
            own()
            v.memset(empty0[:, :, EA:EA + 1], -1.0).then_inc(s_fillv, 1)
            v.memset(empty1[:, :, 1:2], -1.0).then_inc(s_fillv, 1)
            v.memset(empty2[:, :, 1:2], -1.0).then_inc(s_fillv, 1)
            v.wait_ge(s_const, 9)
            v.wait_ge(s_key, 16 * 5)

            def group_edges(n, g):
                pp, T, NB = g.parts, g.cols, g.buckets
                k_, si, hi_, m_, c_, s_ = (a[0:pp, 0:T] for a in (key[n], sloti[n], hi, mask, cum, slotf))
                lo_ = (lo0 if n == 0 else lo)[0:pp, 0:T]
                d.add(v.tensor_scalar(hi_, k_, 7, None, ALU.arith_shift_right))
                d.add(v.tensor_scalar(m_, k_, P - 1, None, ALU.bitwise_and))
                d.add(v.memset(s_, 0.0))
                own()
                d.add(v.tensor_copy(lo_, m_))
                start = d.value
                d.base, d.k = start, 0
                with v.Fori(0, NB) as h:
                    d.enter(h, 1)
                    own()
                    d.add(v.tensor_scalar(m_, hi_, iota[0:pp, bass.ds(h, 1)], 0.0, ALU.is_equal, ALU.add, accum_out=cnt[0:pp, bass.ds(h, 1)]))
                d.leave(NB)
                signal(s_cnt)
                v.wait_ge(s_tot, n + 1)
                d.add(v.tensor_scalar(nch[0:NB, 0:1], bank[0][0:NB, 0:1], float(P - 1), None, ALU.add))
                own()
                d.add(v.tensor_copy(nchi[0:NB, :], nch[0:NB, 0:1]))
                own()
                d.add(v.tensor_scalar(nchi[0:NB, :], nchi[0:NB, :], 7, None, ALU.arith_shift_right))
                own()
                d.add(v.tensor_copy(nch[0:NB, 1:2], nchi[0:NB, :]))
                own()
                d.add(v.tensor_scalar(nrep[0:NB, :], ones[0:NB, :], nch[0:NB, 1:2], float(P), ALU.mult, ALU.mult))
                signal(s_nch)
                v.wait_ge(s_base, n + 1)
                d.add(v.tensor_scalar(base[0:pp, 0:NB], bank[1][0:pp, 0:NB], 1.0, None, ALU.subtract))
                d.add(v.tensor_copy(nch[0:NB, 2:3], bank[2][0:NB, 0:1]))
                own()
                d.add(v.tensor_scalar(ends[0:NB, 0:g.chunks], iota_c[0:NB, 0:g.chunks], nch[0:NB, 2:3], None, ALU.is_ge))
                signal(s_cmp)
                with v.Fori(0, NB) as h:
                    d.enter(h, 4)
                    own()
                    d.add(v.tensor_scalar(m_, hi_, iota[0:pp, bass.ds(h, 1)], None, ALU.is_equal))
                    own()
                    d.add(v.tensor_tensor_scan(c_, m_, zeros[0:pp, 0:T], base[0:pp, bass.ds(h, 1)], ALU.add, ALU.add))
                    own()
                    d.add(v.tensor_tensor(c_, c_, m_, ALU.mult))
                    own()
                    d.add(v.tensor_tensor(s_, s_, c_, ALU.add))
                d.leave(NB)
                own()
                d.add(v.tensor_copy(hi_, s_))
                own()
                d.add(v.tensor_scalar(m_, hi_, P - 1, None, ALU.bitwise_and))
                own()
                d.add(v.tensor_scalar(hi_, hi_, 7, None, ALU.arith_shift_right))
                own()
                d.add(v.scalar_tensor_tensor(out=si, in0=m_, scalar=float(g.chunks), in1=hi_, op0=ALU.mult, op1=ALU.add))

            def buckets_by_chunk(n, g):
                v.wait_ge(s_brow, n + 1)
                for a in range(0, g.chunks, 512):
                    b = min(a + 512, g.chunks)
                    d.add(v.tensor_scalar(brow[0:1, a:b], bank[3 + a // 512][0:1, 0:b - a], float(g.buckets - 1), None, ALU.min))
                own()
                return brow[0:1, 0:g.chunks], brow2[0:1, 0:g.chunks]

            group_edges(0, g0)
            signal(s_slot)
            b, b2 = buckets_by_chunk(0, g0)
            b3 = cum[0:1, 0:g0.chunks]
            d.add(v.tensor_scalar(b2, b, float(A0), None, ALU.mult))
            for k in range(1, 7):
                own()
                d.add(v.tensor_scalar(b3, b, float(k * PB0), float(512 - PB0 * A0), ALU.is_ge, ALU.mult))
                own()
                d.add(v.tensor_tensor(b2, b2, b3, ALU.add))
            own()
            d.add(v.tensor_copy(off0, b2))
            group_edges(1, g1)
            d.add(v.tensor_copy(py1[0:g1.parts].bitcast(I32)[:, :, 0], key[0][0:g1.parts, 0:g1.cols]))
            d.add(v.tensor_copy(py1[0:g1.parts, :, 1], lo[0:g1.parts, 0:g1.cols]))
            d.add(v.tensor_copy(py1[0:g1.parts, :, 2], ew[0:g1.parts, 0:g1.cols]))
            signal(s_slot)
            b, _ = buckets_by_chunk(1, g1)
            d.add(v.tensor_scalar(off1, b, float(P), None, ALU.mult))
            group_edges(2, g2)
            d.add(v.tensor_scalar(py2[0:g2.parts].bitcast(I32)[:, :, 0], srcs[0:g2.parts, 0:g2.cols], float(N - 1), None, ALU.min))
            d.add(v.tensor_copy(py2[0:g2.parts, :, 1], lo[0:g2.parts, 0:g2.cols]))
            signal(s_slot)
            b, b2 = buckets_by_chunk(2, g2)
            d.add(v.tensor_scalar(off2n, b, float(2 * HEADS), None, ALU.mult))
            own()
            d.add(v.tensor_scalar(b, b, float(TILES), None, ALU.min))
            own()
            d.add(v.tensor_scalar(b2, b, float(PB), float(512 - PB * GW), ALU.is_ge, ALU.mult))
            own()
            d.add(v.tensor_scalar(b, b, float(GW), None, ALU.mult))
            own()
            d.add(v.tensor_tensor(off2s, b, b2, ALU.add))
            own()

            v.wait_ge(s_pT, 1)
            d.add(v.tensor_copy(flat(pcol[:]), bank[6][:, 0:3 * P]))
            own()
            for c in range(2):
                b1c, gc, bec, mc, vc = (pcol[:, c, a * Q:(a + 1) * Q] for a in range(5))
                scale, shift = bnf[:, c, 0, :], bnf[:, c, 1, :]
                d.add(v.tensor_scalar(root_in[:], vc, BN_EPS_EXPERTS, None, ALU.add))
                own()
                inverse_root(scale, root_in[:], root_part[:])
                d.add(v.tensor_tensor(shift, b1c, mc, ALU.subtract))
                own()
                d.add(v.tensor_tensor(scale, scale, gc, ALU.mult))
                own()
                d.add(v.tensor_tensor(shift, shift, scale, ALU.mult))
                own()
                d.add(v.tensor_tensor(shift, shift, bec, ALU.add))
            signal(s_par)
            v.wait_ge(s_ub, 1)
            d.add(v.tensor_tensor(gb1[:], pcol[:, 2, 0:KG], bank[7][:, 0:KG], ALU.add))
            v.wait_ge(s_w, 16 * weight_loads)
            for c in range(8):
                rows, k = slice(32 * (c % 4), 32 * (c % 4) + 32), c // 4
                for r in range(8):
                    part = r ^ c
                    d.add(v.tensor_scalar(ham[rows, k, 32 * r:32 * r + 32], wrep[rows, 32 * part:32 * part + 32], float(SIGN[r][c]), None, ALU.mult))

            v.wait_ge(s_sd, 16 * 5)
            v.memset(X[:, whole_tiles:TPAD, :], 0.0).then_inc(s_pre, 1)
            d.add(v.memset(acc0, 0.0))
            signal(s_par)

            with v.Fori(0, C0) as i:
                for s in range(2):
                    v.wait_ge(s_bld[s], i * 16 + 16)
                    v.wait_ge(s_mm[s], i * SC + FREE)
                    for c in range(SC):
                        v.tensor_scalar(oh[:, s * SC + c, :], iota[:], oring[:, s * SC + c, EA:EA + 1], None, ALU.is_equal).then_inc(s_oh[s], 1)
            for s in range(2):
                v.wait_ge(s_mm[s], C0 * SC + FREE)
            own()
            for b in range(-(-TILES // PB0)):
                a, z = b * PB0, min((b + 1) * PB0, TILES)
                d.add(v.tensor_copy(acc0[:, a:z, :], bank[1 + b][:, 0:(z - a) * A0].rearrange("p (t w) -> p t w", w=A0)))
            signal(s_add)

            def norm(source, into, done, eps=LN_EPS):
                v.sem_inc(s_vpass, 1)
                for j in range(TG):
                    d.add(v.bn_stats(lnst[:, j, :], source(j)))
                own()
                v.sem_inc(s_vpass, 1)
                for j in range(TG):
                    d.add(v.bn_aggr(lnmv[:, j, :], lnst[:, j, :]))
                own()
                d.add(v.tensor_scalar(root_in[:, 0:TG], lnmv[:, :, 1], eps, None, ALU.add))
                own()
                inverse_root(rstd[:], root_in[:, 0:TG], root_part[:, 0:TG])
                for j in range(TG):
                    d.add(v.tensor_scalar(into[:, j, :], source(j), lnmv[:, j, 0:1], rstd[:, j:j + 1], ALU.subtract, ALU.mult))
                signal(done)
            NORM = 3 * TG + 1 + ROOT

            v.wait_ge(s_xin, 32)
            def dense(part, f, g, hid, y):
                fx = lambda j: tile_at(X, f, j)
                gx = lambda j: tile_at(X, g, j)
                hidden, outs = 0, 0
                after = {}

                def added(kind, e):
                    nonlocal outs
                    for b in range(2):
                        v.wait_ge(s_yp, y(outs + 1))
                        if part != "front" or outs >= 2:
                            v.wait_ge(s_yr, y(outs - 1) + FREE)
                        if kind == "third":
                            for j in range(2):
                                x_ = gx(2 * b + j)
                                ins = v.scalar_tensor_tensor(out=x_, in0=bank[6 + b][:, j * D:(j + 1) * D], scalar=gate[:, 2 * b + j, e:e + 1], in1=x_, op0=ALU.mult, op1=ALU.add)
                        else:
                            x_ = X[:, bass.ds(past(f, TG, 2 * b), 2), :]
                            ins = v.tensor_tensor(x_, x_, bank[6 + b].rearrange("p (t d) -> p t d", d=D), ALU.add)
                        ins.then_inc(s_yr, 1)
                        outs += 1

                if f:
                    norm(fx, xln, s_xln)
                    d.add(v.tensor_scalar(cmx[:], acc0[:, bass.ds(past(f, TG, 0), TG), EA + 1], 1.0, None, ALU.max))
                    own()
                    d.add(v.reciprocal(cmx[:], cmx[:]))
                    own()
                    for j in range(TG):
                        d.add(v.tensor_scalar(attr[:, j, :], tile_at(acc0, f, j)[:, 0:EA], cmx[:, j:j + 1], None, ALU.mult))
                    signal(s_at)
                for kind, e in steps(part):
                    if kind == "turn1":
                        v.wait_ge(s_tr, past(f, 2, 1))
                        v.tensor_copy(xT[:, 1, :], bank[1]).then_inc(s_xTv, 1)
                        v.wait_ge(s_atr, past(f, 1, 1))
                        v.tensor_copy(attrT, bank[2][0:EA, :]).then_inc(s_atT, 1)
                    if kind == "turn2":
                        v.wait_ge(s_tr, past(f, 2, 2))
                        v.tensor_copy(xT[:, 1, :], bank[1]).then_inc(s_xTv, 1)
                    if kind in OUTS:
                        added(kind, e)
                    if kind == "mlp2":
                        v.wait_ge(s_yr, y(outs) + FREE)
                        norm(fx, xln, s_xln)
                    if kind == "logits":
                        v.wait_ge(s_lg, past(f, 1, 1))
                        lg = bank[3][:, 0:TG * NX].rearrange("p (t e) -> p t e", e=NX)
                        d.add(v.tensor_reduce(gmx[:], lg, AX, ALU.max))
                        own()
                        v.tensor_tensor(gate_next[:], lg, gmx[:].unsqueeze(2).broadcast_to([P, TG, NX]), ALU.subtract).then_inc(s_sh, 1)
                        v.wait_ge(s_ex, past(f, 1, 1))
                        d.add(v.tensor_reduce(gsm[:], gate_next[:], AX, ALU.add))
                        own()
                        d.add(v.reciprocal(gsm[:], gsm[:]))
                        own()
                        v.tensor_tensor(gate_next[:], gate_next[:], gsm[:].unsqueeze(2).broadcast_to([P, TG, NX]), ALU.mult).then_inc(s_gt, 1)
                    if kind == "gates":
                        v.wait_ge(s_gtp, past(f, 1, 1))
                        v.tensor_copy(gateT, bank[3][0:NX, :]).then_inc(s_gT, 1)
                    hidden += HIDDEN.get(kind, 0)
                    if kind == "hand":
                        if g:
                            v.wait_ge(s_hp, hid(hidden))
                        v.wait_ge(s_xTa, past(f, 2, 2))
                        v.wait_ge(s_xTv, past(f, 2, 2))
                        v.tensor_copy(flat(xTb), flat(xT)).then_inc(s_xTb, 1)
                if g:
                    v.wait_ge(s_yr, y(outs) + FREE)
                    v.wait_ge(s_xst, past(g, 16, 0) + FREE)
                    norm(gx, xl3, s_xl3)
                if f:
                    v.wait_ge(s_gt, past(f, 1, 1))
                    d.add(v.tensor_copy(gate[:], gate_next[:]))
                    own()

            def dense_counted(part, f, g, hid, y):
                if part == "both":
                    d.enter(f[0], 3 * NORM + 2 + TG + 3 + 1)
                if part == "back":
                    d.leave(GROUPS - 1)
                dense(part, f, g, hid, y)
            dense_turns(v, dense_counted)
            own()

            d.add(v.memset(big, 0.0))
            with v.Fori(0, C1) as i:
                d.enter(i, 2 * SC)
                for s in range(2):
                    v.wait_ge(s_m1[s], i * 16 + 16)
                    v.wait_ge(s_mm1[s], i * SC + FREE)
                    record = mring[:, s, :].bitcast(F32)
                    for c in range(SC):
                        v.tensor_scalar(oh[:, s * SC + c, :], iota[:], record[:, c * R1 + 1:c * R1 + 2], record[:, c * R1 + 2:c * R1 + 3], ALU.is_equal, ALU.mult).then_inc(s_oh1[s], 1)
                for s in range(2):
                    _, at = nc.values_load_multi_w_load_instructions(off1[:, bass.ds(i * (2 * SC) + s * SC, SC)], engines=DVE_ONLY, min_val=0, max_val=(TILES - 1) * P)
                    for c in range(SC):
                        if c % 2 == 0:
                            v.wait_ge(s_mm1[s], i * SC + (c + 2) + FREE)
                        own()
                        a = big[:, :, bass.ds(at[c], P)]
                        sums_ = bank[4 * s + c // 2][:, (c % 2) * KD * P:(c % 2 + 1) * KD * P].rearrange("p (k n) -> p k n", k=KD)
                        d.add(v.tensor_tensor(a, a, sums_, ALU.add))
                    signal(s_ad1[s])
            d.leave(C1)

            with v.Fori(0, GROUPS - 1) as i:
                for m in range(KD):
                    v.wait_ge(s_hc, i * KD + (m + 1) + FREE)
                    v.sem_inc(s_vpass, 1)
                    v.bn_stats(bst[:, m, bass.ds(i, 1), :].rearrange("p a w -> p (a w)"), big[:, m, bass.ds(i * W, W)]).then_inc(s_hb, 1)
            for m in range(KD):
                v.wait_ge(s_hc, (GROUPS - 1) * KD + m + 1 + FREE)
                v.bn_stats(bst[:, m, GROUPS - 1, :], big[:, m, (GROUPS - 1) * W:N]).then_inc(s_hb, 1)
            v.wait_ge(s_hb, GROUPS * KD)
            for m in range(KD):
                d.add(v.bn_aggr(bmv[:, m, :], bst[:, m, :, :].rearrange("p g w -> p (g w)")))
            own()
            gamma, beta = pcol[:, 2, KG + 1:KG + 1 + KD], pcol[:, 2, KG + 1 + KD:KG + 1 + 2 * KD]
            d.add(v.tensor_scalar(root_in[:, 0:KD], bmv[:, :, 1], BN_EPS_GRAPH, None, ALU.add))
            own()
            inverse_root(root_in[:, KD:2 * KD], root_in[:, 0:KD], root_part[:, 0:KD])
            d.add(v.tensor_copy(bsc[:, :, 0], root_in[:, KD:2 * KD]))
            own()
            d.add(v.tensor_tensor(bsc[:, :, 0], bsc[:, :, 0], gamma, ALU.mult))
            own()
            d.add(v.tensor_tensor(bsc[:, :, 1], bmv[:, :, 0], bsc[:, :, 0], ALU.mult))
            own()
            d.add(v.tensor_tensor(bsc[:, :, 1], beta, bsc[:, :, 1], ALU.subtract))
            signal(s_bn)

            d.add(v.memset(nd, 0.0))
            with v.Fori(0, GROUPS) as i:
                d.enter(i, 2 + NORM + 5)
                v.wait_ge(s_nt, i + 1 + FREE)
                for b in range(2):
                    x_ = X[:, tiles(i, 2 * b, 2), :]
                    d.add(v.tensor_tensor(x_, x_, bank[2 + b].rearrange("p (t d) -> p t d", d=D), ALU.add))
                own()
                norm(lambda j: tile(X, i, j), xln, s_nx)
                for k in range(KD):
                    v.wait_ge(s_nca, i * KD + (k + 1))
                    v.tensor_copy(big[:, k, bass.ds(i * W, W)], xT[:, k, :])
                v.wait_ge(s_nh, i + 1)
                h = bank[6][:, 0:TG * HK].rearrange("p (t q) -> p t q", q=HK)
                d.add(v.tensor_copy(G[:, tiles(i), HEADS:GW], h))
                for a, scores in ((0, G), (1, nd)):
                    own()
                    d.add(v.tensor_tensor(hat[:], h, att[:, a, :].unsqueeze(1).broadcast_to([P, TG, HK]), ALU.mult))
                    own()
                    d.add(v.tensor_reduce(scores[:, tiles(i), 0:HEADS], hat[:].rearrange("p t (h k) -> p t h k", h=HEADS), AX, ALU.add))
                signal(s_nhr)
            d.leave(GROUPS)
            signal(s_gs)
            d.add(v.tensor_reduce(gmax[:], G[:, 0:TILES - 1, 0:HEADS].rearrange("p t h -> p h t"), AX, ALU.max))
            own()
            d.add(v.tensor_tensor(gmax[0:TAIL, :], gmax[0:TAIL, :], G[0:TAIL, TILES - 1, 0:HEADS], ALU.max))
            signal(s_mxa)
            v.wait_ge(s_mxp, 1)
            d.add(v.tensor_reduce(gm4[:, 0:1], bank[0][0:HEADS, 0:P], AX, ALU.max))
            own()
            d.add(v.tensor_scalar(gm4[:, 1:1 + HEADS], ident[0:HEADS, 0:HEADS], gm4[:, 0:1], None, ALU.mult))
            signal(s_mxa)
            v.wait_ge(s_mxp, 2)
            d.add(v.tensor_copy(gmax[:], bank[0][:, P:P + HEADS]))
            own()
            score, shift = nd[:, 0:TPAD, 0:HEADS], nd[:, 0:TPAD, HEADS:2 * HEADS]
            d.add(v.tensor_tensor(es[:], score, G[:, :, 0:HEADS], ALU.add))
            d.add(v.tensor_tensor(shift, score, gmax[:].unsqueeze(1).broadcast_to([P, TPAD, HEADS]), ALU.add))
            own()
            d.add(v.scalar_tensor_tensor(out=es[:], in0=es[:], scalar=0.2, in1=es[:], op0=ALU.mult, op1=ALU.max))
            d.add(v.scalar_tensor_tensor(out=shift, in0=shift, scalar=0.2, in1=shift, op0=ALU.mult, op1=ALU.max))
            own()
            d.add(v.tensor_scalar(tmp[0], es[:], SELF_REACH, None, ALU.add))
            own()
            d.add(v.tensor_tensor(shift, shift, tmp[0], ALU.min))
            own()
            d.add(v.tensor_tensor(es[:], es[:], shift, ALU.subtract))
            d.add(v.memset(zero, 0.0))
            signal(s_nd)
            v.wait_ge(s_z2, 2)

            with v.Fori(0, C2) as i:
                d.enter(i, 2 * 5)
                for s in range(2):
                    v.wait_ge(s_m2[s], i * 16 + 16)
                    v.wait_ge(s_a2[s], i * SC + FREE)
                    record = mring[:, s, :].bitcast(F32)
                    for c in range(SC):
                        v.tensor_scalar(oh[:, s * SC + c, :], iota[:], record[:, c * R2 + 1:c * R2 + 2], None, ALU.is_equal).then_inc(s_oh2[s], 1)
                for s in range(2):
                    at_dst = bank[(1, 5)[s]][:, 0:SC * 2 * HEADS].rearrange("p (c w) -> p c w", w=2 * HEADS)
                    row = r2[:, s, :].rearrange("p (c w) -> p c w", w=GW)
                    msg = v2[:, s, :].rearrange("p (c w) -> p c w", w=GW)
                    e = ev[:, s, :].rearrange("p (c h) -> p c h", h=HEADS)
                    v.wait_ge(s_g2[s], i * (16 * SC) + 16 * SC)
                    v.wait_ge(s_d2[s], i + 1)
                    d.add(v.tensor_tensor(e, row[:, :, 0:HEADS], at_dst[:, :, 0:HEADS], ALU.add))
                    own()
                    d.add(v.scalar_tensor_tensor(out=e, in0=e, scalar=0.2, in1=e, op0=ALU.mult, op1=ALU.max))
                    own()
                    d.add(v.tensor_tensor(e, e, at_dst[:, :, HEADS:2 * HEADS], ALU.subtract))
                    own()
                    d.add(v.tensor_scalar(e, e, SELF_REACH, None, ALU.min))
                    signal(s_e2[s])
                    v.wait_ge(s_x2[s], i + 1)
                    d.add(v.tensor_tensor(msg[:, :, HEADS:GW].rearrange("p c (h k) -> p c h k", h=HEADS), row[:, :, HEADS:GW].rearrange("p c (h k) -> p c h k", h=HEADS),
                                          msg[:, :, 0:HEADS].unsqueeze(3).broadcast_to([P, SC, HEADS, HK // HEADS]), ALU.mult))
                    signal(s_v2[s])
            d.leave(C2)

            for s in range(2):
                v.wait_ge(s_a2[s], C2 * SC + FREE)
            v.wait_ge(s_fx, 1)
            for b in range(-(-TILES // PB)):
                a, z = b * PB, min((b + 1) * PB, TILES)
                d.add(v.tensor_copy(sums[:, a:z, :], sumbank[:, 512 * b:512 * b + (z - a) * GW].rearrange("p (t w) -> p t w", w=GW)))
            den, num = sums[:, :, 0:HEADS], sums[:, :, HEADS:GW]
            by_head = lambda a: a.rearrange("p t (h k) -> p t h k", h=HEADS)
            wide = lambda a: a.unsqueeze(3).broadcast_to([P, TILES, HEADS, HK // HEADS])
            vec = lambda a: att[:, a, :].unsqueeze(1).broadcast_to([P, TILES, HK])
            over16 = lambda a: a.broadcast_to([P, TILES, HK])
            own_e = es[:, 0:TILES, :]
            d.add(v.tensor_tensor(by_head(t16), by_head(G[:, 0:TILES, HEADS:GW]), wide(own_e), ALU.mult))
            own()
            d.add(v.tensor_tensor(den, den, own_e, ALU.add))
            d.add(v.tensor_tensor(num, num, t16, ALU.add))
            own()
            d.add(v.reciprocal(den, den))
            own()
            d.add(v.tensor_tensor(by_head(num), by_head(num), wide(den), ALU.mult))
            own()
            d.add(v.tensor_tensor(num, num, vec(2), ALU.add))
            own()
            m1, m2 = tmp[0][:, 0:TILES, 0:1], tmp[1][:, 0:TILES, 0:1]
            m1s, m2s = tmp[0][:, 0:TILES, 0], tmp[1][:, 0:TILES, 0]
            d.add(v.tensor_reduce(m1s, num, AX, ALU.add))
            own()
            d.add(v.tensor_scalar(m1s, m1s, 1.0 / HK, None, ALU.mult))
            own()
            d.add(v.tensor_tensor(num, num, over16(m1), ALU.subtract))
            own()
            d.add(v.tensor_tensor(t16, num, num, ALU.mult))
            own()
            d.add(v.tensor_reduce(m2s, t16, AX, ALU.add))
            own()
            d.add(v.tensor_scalar(m2s, m2s, 1.0 / HK, LN_EPS, ALU.mult, ALU.add))
            own()
            d.add(v.tensor_copy(roots[:, 0, 0:TILES], m2s))
            own()
            inverse_root(roots[:, 1, 0:TILES], roots[:, 0, 0:TILES], roots[:, 2, 0:TILES])
            d.add(v.tensor_tensor(num, num, roots[:, 1, 0:TILES].unsqueeze(2).broadcast_to([P, TILES, HK]), ALU.mult))
            own()
            d.add(v.tensor_tensor(num, num, vec(3), ALU.mult))
            own()
            d.add(v.tensor_tensor(num, num, vec(4), ALU.add))
            own()
            score, rank, ahead = es[:, 0:TILES, :], tmp[0][:, 0:TILES, :], tmp[1][:, 0:TILES, :]
            d.add(v.tensor_reduce(score, num.rearrange("p t (h k) -> p t k h", h=HEADS), AX, ALU.add))
            own()
            d.add(v.tensor_scalar(score, score, 1.0 / HEADS, None, ALU.mult))
            d.add(v.memset(rank, 0.0))
            own()
            best = tmp[2][:, 0:TILES, 0:1]
            d.add(v.tensor_reduce(tmp[2][:, 0:TILES, 0], score, AX, ALU.max))
            for f in range(NE):
                for a, z, op in ((0, f + 1, ALU.is_gt), (f + 1, NE, ALU.is_ge)):
                    if a < z:
                        d.add(v.tensor_tensor(ahead[:, :, a:z], score[:, :, f:f + 1].broadcast_to([P, TILES, z - a]), score[:, :, a:z], op))
                own()
                d.add(v.tensor_tensor(rank, rank, ahead, ALU.add))
                own()
            d.add(v.tensor_scalar(rank, rank, 1.5, None, ALU.is_lt))
            d.add(v.tensor_tensor(score, score, best.broadcast_to([P, TILES, NE]), ALU.subtract))
            signal(s_fe)
            v.wait_ge(s_fx, 2)
            d.add(v.tensor_tensor(score, score, rank, ALU.mult))
            d.add(v.memset(gates, 0.0))
            own()
            d.add(v.tensor_reduce(tmp[2][:, 0:TILES, 0], score, AX, ALU.add))
            own()
            d.add(v.reciprocal(tmp[2][:, 0:TILES, 0], tmp[2][:, 0:TILES, 0]))
            own()
            d.add(v.tensor_tensor(gates[:, 0:TILES, :], score, best.broadcast_to([P, TILES, NE]), ALU.mult))
            own()
            with v.Fori(0, GROUPS) as i:
                for u in range(2 * NE):
                    b, e = u % 2, u // 2
                    v.wait_ge(s_fyp, i * (2 * NE) + (u + 1))
                    if u >= 2:
                        v.wait_ge(s_fyr, i * (2 * NE) + (u - 1) + FREE)
                    for j in range(2):
                        x_ = tile(X, i, 2 * b + j)
                        ins = v.scalar_tensor_tensor(out=x_, in0=bank[2 + b][:, j * D:(j + 1) * D], scalar=gates[:, tiles(i, 2 * b + j, 1), e:e + 1].rearrange("p a e -> p (a e)"), in1=x_, op0=ALU.mult, op1=ALU.add)
                    ins.then_inc(s_fyr, 1)

        @block.scalar
        def _(a):
            load = lambda dst, src: a.dma_start(dst, src).then_inc(s_w, 16)
            for dst, src in weights:
                load(dst, src)
            a.wait_ge(s_fillv, 3)
            for dst, src in param_rows:
                load(dst, src)
            a.wait_ge(s_fill[0], 16 * FILLS[0])
            for dst, src in late_weights:
                load(dst, src)
            a.wait_ge(s_slot, 1)
            for s in range(2):
                a.activation(aring[0:g0.parts, s, :, EA], lo0[0:g0.parts, s * SS:(s + 1) * SS], ACT.Copy).then_inc(s_loc[s], 1)
            with a.Fori(0, ITERS[0] - 1) as i:
                for s in range(2):
                    a.wait_ge(s_sc[s], i * (16 * SS) + 16 * SS)
                    a.activation(aring[0:g0.parts, s, :, EA], lo0[0:g0.parts, bass.ds(i * (2 * SS) + (2 + s) * SS, SS)], ACT.Copy).then_inc(s_loc[s], 1)
            for s in range(2):
                a.wait_ge(s_sc[s], 16 * SS * ITERS[0])
            a.wait_ge(s_sd, 16 * 5)
            with a.Fori(0, C0) as i:
                for s in range(2):
                    a.wait_ge(s_mm[s], i * SC + FREE)
                    a.dma_start(flat(oring[:, s * SC:(s + 1) * SC, :]), r0v[:, bass.ds((i * 2 + s) * (SC * A0), SC * A0)]).then_inc(s_bld[s], 16)
            a.wait_ge(s_par, 2)
            def dense(part, f, g, hid, y):
                hidden = 0

                def take(into, func, bias, scale=1.0):
                    nonlocal hidden
                    a.wait_ge(s_hp, hid(hidden + 1))
                    a.activation(into, bank[4 + hidden % 2], func, bias=bias, scale=scale).then_inc(s_hr, 1)
                    hidden += 1

                for kind, e in steps(part):
                    if kind in ("turn1", "turn2"):
                        a.wait_ge(s_tr, past(f, 2, int(kind[-1])))
                        a.activation(xT[:, 0, :], bank[0], ACT.Copy).then_inc(s_xTa, 1)
                    if kind == "mlp1":
                        for m in range(KG):
                            take(HG[:, m, :], ACT.Relu, gb1[:, m:m + 1])
                    if kind in ("first", "second"):
                        c = BACK.index(kind)
                        for m in range(KD):
                            q = e * KD + m
                            take(HB[:, 4 * c + (e % 2) * KD + m, :], ACT.Relu, bnf[:, c, 1, q:q + 1], bnf[:, c, 0, q:q + 1])
                    if kind == "logits":
                        a.wait_ge(s_sh, past(f, 1, 1))
                        a.activation(gate_next[:], gate_next[:], ACT.Exp).then_inc(s_ex, 1)
                if g:
                    a.wait_ge(s_xl3, past(g, 1, 1))
                    a.dma_start(xl_d[bass.ds(past(g, W, 0), W), :].rearrange("(t p) d -> p t d", p=P), xl3).then_inc(s_xst, 16)

            dense_turns(a, dense)
            with a.Fori(0, GROUPS) as i:
                a.wait_ge(s_hm, i * KD + KD)
                for m in range(KD):
                    a.activation(big[:, m, bass.ds(i * W, W)], bank[m], ACT.Copy).then_inc(s_hc, 1)
            a.wait_ge(s_bn, 1)
            with a.Fori(0, GROUPS) as i:
                a.wait_ge(s_nt, i + FREE)
                a.wait_ge(s_hc, GROUPS * KD + FREE)
                for k in range(KD):
                    a.activation(HB[:, k, :], big[:, k, bass.ds(i * W, W)], ACT.Tanh, bias=bsc[:, k, 1:2], scale=bsc[:, k, 0:1]).then_inc(s_th, 1)
                a.wait_ge(s_nr, i + 1)
                for k in range(KD):
                    a.activation(xT[:, k, :], bank[4 + k], ACT.Copy).then_inc(s_nca, 1)
            with a.Fori(0, C2) as i:
                for s in range(2):
                    a.wait_ge(s_t2[s], i + 1)
                    for b in range(2):
                        c0 = s * SC + 4 * b
                        a.activation(flat(ohT[:, c0:c0 + 4, :]), bank[(0, 2, 3, 4)[2 * s + b]], ACT.Copy).then_inc(s_c2[s], 1)
                for s in range(2):
                    a.wait_ge(s_e2[s], i + 1)
                    a.wait_ge(s_a2[s], i * SC + FREE)
                    a.activation(v2[:, s, :].rearrange("p (c w) -> p c w", w=GW)[:, :, 0:HEADS], ev[:, s, :].rearrange("p (c h) -> p c h", h=HEADS), ACT.Exp).then_inc(s_x2[s], 1)
            a.wait_ge(s_nd, 1)
            a.activation(es[:], es[:], ACT.Exp).then_inc(s_fx, 1)
            a.wait_ge(s_fe, 1)
            a.activation(es[:, 0:TILES, :], es[:, 0:TILES, :], ACT.Exp).then_inc(s_fx, 1)
            bias4 = pcol[:, 2, KG + 1 + 2 * KD:KG + 1 + 2 * KD + NE * KF]
            with a.Fori(0, GROUPS) as i:
                for e in range(NE):
                    for m in range(KF):
                        u = e * KF + m
                        a.wait_ge(s_fhp, i * (NE * KF) + (u + 1))
                        a.activation(HB[:, (e % 2) * KF + m, :], bank[u % 2], ACT.Gelu, bias=bias4[:, u:u + 1]).then_inc(s_fhr, 1)

        @block.tensor
        def _(pe):
            pe.wait_ge(s_const, 9)
            for n, g in enumerate(graphs):
                pp, NB = g.parts, g.buckets
                pe.wait_ge(s_cnt, n + 1)
                pe.matmul(bank[0][0:NB, 0:1], cnt[0:pp, 0:NB], ones[0:pp, 0:1], start=True, stop=True).then_inc(s_tot, 1)
                pe.wait_ge(s_nch, n + 1)
                pe.matmul(bank[1][0:pp, 0:NB], before[0:pp, 0:pp], cnt[0:pp, 0:NB], start=True, stop=False)
                pe.matmul(bank[1][0:pp, 0:NB], nrep[0:NB, 0:pp], before[0:NB, 0:NB], start=False, stop=True)
                pe.matmul(bank[2][0:NB, 0:1], upto[0:NB, 0:NB], nch[0:NB, 1:2], start=True, stop=True).then_inc(s_base, 1)
                pe.wait_ge(s_cmp, n + 1)
                for c in range(0, g.chunks, 512):
                    z = min(c + 512, g.chunks)
                    mm = pe.matmul(bank[3 + c // 512][0:1, 0:z - c], ones[0:NB, 0:1], ends[0:NB, c:z], start=True, stop=True)
                mm.then_inc(s_brow, 1)
            pe.wait_ge(s_w, 16 * weight_loads)
            for c in range(3):
                mm = pe.transpose(bank[6][:, c * P:(c + 1) * P], prow[:, c, :], ident[:])
            mm.then_inc(s_pT, 1)
            pe.wait_ge(s_par, 1)
            for m in range(KG):
                mm = pe.matmul(bank[7][:, m:m + 1], gw1u[:, m * P:(m + 1) * P], pcol[:, 2, KG:KG + 1], start=True, stop=True)
            mm.then_inc(s_ub, 1)

            pe.wait_ge(s_par, 2)
            for b in range(1, 8):
                pe.matmul(bank[b], zero_l0, zero_r0, start=True, stop=False, skip_group_check=True)
            with pe.Fori(0, C0) as i:
                for s in range(2):
                    _, at = nc.values_load_multi_w_load_instructions(off0[:, bass.ds(i * (2 * SC) + s * SC, SC)], engines=PE_ONLY, min_val=0, max_val=7 * 512 - A0)
                    pe.wait_ge(s_bld[s], i * 16 + 16)
                    for c in range(SC):
                        pe.wait_ge(s_oh[s], i * SC + (c + 1))
                        pe.matmul(sumbank0[:, bass.ds(at[c], A0)], oh[:, s * SC + c, :], oring[:, s * SC + c, :], start=False, stop=False, skip_group_check=True).then_inc(s_mm[s], 1)

            def turn(source, banks, j0=0):
                for k in range(KD):
                    for j in range(TG):
                        mm = pe.transpose(banks[k][:, j * P:(j + 1) * P], source[:, j, k * P:(k + 1) * P], ident[:])
                return mm

            pe.wait_ge(s_add, 1)
            cols = lambda j: slice(j * P, (j + 1) * P)

            def dense(part, f, g, hid, y):
                hidden, outs = 0, 0
                after = {("first", 0): 0}

                def into_hidden(products):
                    nonlocal hidden
                    if part != "front" or hidden >= 2:
                        pe.wait_ge(s_hr, hid(hidden - 1) + FREE)
                    for n, (w_, x_) in enumerate(products):
                        mm = pe.matmul(bank[4 + hidden % 2], w_, x_, start=(n == 0), stop=(n == len(products) - 1))
                    mm.then_inc(s_hp, 1)
                    hidden += 1

                def into_outputs(products):
                    nonlocal outs
                    for b in range(2):
                        if part != "front" or outs >= 2:
                            pe.wait_ge(s_yr, y(outs - 1) + FREE)
                        for j in range(2):
                            ps = products(2 * b + j)
                            for n, (x_, w_) in enumerate(ps):
                                mm = pe.matmul(bank[6 + b][:, j * D:(j + 1) * D], x_, w_, start=(n == 0), stop=(n == len(ps) - 1))
                        mm.then_inc(s_yp, 1)
                        outs += 1

                for kind, e in steps(part):
                    if kind == "turn1":
                        pe.wait_ge(s_xln, past(f, 2, 1))
                        turn(xln, bank[0:2]).then_inc(s_tr, 1)
                        pe.wait_ge(s_at, past(f, 1, 1))
                        pe.sem_inc(s_ppass, 1)
                        for j in range(TG):
                            mm = pe.transpose(bank[2][0:EA, cols(j)], attr[:, j, :], ident[:])
                        mm.then_inc(s_atr, 1)
                    if kind == "mlp1":
                        pe.wait_ge(s_xTa, past(f, 2, 1))
                        pe.wait_ge(s_xTv, past(f, 2, 1))
                        pe.wait_ge(s_atT, past(f, 1, 1))
                        for m in range(KG):
                            into_hidden([(gw1[:, k, cols(m)], xT[:, k, :]) for k in range(KD)] + [(gw1e[:, cols(m)], attrT)])
                    if kind == "mlp2":
                        pe.wait_ge(s_hr, hid(after["mlp1", 0]) + FREE)
                        into_outputs(lambda j: [(ones[0:1, :], gb2r)] + [(HG[:, m, cols(j)], gw2[:, m, :]) for m in range(KG)])
                    if kind == "turn2":
                        pe.wait_ge(s_xln, past(f, 2, 2))
                        turn(xln, bank[0:2]).then_inc(s_tr, 1)
                    if kind == "logits":
                        pe.wait_ge(s_xTa, past(f, 2, 2))
                        pe.wait_ge(s_xTv, past(f, 2, 2))
                        for j in range(TG):
                            for k in range(KD):
                                pe.matmul(bank[3][:, j * NX:(j + 1) * NX], xT[:, k, cols(j)], wr[:, k, :], start=(k == 0), stop=False)
                            mm = pe.matmul(bank[3][:, j * NX:(j + 1) * NX], ones[0:1, :], brr, start=False, stop=True)
                        mm.then_inc(s_lg, 1)
                    if kind == "gates":
                        pe.wait_ge(s_gt, past(f, 1, 1))
                        for j in range(TG):
                            mm = pe.transpose(bank[3][0:NX, cols(j)], gate_next[:, j, :], ident[:])
                        mm.then_inc(s_gtp, 1)
                    if kind == "bias":
                        pe.wait_ge(s_gT, past(f, 1, 1))
                        into_outputs(lambda j: [(gateT[:, cols(j)], bo)])
                    if kind == "first":
                        if e == 0:
                            pe.wait_ge(s_xTb, past(f, 1, 1))
                        for m in range(KD):
                            into_hidden([(EW1[:, e, k, cols(m)], xTb[:, k, :]) for k in range(KD)])
                    if kind == "second":
                        pe.wait_ge(s_hr, hid(after["first", e]) + FREE)
                        for m in range(KD):
                            into_hidden([(EW2[:, e, k, cols(m)], HB[:, (e % 2) * KD + k, :]) for k in range(KD)])
                    if kind == "third":
                        pe.wait_ge(s_hr, hid(after["second", e]) + FREE)
                        into_outputs(lambda j: [(HB[:, 4 + (e % 2) * KD + k, cols(j)], EWo[:, e, k, :]) for k in range(KD)])
                    after[kind, e] = hidden
                assert part != "both" or (hidden, outs) == (HP, YP)

            dense_turns(pe, dense)

            pe.wait_ge(s_yr, GROUPS * YP + FREE)
            with pe.Fori(0, C1) as i:
                for s in range(2):
                    pe.wait_ge(s_g1[s], i * (16 * SC) + 16 * SC)
                    pe.wait_ge(s_ad1[s], i + FREE)
                    for c in range(SC):
                        pe.wait_ge(s_oh1[s], i * SC + (c + 1))
                        for k in range(KD):
                            at = (c % 2) * KD * P + k * P
                            mm = pe.matmul(bank[4 * s + c // 2][:, at:at + P], rows1[:, s * SC + c, k * P:(k + 1) * P], oh[:, s * SC + c, :], start=True, stop=True)
                        mm.then_inc(s_mm1[s], 1)
            for s in range(2):
                pe.wait_ge(s_ad1[s], C1 + FREE)
            with pe.Fori(0, GROUPS) as i:
                pe.wait_ge(s_hc, i * KD + FREE)
                for m in range(KD):
                    for k in range(KD):
                        mm = pe.matmul(bank[m], ham[:, k, m * P:(m + 1) * P], big[:, k, bass.ds(i * W, W)], start=(k == 0), stop=(k == KD - 1))
                    mm.then_inc(s_hm, 1)
            with pe.Fori(0, GROUPS) as i:
                pe.wait_ge(s_th, i * KD + KD)
                for j in range(TG):
                    for k in range(KD):
                        mm = pe.transpose(bank[2 + j // 2][:, (j % 2) * D + k * P:(j % 2) * D + (k + 1) * P], HB[:, k, j * P:(j + 1) * P], ident[:])
                mm.then_inc(s_nt, 1)
                pe.wait_ge(s_nx, i + 1)
                turn(xln, bank[4:6]).then_inc(s_nr, 1)
                pe.wait_ge(s_nca, i * KD + KD)
                for j in range(TG):
                    for k in range(KD):
                        mm = pe.matmul(bank[6][:, j * HK:(j + 1) * HK], xT[:, k, j * P:(j + 1) * P], wg[:, k, :], start=(k == 0), stop=(k == KD - 1))
                mm.then_inc(s_nh, 1)
                pe.wait_ge(s_nhr, i + 1)
            pe.wait_ge(s_mxa, 1)
            pe.transpose(bank[0][0:HEADS, 0:P], gmax[:], ident[:]).then_inc(s_mxp, 1)
            pe.wait_ge(s_mxa, 2)
            pe.matmul(bank[0][:, P:P + HEADS], ones[0:HEADS, :], gm4[:, 1:1 + HEADS], start=True, stop=True).then_inc(s_mxp, 1)

            pe.wait_ge(s_nd, 1)
            for b in range(2):
                pe.matmul(bank[6 + b], zero_l, zero_r, start=True, stop=False, skip_group_check=True).then_inc(s_z2, 1)
            with pe.Fori(0, C2) as i:
                for s in range(2):
                    pe.wait_ge(s_c2[s], i * 2 + FREE)
                    for c in range(SC):
                        pe.wait_ge(s_oh2[s], i * SC + (c + 1))
                        mm = pe.transpose(bank[(0, 2, 3, 4)[2 * s + c // 4]][:, (c % 4) * P:(c % 4 + 1) * P], oh[:, s * SC + c, :], ident[:])
                    mm.then_inc(s_t2[s], 1)
                for s in range(2):
                    _, at = nc.values_load_multi_w_load_instructions(off2n[:, bass.ds(i * (2 * SC) + s * SC, SC)], engines=PE_ONLY, min_val=0, max_val=(g2.buckets - 1) * 2 * HEADS)
                    pe.wait_ge(s_c2[s], i * 2 + 2 + FREE)
                    pe.wait_ge(s_v2[s], i + FREE)
                    for c in range(SC):
                        mm = pe.matmul(bank[(1, 5)[s]][:, c * 2 * HEADS:(c + 1) * 2 * HEADS], ohT[:, s * SC + c, :], flat(nd)[:, bass.ds(at[c], 2 * HEADS)], start=True, stop=True)
                    mm.then_inc(s_d2[s], 1)
                for s in range(2):
                    _, at = nc.values_load_multi_w_load_instructions(off2s[:, bass.ds(i * (2 * SC) + s * SC, SC)], engines=PE_ONLY, min_val=0, max_val=2 * 512 - GW)
                    pe.wait_ge(s_v2[s], i + 1 + FREE)
                    for c in range(SC):
                        pe.matmul(sumbank[:, bass.ds(at[c], GW)], oh[:, s * SC + c, :], v2[:, s, c * GW:(c + 1) * GW], start=False, stop=False, skip_group_check=True).then_inc(s_a2[s], 1)

            pe.wait_ge(s_w4, 48)
            pe.wait_ge(s_fe, 1)
            with pe.Fori(0, GROUPS) as i:
                def first4(e):
                    for m in range(KF):
                        u = e * KF + m
                        pe.wait_ge(s_fhr, i * (NE * KF) + max(u - 1, 0) + FREE)
                        for k in range(KD):
                            mm = pe.matmul(bank[u % 2], FW1[:, e, k, m * P:(m + 1) * P], big[:, k, bass.ds(i * W, W)], start=(k == 0), stop=(k == KD - 1))
                        mm.then_inc(s_fhp, 1)

                def second4(e):
                    pe.wait_ge(s_fhr, i * (NE * KF) + (e + 1) * KF + FREE)
                    for b in range(2):
                        u = e * 2 + b
                        pe.wait_ge(s_fyr, i * (2 * NE) + max(u - 1, 0) + FREE)
                        for j in range(2):
                            o = bank[2 + b][:, j * D:(j + 1) * D]
                            pe.matmul(o, ones[0:1, :], fb2r[:, e, :], start=True, stop=False)
                            for m in range(KF):
                                mm = pe.matmul(o, HB[:, (e % 2) * KF + m, (2 * b + j) * P:(2 * b + j + 1) * P], FW2[:, e, m, :], start=False, stop=(m == KF - 1))
                        mm.then_inc(s_fyp, 1)

                first4(0)
                for e in range(1, NE):
                    first4(e)
                    second4(e - 1)
                second4(NE - 1)


def kernel(**inputs):
    import numpy as _np
    import concourse.bacc as _bacc
    from concourse.bass_utils import run_bass_kernel_spmd as _run

    nc = _bacc.Bacc("TRN2", target_bir_lowering=False, num_devices=1)
    arrays, args = {}, {}
    for name, value in inputs.items():
        a = _np.ascontiguousarray(value)
        arrays[f"in_{name}"] = a
        args[name] = nc.dram_tensor(f"in_{name}", a.shape, mybir.dt.from_np(a.dtype), kind="ExternalInput").ap()
    shape = args["x"].shape
    result = nc.dram_tensor("out_x", shape, F32, kind="ExternalOutput").ap()
    build(nc, args, result)
    r = _run(nc, [arrays], core_ids=[0])
    return r.results[0]["out_x"]
```

```python
from contextlib import ExitStack

import concourse.bass as bass
from concourse import mybir

F32 = mybir.dt.float32
I32 = mybir.dt.int32
BF16 = mybir.dt.bfloat16
ALU = mybir.AluOpType
ACT = mybir.ActivationFunctionType
AX = mybir.AxisListType.X
DVE_ONLY = (mybir.EngineType.DVE,)
PE_ONLY = (mybir.EngineType.PE,)

P = 128
LN_EPS = 1e-5
BN_EPS_EXPERTS = 1e-3
BN_EPS_GRAPH = 1e-5
SIGN = [[1, 1, 1, 1, 1, 1, 1, 1], [1, -1, 1, -1, 1, -1, -1, 1], [1, -1, -1, 1, 1, 1, -1, -1],
        [1, 1, -1, -1, 1, -1, 1, -1], [1, -1, -1, -1, -1, 1, 1, 1], [1, 1, -1, 1, -1, -1, -1, 1],
        [1, 1, 1, -1, -1, 1, -1, -1], [1, -1, 1, 1, -1, -1, 1, -1]]
CLAMPED = "buckets_by_chunk bounds the buckets from which the chip works out every place"
SELF_REACH = 80.0


def most(n):
    return max(p for p in range(1, P + 1) if n % p == 0)


class Graph:

    def __init__(self, edges, keys, unroll):
        self.parts = most(edges)
        self.cols = edges // self.parts
        self.buckets = -(-keys // (2 * P)) * 2
        chunks = (edges + self.buckets * (P - 1)) // P
        self.chunks = -(-chunks // unroll) * unroll


class Count:

    def __init__(self, sem):
        self.sem, self.base, self.k, self.turn, self.per = sem, 0, 0, None, 0

    def add(self, instruction, n=1):
        instruction.then_inc(self.sem, n)
        self.k += n

    @property
    def value(self):
        v = self.base + self.k
        return v if self.turn is None else self.turn * self.per + v

    def enter(self, turn, per):
        self.base, self.k, self.turn, self.per = self.base + self.k, 0, turn, per

    def leave(self, turns):
        assert self.k == self.per, (self.k, self.per)
        self.base, self.k, self.turn = self.base + turns * self.per, 0, None


def build(nc, t, out):
    N, D = t["x"].shape
    E0 = t["src"].shape[0]
    E2 = t["L1_ffn_edge_index"].shape[1]
    EA = t["edge_attr_64"].shape[1]
    NX, _, H1 = t["L0_ffn_W1"].shape
    GH = t["L0_gnn_W1"].shape[1]
    NE, _, H2 = t["L1_ffn_W1"].shape
    HEADS = t["L1_ffn_att_src"].shape[0]
    HK = t["L1_ffn_W_gat"].shape[1]
    TG = 4
    TILES = -(-N // P)
    GROUPS = -(-TILES // TG)
    TPAD = GROUPS * TG
    W = TG * P
    TAIL = N - (TILES - 1) * P
    KD, KG, KF = D // P, GH // P, H2 // P
    A0 = EA + 2
    GW = HEADS + HK
    PB = 512 // GW
    PB0 = 512 // A0
    SC = 8
    SS = 16
    R1, R2 = 3, 2
    g0 = Graph(E0, N, 2 * SC)
    g1 = Graph(E0, N, 2 * SC)
    g2 = Graph(E2, 8192, 2 * SC)
    graphs = (g0, g1, g2)
    TMAX = max(g.cols for g in graphs)
    CMAX = max(g.chunks for g in graphs)
    ITERS = [g.cols // (2 * SS) for g in graphs]
    C0, C1, C2 = (g.chunks // (2 * SC) for g in graphs)
    FILL = [2 * SC, 64, 64]
    FILLS = [g.chunks // f for g, f in zip(graphs, FILL)]
    for g, n, f, fs in zip(graphs, ITERS, FILL, FILLS):
        assert n * 2 * SS == g.cols and f * fs == g.chunks
    Q = NX * KD
    HP, YP = KG + NX * 2 * KD, 4 + 2 * NX

    ctx = ExitStack()
    with ctx:
        def sb(name, shape, dt=F32):
            return ctx.enter_context(nc.sbuf_tensor(name, shape, dt))

        def sem(name):
            return ctx.enter_context(nc.semaphore(name))

        def pair(name):
            return [sem(f"{name}_a"), sem(f"{name}_b")]

        rec0 = nc.dram_tensor("rec0", [P * g0.chunks, A0], F32)
        rec1 = nc.dram_tensor("rec1", [P * g1.chunks, R1], I32)
        rec2 = nc.dram_tensor("rec2", [P * g2.chunks, R2], I32)
        slot_d = [nc.dram_tensor(f"slots{n}", [g.parts, g.cols], I32) for n, g in enumerate(graphs)]
        pay_d = [None, nc.dram_tensor("pay1", [g1.parts, g1.cols * R1], I32),
                 nc.dram_tensor("pay2", [g2.parts, g2.cols * R2], I32)]
        xl_d = nc.dram_tensor("xl", [(TPAD + TG) * P, D], F32)
        y_d = nc.dram_tensor("experts_out", [GROUPS * P, NE * TG * D], F32)
        gat_d = nc.dram_tensor("gat", [TPAD * P, GW], F32)

        class Region:
            def __init__(self, name, size):
                self.ap, self.size, self.at = sb(name, [P, size])[:], size, 0

            def restart(self, at=0):
                self.at = at

            def take(self, *shape, rows=P, dt=F32):
                n = 1
                for k in shape:
                    n *= k
                if dt is BF16:
                    n = -(-n // 2)
                a = self.ap[0:rows, self.at:self.at + n]
                self.at += n
                assert self.at <= self.size
                if dt is not F32:
                    a = a.bitcast(dt)
                if len(shape) == 2:
                    a = a.rearrange("p (a b) -> p a b", a=shape[0])
                if len(shape) == 3:
                    a = a.rearrange("p (a b c) -> p a b c", a=shape[0], b=shape[1])
                return a

        rX = Region("rX", TPAD * D)
        X = rX.take(TPAD, D)
        rX.restart()
        key = [rX.take(TMAX, dt=I32) for _ in graphs]
        sloti = [rX.take(TMAX, dt=I32) for _ in graphs]
        hi, mask, mask2 = (rX.take(TMAX, dt=I32) for _ in range(3))
        lo, cum, slotf, zeros = (rX.take(TMAX) for _ in range(4))
        rB = Region("rB", KD * TPAD * P)
        big = rB.take(KD, TPAD * P)
        rB.restart()
        YR = 3
        yring = [rB.take(NE, TG, D) for _ in range(YR)]
        rB.restart()
        EW1, EW2, EWo = (rB.take(NX, KD, H1) for _ in range(3))
        attr = rB.take(TG, EA)
        bo = rB.take(D, rows=NX)
        gb2r = rB.take(D, rows=1)
        brr = rB.take(NX, rows=1)
        wr = rB.take(KD, NX)
        rS = Region("rS", NE * KD * H2 + NE * KF * D)
        ew, srcs = rS.take(TMAX), rS.take(TMAX, dt=I32)
        ends = rS.take(CMAX)
        py1, py2 = rS.take(g1.cols, R1), rS.take(g2.cols, R2)
        rS.restart()
        acc0 = rS.take(TPAD, A0)
        oring = rS.take(2 * SC, A0)
        xTb, xl3 = rS.take(KD, W), rS.take(TG, D)
        rS.restart()
        FW1, FW2 = rS.take(NE, KD, H2), rS.take(NE, KF, D)
        rH = Region("rH", 8 * W)
        HB = rH.take(8, W)
        rH.restart()
        iota_c = rH.take(CMAX)
        brow = rH.take(CMAX, rows=1)
        brow2 = rH.take(CMAX, rows=1)
        gw1u = rH.take(GH)
        empty1, empty2 = rH.take(FILL[1], R1), rH.take(FILL[2], R2)
        rH.restart()
        rows1 = rH.take(2 * SC, D)
        rG = Region("rG", 3328)
        gw1, gw2, gw1e = rG.take(KD, GH), rG.take(KG, D), rG.take(GH, rows=EA)
        rG.restart()
        G, nd = rG.take(TPAD, GW), rG.take(TPAD, 2 * HEADS)
        nd3 = rG.take(3, 2 * 512, dt=BF16)
        rG.restart(nd.shape[1] * 2 * HEADS + TPAD * GW)
        sums, t16 = rG.take(TILES, GW), rG.take(TILES, HK)
        rD = Region("rD", 3 * TG * D)
        aring = rD.take(2, SS, A0)
        rD.restart()
        xln, xT = rD.take(TG, D), rD.take(KD, W)
        rD.restart()
        ohT = rD.take(2 * SC, P, dt=BF16)
        r2, v2, ev = rD.take(2, SC * GW), rD.take(2, SC * GW), rD.take(2, SC * HEADS)
        es = rD.take(TPAD, HEADS)
        v3 = rD.take(2, 3, SC * GW, dt=BF16)
        vrest, at_dst = rD.take(SC * GW), rD.take(SC, 2 * HEADS)
        rD.restart()
        ndrest = rD.take(PB, 2 * HEADS)
        rD.restart(2048)
        hat = rD.take(TPAD, HK)
        rO = Region("rO", 2 * SC * P)
        oh = rO.take(2 * SC, P)
        rO.restart()
        ohb = rO.take(2 * SC, P, dt=BF16)
        rO.restart()
        HG = rO.take(KG, W)
        rO.restart()
        lo0, prow, wrep = rO.take(g0.cols), rO.take(3, P), rO.take(D)
        rA = Region("rA", 2 * W)
        cum2 = rA.take(TMAX)
        rA.restart()
        attrT, gateT = rA.take(W, rows=EA), rA.take(W, rows=NX)
        rA.restart()
        fb2 = rA.take(NE, D)
        rE = Region("rE", (3 * HEADS + NE) * TPAD)
        before, upto = rE.take(P), rE.take(P)
        nrep, cnt, base = rE.take(P), rE.take(64), rE.take(64)
        rE.restart()
        tmp, gates = [rE.take(TPAD, HEADS) for _ in range(3)], rE.take(TPAD, NE)
        iota = sb("iota", [P, P])
        zero = rO.ap[:, 2 * SC * P - 512:2 * SC * P]
        ident = sb("ident", [P, P])
        identb = sb("identb", [P, P], BF16)
        ones = sb("ones", [P, P])
        nch = sb("nch", [64, 3])
        nchi = sb("nchi", [64, 1], I32)
        offs = sb("offs", [P, CMAX], I32)
        off0, off1, off2 = (offs[32 * q:32 * q + 1, 0:g.chunks] for q, g in enumerate(graphs))
        pcol = sb("pcol", [P, 3, P])
        bnf = sb("bnf", [P, 2, 2, Q])
        gb1 = sb("gb1", [P, KG])
        ham = sb("ham", [P, KD, D])
        wg = sb("wg", [P, KD, HK])
        att = sb("att", [P, 5, HK])
        root_in = sb("root_in", [P, Q])
        root_part = sb("root_part", [P, Q])
        lnst = sb("lnst", [P, TG, 6])
        lnmv = sb("lnmv", [P, TG, 2])
        rstd = sb("rstd", [P, TG])
        cmx = sb("cmx", [P, TG])
        gate = sb("gate", [P, TG, NX])
        gate_next = sb("gate_next", [P, TG, NX])
        gmx = sb("gmx", [P, TG])
        gsm = sb("gsm", [P, TG])
        iring = sb("iring", [P, 2, SS], I32)
        pring = sb("pring", [P, 2, SS * R1], I32)
        mring = sb("mring", [P, 2, SC * R1], I32)
        bst = sb("bst", [P, KD, GROUPS, 6])
        bmv = sb("bmv", [P, KD, 2])
        bsc = sb("bsc", [P, KD, 2])
        roots = sb("roots", [P, 3, TPAD])
        gmax = sb("gmax", [P, HEADS])
        ystage = [ham[:].rearrange("p k n -> p (k n)"), sb("ystage", [P, 2 * D])[:]]
        assert KD == 2
        gm4 = sb("gm4", [HEADS, 1 + HEADS])

        psum = ctx.enter_context(nc.psum_tensor("psum", [P, 8 * 512], F32))[:]
        bank = [psum[:, 512 * n:512 * (n + 1)] for n in range(8)]
        sumbank0, sumbank = psum[:, 512:], psum[:, 6 * 512:]
        assert TILES <= 7 * PB0 and TILES < 2 * PB

        def tiles(i, j=0, n=TG):
            return bass.ds(i * TG + j, n)

        def tile_at(x, g, j):
            return x[:, bass.ds(past(g, TG, j), 1), :].rearrange("p a d -> p (a d)")

        def tile(x, i, j):
            return x[:, tiles(i, j, 1), :].rearrange("p a d -> p (a d)")

        empty0 = rB.ap[:, 0:FILL[0] * A0].rearrange("p (c w) -> p c w", w=A0)
        empty0f = rB.ap[:, 0:FILL[0] * A0]
        zero_l, zero_r = zero[:, 0:P], zero[:]
        acc0f = acc0.rearrange("p t w -> p (t w)")
        zero_l0, zero_r0 = acc0f[:, 0:P], acc0f[:, 0:512]

        by_k = lambda a: a.rearrange("(k p) n -> p k n", p=P)
        row = lambda a: a.rearrange("(a n) -> a n", a=1)
        experts = lambda a: a.rearrange("e (k p) n -> p e k n", p=P)
        gW1 = t["L0_gnn_W1"]
        weights = [(gw1u, gW1[D + EA:, :]), (wrep[0:32, :], t["L1_gnn_weight"]), (wrep[32:64, :], t["L1_gnn_weight"]),
                   (wrep[64:96, :], t["L1_gnn_weight"]), (wrep[96:128, :], t["L1_gnn_weight"]),
                   (gw1, by_k(gW1[0:D, :])), (gw1e, gW1[D:D + EA, :]), (gw2, by_k(t["L0_gnn_W2"])), (gb2r, row(t["L0_gnn_b2"])),
                   (brr, row(t["L0_ffn_br"])), (wr, by_k(t["L0_ffn_Wr"])), (bo, t["L0_ffn_bo"]), (wg[:], by_k(t["L1_ffn_W_gat"]))]
        for q, name in enumerate(("att_src", "att_dst", "b_gat", "ln_gamma", "ln_beta")):
            vector = t["L1_ffn_" + name]
            vector = vector.rearrange("(a h) k -> a (h k)", a=1) if q < 2 else row(vector)
            weights.append((att[:, q, :], vector.broadcast_to([P, HK])))
        param_rows = []
        for c, names in enumerate((("b1", "g1", "be1", "m1", "v1"), ("b2", "g2", "be2", "m2", "v2"))):
            for q, name in enumerate(names):
                param_rows.append((prow[q * Q:(q + 1) * Q, c, :], t["L0_ffn_" + name].rearrange("e (m p) -> (e m) p", p=P)))
        at = 0
        for a in (t["L0_gnn_b1"].rearrange("(m p) -> m p", p=P), t["L0_gnn_u"][0:1, :], t["L1_gnn_gamma"].rearrange("(m p) -> m p", p=P),
                  t["L1_gnn_beta"].rearrange("(m p) -> m p", p=P), t["L1_ffn_b1"].rearrange("e (m p) -> (e m) p", p=P)):
            param_rows.append((prow[at:at + a.shape[0], 2, :], a))
            at += a.shape[0]
        late_weights = [(EW1, experts(t["L0_ffn_W1"])), (EW2, experts(t["L0_ffn_W2"])), (EWo, experts(t["L0_ffn_Wo"]))]
        weight_loads = len(weights) + len(param_rows) + len(late_weights)

        s_const = sem("constants")
        s_dve = sem("dve_own")
        s_key = sem("keys_in")
        s_fillv = sem("empty_records")
        s_fill = [sem(f"records{n}_emptied") for n in range(3)]
        s_cnt = sem("bucket_counts")
        s_tot = sem("bucket_totals")
        s_nch = sem("bucket_chunks")
        s_base = sem("bucket_starts")
        s_cmp = sem("bucket_ends_compared")
        s_brow = sem("buckets_by_chunk")
        s_slot = sem("slots_ready")
        s_sd = sem("slots_stored")
        s_idx = pair("scatter_indices_in")
        s_prg = pair("scatter_payload_in")
        s_loc = pair("scatter_nodes_in")
        s_sc = pair("scattered")
        s_pass = sem("pool_passed")
        s_vpass = sem("dve_passed")
        s_ppass = sem("pe_passed")
        s_spass = sem("sp_passed")
        s_w = sem("weights_in")
        s_w4 = sem("weights4_in")
        s_xin = sem("x_in")
        s_pre = sem("preset")
        s_bld = pair("records0_back")
        s_oh = pair("onehots0")
        s_mm = pair("chunk_sums0")
        s_add = sem("sums0_in_sbuf")
        s_pT = sem("parameters_turned")
        s_par = sem("parameters_ready")
        s_ub = sem("u_bias")
        s_xln = sem("tokens_normed")
        s_tr = sem("tokens_turned")
        s_xTa = sem("turned_in_sbuf_act")
        s_xTv = sem("turned_in_sbuf_dve")
        s_at = sem("edge_means")
        s_atr = sem("edge_means_turned")
        s_atT = sem("edge_means_in_sbuf")
        s_hp = sem("hidden_psum")
        s_hr = sem("hidden_sbuf")
        s_yp = sem("outputs_psum")
        s_yr = sem("outputs_added")
        s_lg = sem("router_logits")
        s_sh = sem("router_shifted")
        s_ex = sem("router_exp")
        s_gt = sem("router_gates")
        s_gtp = sem("gates_turned")
        s_gT = sem("gates_in_sbuf")
        s_xTb = sem("turned_handed_over")
        s_xl3 = sem("tokens3_normed")
        s_xst = sem("tokens3_stored")
        s_m1 = pair("records1_back")
        s_g1 = pair("rows1_gathered")
        s_oh1 = pair("onehots1")
        s_mm1 = pair("chunk_sums1")
        s_ad1 = pair("added1")
        s_hm = sem("octonion_psum")
        s_hc = sem("octonion_sbuf")
        s_hb = sem("octonion_stats")
        s_bn = sem("batch_norm_ready")
        s_th = sem("tanh_done")
        s_nt = sem("tanh_turned")
        s_ta = sem("tanh_added")
        s_nx = sem("tokens4_normed")
        s_nr = sem("tokens4_turned")
        s_nca = sem("tokens4_sbuf_act")
        s_nb = sem("tokens4_kept")
        s_nh = sem("projected")
        s_nhr = sem("projected_taken")
        s_gs = sem("rows2_ready")
        s_gst = sem("rows2_stored")
        s_mxa = sem("max_asked")
        s_mxp = sem("max_turned")
        s_nd = sem("node_table_ready")
        s_m2 = pair("records2_back")
        s_g2 = pair("rows2_gathered")
        s_oh2 = pair("onehots2")
        s_t2 = pair("onehots2_turned")
        s_c2 = pair("onehots2_sbuf")
        s_d2 = pair("destination_values")
        s_e2 = pair("scores_shifted")
        s_x2 = pair("scores_exp")
        s_v2 = pair("messages")
        s_a2 = pair("messages_summed")
        s_z2 = sem("sums2_zeroed")
        s_fe = sem("final_asked")
        s_fx = sem("final_exp")
        s_fhp = sem("hidden4_psum")
        s_fhr = sem("hidden4_sbuf")
        s_fyp = sem("outputs4_psum")
        s_fyr = sem("outputs4_staged")
        s_yst = pair("outputs4_stored")
        s_yin = [sem(f"outputs4_back{n}") for n in range(3)]
        s_comb = sem("outputs4_added")
        s_out = sem("stored")

        FREE = 1
        FREE_PAIR = KD + FREE
        free_again = [s_nhr, s_nb, s_nt, s_hr, s_yr, s_fhr, s_fyr] + s_yst
        for two in (s_mm, s_mm1, s_v2, s_a2, s_ad1, s_c2):
            free_again += two

        def halves(a, n):
            return a.rearrange("(p c) -> p c", p=n)

        r0v = rec0[:].rearrange("(p c) w -> p (c w)", p=P)
        r1v = rec1[:].rearrange("(p c) w -> p (c w)", p=P)
        r2v = rec2[:].rearrange("(p c) w -> p (c w)", p=P)
        flat = lambda a: a.rearrange("p a b -> p (a b)")
        whole_tiles = N // P

        BACK = ("first", "second", "third")
        order = [("second", 0), ("first", 1), ("third", 0), ("second", 1), ("turn1", 0), ("first", 2), ("third", 1), ("mlp1", 0),
                 ("second", 2), ("first", 3), ("third", 2), ("mlp2", 0), ("second", 3), ("first", 4), ("third", 3), ("second", 4),
                 ("turn2", 0), ("first", 5), ("third", 4), ("logits", 0), ("second", 5), ("first", 6), ("third", 5), ("gates", 0),
                 ("second", 6), ("first", 7), ("third", 6), ("bias", 0), ("hand", 0), ("second", 7), ("first", 0), ("third", 7)]
        assert [e for k, e in order if k == "third"] == list(range(NX))
        HIDDEN = {"first": KD, "second": KD, "mlp1": KG}
        OUTS = {"third": 2, "mlp2": 2, "bias": 2}
        FRONT_H, FRONT_Y = KG + KD, 4

        def steps(part):
            if part == "front":
                return [x for x in order if x[0] not in BACK or x == ("first", 0)]
            if part == "back":
                return [x for x in order if x[0] in BACK and x != ("first", 0)]
            return order

        def past(g, per, k):
            i, more, *factor = g
            return more * per + k if i is None else i * (per * (factor or [1])[0]) + (more * per + k)

        def dense_turns(engine, turn):
            turn("front", (None, 0), None, lambda k: k, lambda k: k)
            with engine.Fori(0, GROUPS - 1) as i:
                turn("both", (i, 1), (i, 0), lambda k: i * HP + (FRONT_H + k), lambda k: i * YP + (FRONT_Y + k))
            turn("back", None, (None, GROUPS - 1), lambda k: (GROUPS - 1) * HP + FRONT_H + k, lambda k: (GROUPS - 1) * YP + FRONT_Y + k)

        EPG = C2 // GROUPS
        REST = C2 - EPG * GROUPS
        work = []
        for e in range(NE):
            work += [("h", e, m) for m in range(KF)]
            if e:
                work += [("o", e - 1, b) for b in range(2)]
        work += [("o", NE - 1, b) for b in range(2)]
        cost = [1 if w[0] == "h" else 2 for w in work]
        pieces = [[[] for _ in range(3)] for _ in range(EPG)]
        for n, w in enumerate(work):
            piece = sum(cost[:n]) * 3 * EPG // sum(cost)
            pieces[piece // 3][piece % 3].append(w)
        nothing = [[], [], []]

        ring_turns = (GROUPS - 1) // YR
        assert GROUPS == ring_turns * YR + 1

        def edge_turns(engine, turn):
            with engine.Fori(0, GROUPS) as i:
                for q in range(EPG):
                    turn((i, q, EPG), (i, 0), pieces[q])
            with engine.Fori(0, REST) as i:
                turn((i, EPG * GROUPS), None, nothing)

        block = ctx.enter_context(nc.Block())

        @block.sync
        def _(sp):
            sp.dma_start(key[0][0:g0.parts, 0:g0.cols], halves(t["src"], g0.parts)).then_inc(s_key, 16)
            sp.dma_start(key[1][0:g1.parts, 0:g1.cols], halves(t["dst"], g1.parts)).then_inc(s_key, 16)
            sp.dma_start(key[2][0:g2.parts, 0:g2.cols], halves(t["L1_ffn_edge_index"][1], g2.parts)).then_inc(s_key, 16)
            sp.dma_start(ew[0:g1.parts, 0:g1.cols], halves(t["edge_weight"], g1.parts)).then_inc(s_key, 16)
            sp.dma_start(srcs[0:g2.parts, 0:g2.cols], halves(t["L1_ffn_edge_index"][0], g2.parts)).then_inc(s_key, 16)
            sp.wait_ge(s_fillv, 3)
            with sp.Fori(0, FILLS[0]) as i:
                sp.dma_start(r0v[:, bass.ds(i * FILL[0] * A0, FILL[0] * A0)], empty0f).then_inc(s_fill[0], 16)
            with sp.Fori(0, FILLS[1]) as i:
                sp.dma_start(r1v[:, bass.ds(i * FILL[1] * R1, FILL[1] * R1)], flat(empty1).bitcast(I32)).then_inc(s_fill[1], 16)
            with sp.Fori(0, FILLS[2]) as i:
                sp.dma_start(r2v[:, bass.ds(i * FILL[2] * R2, FILL[2] * R2)], flat(empty2).bitcast(I32)).then_inc(s_fill[2], 16)

            attr_v = t["edge_attr_64"].rearrange("(p c) w -> p c w", p=g0.parts)

            def store_slots(n, g):
                sp.wait_ge(s_slot, n + 1)
                sp.dma_start(slot_d[n][:], sloti[n][0:g.parts, 0:g.cols]).then_inc(s_sd, 16)
                if n:
                    py = (None, py1, py2)[n]
                    sp.dma_start(pay_d[n][:], flat(py[0:g.parts]).bitcast(I32)).then_inc(s_sd, 16)

            scattered = 0
            for n, g in enumerate(graphs):
                if n == 0:
                    store_slots(0, g0)
                    sp.wait_ge(s_sd, 16)
                if n == 1:
                    store_slots(1, g1)
                    store_slots(2, g2)
                    sp.wait_ge(s_sd, 16 * 5)
                    sp.wait_ge(s_pre, 1)
                    sp.dma_start(X[:, 0:whole_tiles, :], t["x"][0:whole_tiles * P, :].rearrange("(t p) d -> p t d", p=P)).then_inc(s_xin, 16)
                    sp.dma_start(X[0:TAIL, whole_tiles, :], t["x"][whole_tiles * P:N, :]).then_inc(s_xin, 16)

                def stage(n, g, at, s):
                    sp.dma_start(iring[0:g.parts, s, :], slot_d[n][:, bass.ds(at, SS)]).then_inc(s_idx[s], 16)
                    if n == 0:
                        sp.dma_start(aring[0:g.parts, s, :, 0:EA], attr_v[:, bass.ds(at, SS), :]).then_inc(s_prg[s], 16)
                    else:
                        rw = (0, R1, R2)[n]
                        sp.dma_start(pring[0:g.parts, s, 0:SS * rw], pay_d[n][:, bass.ds(at * rw, SS * rw)]).then_inc(s_prg[s], 16)

                for s in range(2):
                    if n:
                        sp.wait_ge(s_sc[s], scattered)
                    stage(n, g, s * SS, s)
                with sp.Fori(0, ITERS[n] - 1) as i:
                    for s in range(2):
                        sp.wait_ge(s_sc[s], i * (16 * SS) + (scattered + 16 * SS))
                        sp.sem_inc(s_spass, 1)
                        stage(n, g, i * (2 * SS) + (2 + s) * SS, s)
                scattered += 16 * SS * ITERS[n]

            for s in range(2):
                sp.dma_start(mring[:, s, 0:SC * R1], r1v[:, s * (SC * R1):(s + 1) * (SC * R1)]).then_inc(s_m1[s], 16)
            with sp.Fori(0, C1 - 1) as i:
                for s in range(2):
                    sp.wait_ge(s_g1[s], i * (16 * SC) + 16 * SC)
                    sp.sem_inc(s_spass, 1)
                    sp.wait_ge(s_oh1[s], i * SC + SC)
                    sp.sem_inc(s_spass, 1)
                    sp.dma_start(mring[:, s, 0:SC * R1], r1v[:, bass.ds(i * (2 * SC * R1) + (2 + s) * (SC * R1), SC * R1)]).then_inc(s_m1[s], 16)
            sp.dma_start(FW1, t["L1_ffn_W1"].rearrange("e (k p) n -> p e k n", p=P)).then_inc(s_w4, 16)
            sp.dma_start(FW2, t["L1_ffn_W2"].rearrange("e (k p) n -> p e k n", p=P)).then_inc(s_w4, 16)
            sp.dma_start(flat(fb2), t["L1_ffn_b2"].rearrange("(a e) d -> a (e d)", a=1).broadcast_to([P, NE * D])).then_inc(s_w4, 16)
            sp.wait_ge(s_gs, 1)
            sp.dma_start(gat_d[:].rearrange("(t p) w -> p t w", p=P), G).then_inc(s_gst, 16)
            for s in range(2):
                sp.wait_ge(s_g1[s], C1 * 16 * SC)
                sp.wait_ge(s_oh1[s], C1 * SC)
                sp.wait_ge(s_sc[s], scattered)
            for s in range(2):
                sp.dma_start(mring[:, s, 0:SC * R2], r2v[:, s * (SC * R2):(s + 1) * (SC * R2)]).then_inc(s_m2[s], 16)
            with sp.Fori(0, C2 - 1) as i:
                for s in range(2):
                    sp.wait_ge(s_g2[s], i * (16 * SC) + 16 * SC)
                    sp.sem_inc(s_spass, 1)
                    sp.wait_ge(s_oh2[s], i * SC + SC)
                    sp.sem_inc(s_spass, 1)
                    sp.dma_start(mring[:, s, 0:SC * R2], r2v[:, bass.ds(i * (2 * SC * R2) + (2 + s) * (SC * R2), SC * R2)]).then_inc(s_m2[s], 16)
            def fetch(g, slot):
                sp.dma_start(yring[slot].rearrange("p e t d -> p (e t d)"), y_d[bass.ds(past(g, P, 0), P), :]).then_inc(s_yin[slot], 16)

            def store(g):
                sp.dma_start(out[bass.ds(past(g, W, 0), W), :].rearrange("(t p) d -> p t d", p=P), X[:, bass.ds(past(g, TG, 0), TG), :]).then_inc(s_out, 16)

            sp.wait_ge(s_fhp, GROUPS * NE * KF)
            sp.wait_ge(s_fyp, GROUPS * 2 * NE)
            for b in range(2):
                sp.wait_ge(s_yst[b], 16 * GROUPS * NE + FREE)
            for slot in range(YR):
                fetch((None, slot), slot)
            with sp.Fori(0, ring_turns - 1) as i:
                for slot in range(YR):
                    sp.wait_ge(s_comb, i * YR + (slot + 1))
                    sp.sem_inc(s_spass, 1)
                    store((i, slot, YR))
                    fetch((i, slot + YR, YR), slot)
            for g in range((ring_turns - 1) * YR, GROUPS - 1):
                sp.wait_ge(s_comb, g + 1)
                store((None, g))
                if g + YR < GROUPS:
                    fetch((None, g + YR), g % YR)
            sp.wait_ge(s_comb, GROUPS)
            last = (GROUPS - 1) * TG
            stores = GROUPS
            if last < whole_tiles:
                sp.dma_start(out[last * P:whole_tiles * P, :].rearrange("(t p) d -> p t d", p=P), X[:, last:whole_tiles, :]).then_inc(s_out, 16)
                stores += 1
            sp.dma_start(out[whole_tiles * P:N, :], X[0:TAIL, whole_tiles, :]).then_inc(s_out, 16)
            sp.wait_ge(s_out, 16 * stores)

        @block.gpsimd
        def _(pool):
            for s in free_again:
                pool.sem_inc(s, FREE)
            pool.sem_inc(s_hc, FREE_PAIR)
            pool.iota(iota_c, [[1, CMAX]], base=0, channel_multiplier=0, allow_small_or_imprecise_dtypes=True).then_inc(s_const, 1)
            pool.iota(iota[:], [[1, P]], base=0, channel_multiplier=0, allow_small_or_imprecise_dtypes=True).then_inc(s_const, 1)
            pool.memset(ones[:], 1.0).then_inc(s_const, 1)
            pool.memset(ident[:], 0.0).then_inc(s_const, 1)
            pool.memset(before, 1.0).then_inc(s_const, 1)
            pool.memset(upto, 1.0).then_inc(s_const, 1)
            pool.wait_ge(s_const, 6)
            pool.affine_select(out=ident[:], in_=ident[:], compare_op=ALU.not_equal, fill=1.0, base=0, pattern=[[-1, P]], channel_multiplier=1).then_inc(s_const, 1)
            pool.affine_select(out=before, in_=before, compare_op=ALU.is_gt, fill=0.0, base=0, pattern=[[1, P]], channel_multiplier=-1).then_inc(s_const, 1)
            pool.affine_select(out=upto, in_=upto, compare_op=ALU.is_ge, fill=0.0, base=0, pattern=[[1, P]], channel_multiplier=-1).then_inc(s_const, 1)

            records = [rec0[:], rec1[:], rec2[:]]
            staged = 0

            def scatter(n, g, i):
                for s in range(2):
                    pool.wait_ge(s_idx[s], past(i, 16, staged + 16))
                    pool.wait_ge(s_prg[s], past(i, 16, staged + 16))
                    if n == 0:
                        pool.wait_ge(s_loc[s], past(i, 1, 1))
                    pool.sem_inc(s_pass, 1)
                    for c in range(SS):
                        if n == 0:
                            record = aring[0:g.parts, s, c, :]
                        else:
                            rw = (0, R1, R2)[n]
                            record = pring[0:g.parts, s, c * rw:(c + 1) * rw]
                        pool.indirect_dma_start(records[n], bass.IndirectOffsetOnAxis(ap=iring[0:g.parts, s, c:c + 1], axis=0), record, None).then_inc(s_sc[s], 16)

            for n, g in enumerate(graphs):
                pool.wait_ge(s_fill[n], 16 * FILLS[n])
                with pool.Fori(0, ITERS[n] - (n == 2)) as i:
                    scatter(n, g, (i, 0))
                if n < 2:
                    staged += 16 * ITERS[n]
            pool.wait_ge(s_xst, 16 * (GROUPS + 1))
            with pool.Fori(0, C1) as i:
                for s in range(2):
                    pool.wait_ge(s_m1[s], i * 16 + 16)
                    pool.wait_ge(s_mm1[s], i * SC + FREE)
                    pool.sem_inc(s_pass, 1)
                    for c in range(SC):
                        pool.indirect_dma_start(rows1[:, s * SC + c, :], None, xl_d[:], bass.IndirectOffsetOnAxis(ap=mring[:, s, c * R1:c * R1 + 1], axis=0)).then_inc(s_g1[s], 16)
            scatter(2, g2, (None, ITERS[2] - 1))
            pool.wait_ge(s_gst, 16)
            with pool.Fori(0, C2) as i:
                for s in range(2):
                    pool.wait_ge(s_m2[s], i * 16 + 16)
                    pool.wait_ge(s_v2[s], i + FREE)
                    pool.sem_inc(s_pass, 1)
                    for c in range(SC):
                        pool.indirect_dma_start(r2[:, s, c * GW:(c + 1) * GW], None, gat_d[:], bass.IndirectOffsetOnAxis(ap=mring[:, s, c * R2:c * R2 + 1], axis=0)).then_inc(s_g2[s], 16)

        @block.vector
        def _(v):
            d = Count(s_dve)

            def own():
                v.wait_ge(s_dve, d.value)

            def signal(s):
                own()
                v.sem_inc(s, 1)

            def three_parts(parts, x_, rest):
                own()
                d.add(v.tensor_copy(parts[0], x_))
                own()
                d.add(v.tensor_tensor(rest, x_, parts[0], ALU.subtract))
                own()
                d.add(v.tensor_copy(parts[1], rest))
                own()
                d.add(v.tensor_tensor(parts[2], rest, parts[1], ALU.subtract))

            def inverse_root(y, x_, part):
                d.add(v.tensor_scalar(y.bitcast(I32), x_.bitcast(I32), 1, None, ALU.arith_shift_right))
                own()
                d.add(v.tensor_scalar(y.bitcast(I32), y.bitcast(I32), -1.0, float(0x5F3759DF), ALU.mult, ALU.add))
                own()
                for _ in range(3):
                    d.add(v.scalar_tensor_tensor(out=part, in0=y, scalar=-0.5, in1=y, op0=ALU.mult, op1=ALU.mult))
                    own()
                    d.add(v.tensor_tensor(part, part, x_, ALU.mult))
                    own()
                    d.add(v.scalar_tensor_tensor(out=y, in0=part, scalar=1.5, in1=y, op0=ALU.add, op1=ALU.mult))
                    own()
            ROOT = 11

            d.add(v.memset(empty0, 0.0))
            d.add(v.memset(empty1, 0.0))
            d.add(v.memset(empty2, 0.0))
            d.add(v.memset(zeros, 0.0))
            d.add(v.memset(prow, 0.0))
            d.add(v.memset(aring[:, :, :, EA + 1:EA + 2], 1.0))
            own()
            v.memset(empty0[:, :, EA:EA + 1], -1.0).then_inc(s_fillv, 1)
            v.memset(empty1[:, :, 1:2], -1.0).then_inc(s_fillv, 1)
            v.memset(empty2[:, :, 1:2], -1.0).then_inc(s_fillv, 1)
            v.wait_ge(s_const, 9)
            v.wait_ge(s_key, 16 * 5)

            def group_edges(n, g):
                pp, T, NB = g.parts, g.cols, g.buckets
                k_, si, hi_, m_, m2_, c_, c2_, s_ = (a[0:pp, 0:T] for a in (key[n], sloti[n], hi, mask, mask2, cum, cum2, slotf))
                lo_ = (lo0 if n == 0 else lo)[0:pp, 0:T]
                d.add(v.tensor_scalar(hi_, k_, 7, None, ALU.arith_shift_right))
                d.add(v.tensor_scalar(m_, k_, P - 1, None, ALU.bitwise_and))
                d.add(v.memset(s_, 0.0))
                own()
                d.add(v.tensor_copy(lo_, m_))
                start = d.value
                d.base, d.k = start, 0
                own()
                with v.Fori(0, NB // 2) as h:
                    d.enter(h, 2)
                    for b, into in enumerate((m_, m2_)):
                        v.wait_ge(s_dve, d.value - 1)
                        at_b = bass.ds(h * 2 + b, 1)
                        d.add(v.tensor_scalar(into, hi_, iota[0:pp, at_b], 0.0, ALU.is_equal, ALU.add, accum_out=cnt[0:pp, at_b]))
                d.leave(NB // 2)
                signal(s_cnt)
                v.wait_ge(s_tot, n + 1)
                d.add(v.tensor_scalar(nch[0:NB, 0:1], bank[0][0:NB, 0:1], float(P - 1), None, ALU.add))
                own()
                d.add(v.tensor_copy(nchi[0:NB, :], nch[0:NB, 0:1]))
                own()
                d.add(v.tensor_scalar(nchi[0:NB, :], nchi[0:NB, :], 7, None, ALU.arith_shift_right))
                own()
                d.add(v.tensor_copy(nch[0:NB, 1:2], nchi[0:NB, :]))
                own()
                d.add(v.tensor_scalar(nrep[0:NB, :], ones[0:NB, :], nch[0:NB, 1:2], float(P), ALU.mult, ALU.mult))
                signal(s_nch)
                v.wait_ge(s_base, n + 1)
                d.add(v.tensor_scalar(base[0:pp, 0:NB], bank[1][0:pp, 0:NB], 1.0, None, ALU.subtract))
                d.add(v.tensor_copy(nch[0:NB, 2:3], bank[2][0:NB, 0:1]))
                own()
                d.add(v.tensor_scalar(ends[0:NB, 0:g.chunks], iota_c[0:NB, 0:g.chunks], nch[0:NB, 2:3], None, ALU.is_ge))
                signal(s_cmp)
                with v.Fori(0, NB // 2) as h:
                    d.enter(h, 6)
                    own()
                    for b, (mask_, count_) in enumerate(((m_, c_), (m2_, c2_))):
                        d.add(v.tensor_scalar(mask_, hi_, iota[0:pp, bass.ds(h * 2 + b, 1)], None, ALU.is_equal))
                    for b, (mask_, count_) in enumerate(((m_, c_), (m2_, c2_))):
                        v.wait_ge(s_dve, d.value - 1)
                        d.add(v.tensor_tensor_scan(count_, mask_, zeros[0:pp, 0:T], base[0:pp, bass.ds(h * 2 + b, 1)], ALU.add, ALU.add))
                    for b, (mask_, count_) in enumerate(((m_, c_), (m2_, c2_))):
                        v.wait_ge(s_dve, d.value - (1 - b))
                        v.sem_inc(s_vpass, 1)
                        d.add(v.copy_predicated(s_, mask_, count_))
                d.leave(NB // 2)
                own()
                d.add(v.tensor_copy(hi_, s_))
                own()
                d.add(v.tensor_scalar(m_, hi_, P - 1, None, ALU.bitwise_and))
                own()
                d.add(v.tensor_scalar(hi_, hi_, 7, None, ALU.arith_shift_right))
                own()
                d.add(v.scalar_tensor_tensor(out=si, in0=m_, scalar=float(g.chunks), in1=hi_, op0=ALU.mult, op1=ALU.add))

            def buckets_by_chunk(n, g):
                v.wait_ge(s_brow, n + 1)
                for a in range(0, g.chunks, 512):
                    b = min(a + 512, g.chunks)
                    d.add(v.tensor_scalar(brow[0:1, a:b], bank[3 + a // 512][0:1, 0:b - a], float(TILES - 1 if n < 2 else TILES), None, ALU.min))
                own()
                return brow[0:1, 0:g.chunks], brow2[0:1, 0:g.chunks]

            group_edges(0, g0)
            signal(s_slot)
            b, b2 = buckets_by_chunk(0, g0)
            b3 = cum[0:1, 0:g0.chunks]
            d.add(v.tensor_scalar(b2, b, float(A0), None, ALU.mult))
            for k in range(1, 7):
                own()
                d.add(v.tensor_scalar(b3, b, float(k * PB0), float(512 - PB0 * A0), ALU.is_ge, ALU.mult))
                own()
                d.add(v.tensor_tensor(b2, b2, b3, ALU.add))
            own()
            d.add(v.tensor_copy(off0, b2))
            group_edges(1, g1)
            d.add(v.tensor_scalar(py1[0:g1.parts].bitcast(I32)[:, :, 0], key[0][0:g1.parts, 0:g1.cols], float(N - 1), float(W), ALU.min, ALU.add))
            d.add(v.tensor_copy(py1[0:g1.parts, :, 1], lo[0:g1.parts, 0:g1.cols]))
            d.add(v.tensor_copy(py1[0:g1.parts, :, 2], ew[0:g1.parts, 0:g1.cols]))
            signal(s_slot)
            b, _ = buckets_by_chunk(1, g1)
            d.add(v.tensor_scalar(off1, b, float(P), None, ALU.mult))
            group_edges(2, g2)
            d.add(v.tensor_scalar(py2[0:g2.parts].bitcast(I32)[:, :, 0], srcs[0:g2.parts, 0:g2.cols], float(N - 1), None, ALU.min))
            d.add(v.tensor_copy(py2[0:g2.parts, :, 1], lo[0:g2.parts, 0:g2.cols]))
            signal(s_slot)
            b, b2 = buckets_by_chunk(2, g2)
            d.add(v.tensor_scalar(b2, b, float(PB), float(512 - PB * GW), ALU.is_ge, ALU.mult))
            own()
            d.add(v.tensor_scalar(b, b, float(GW), None, ALU.mult))
            own()
            d.add(v.tensor_tensor(off2, b, b2, ALU.add))
            own()

            v.wait_ge(s_pT, 1)
            d.add(v.tensor_copy(flat(pcol[:]), bank[6][:, 0:3 * P]))
            own()
            for c in range(2):
                b1c, gc, bec, mc, vc = (pcol[:, c, a * Q:(a + 1) * Q] for a in range(5))
                scale, shift = bnf[:, c, 0, :], bnf[:, c, 1, :]
                d.add(v.tensor_scalar(root_in[:], vc, BN_EPS_EXPERTS, None, ALU.add))
                own()
                inverse_root(scale, root_in[:], root_part[:])
                d.add(v.tensor_tensor(shift, b1c, mc, ALU.subtract))
                own()
                d.add(v.tensor_tensor(scale, scale, gc, ALU.mult))
                own()
                d.add(v.tensor_tensor(shift, shift, scale, ALU.mult))
                own()
                d.add(v.tensor_tensor(shift, shift, bec, ALU.add))
            signal(s_par)
            v.wait_ge(s_ub, 1)
            d.add(v.tensor_tensor(gb1[:], pcol[:, 2, 0:KG], bank[7][:, 0:KG], ALU.add))
            v.wait_ge(s_w, 16 * weight_loads)
            for c in range(8):
                rows, k = slice(32 * (c % 4), 32 * (c % 4) + 32), c // 4
                for r in range(8):
                    part = r ^ c
                    d.add(v.tensor_scalar(ham[rows, k, 32 * r:32 * r + 32], wrep[rows, 32 * part:32 * part + 32], float(SIGN[r][c]), None, ALU.mult))

            v.wait_ge(s_sd, 16 * 5)
            v.memset(X[:, whole_tiles:TPAD, :], 0.0).then_inc(s_pre, 1)
            d.add(v.memset(acc0, 0.0))
            v.memset(xl3, 0.0).then_inc(s_xl3, 1)
            signal(s_par)

            with v.Fori(0, C0) as i:
                for s in range(2):
                    v.wait_ge(s_bld[s], i * 16 + 16)
                    v.wait_ge(s_mm[s], i * SC + FREE)
                    for c in range(SC):
                        v.tensor_scalar(oh[:, s * SC + c, :], iota[:], oring[:, s * SC + c, EA:EA + 1], None, ALU.is_equal).then_inc(s_oh[s], 1)
            for s in range(2):
                v.wait_ge(s_mm[s], C0 * SC + FREE)
            own()
            for b in range(-(-TILES // PB0)):
                a, z = b * PB0, min((b + 1) * PB0, TILES)
                d.add(v.tensor_copy(acc0[:, a:z, :], bank[1 + b][:, 0:(z - a) * A0].rearrange("p (t w) -> p t w", w=A0)))
            signal(s_add)

            def norm(source, into, done, eps=LN_EPS):
                v.sem_inc(s_vpass, 1)
                for j in range(TG):
                    d.add(v.bn_stats(lnst[:, j, :], source(j)))
                own()
                v.sem_inc(s_vpass, 1)
                for j in range(TG):
                    d.add(v.bn_aggr(lnmv[:, j, :], lnst[:, j, :]))
                own()
                d.add(v.tensor_scalar(root_in[:, 0:TG], lnmv[:, :, 1], eps, None, ALU.add))
                own()
                inverse_root(rstd[:], root_in[:, 0:TG], root_part[:, 0:TG])
                for j in range(TG):
                    d.add(v.tensor_scalar(into[:, j, :], source(j), lnmv[:, j, 0:1], rstd[:, j:j + 1], ALU.subtract, ALU.mult))
                signal(done)
            NORM = 3 * TG + 1 + ROOT

            v.wait_ge(s_xin, 32)
            def dense(part, f, g, hid, y):
                fx = lambda j: tile_at(X, f, j)
                gx = lambda j: tile_at(X, g, j)
                hidden, outs = 0, 0

                def added(kind, e):
                    nonlocal outs
                    for b in range(2):
                        v.wait_ge(s_yp, y(outs + 1))
                        if part != "front" or outs >= 2:
                            v.wait_ge(s_yr, y(outs - 1) + FREE)
                        if kind == "third":
                            for j in range(2):
                                x_ = gx(2 * b + j)
                                ins = v.scalar_tensor_tensor(out=x_, in0=bank[6 + b][:, j * D:(j + 1) * D], scalar=gate[:, 2 * b + j, e:e + 1], in1=x_, op0=ALU.mult, op1=ALU.add)
                        else:
                            x_ = X[:, bass.ds(past(f, TG, 2 * b), 2), :]
                            ins = v.tensor_tensor(x_, x_, bank[6 + b].rearrange("p (t d) -> p t d", d=D), ALU.add)
                        ins.then_inc(s_yr, 1)
                        outs += 1

                if f:
                    norm(fx, xln, s_xln)
                    d.add(v.tensor_scalar(cmx[:], acc0[:, bass.ds(past(f, TG, 0), TG), EA + 1], 1.0, None, ALU.max))
                    own()
                    d.add(v.reciprocal(cmx[:], cmx[:]))
                    own()
                    for j in range(TG):
                        d.add(v.tensor_scalar(attr[:, j, :], tile_at(acc0, f, j)[:, 0:EA], cmx[:, j:j + 1], None, ALU.mult))
                    signal(s_at)
                for kind, e in steps(part):
                    if kind == "turn1":
                        v.wait_ge(s_tr, past(f, 2, 1))
                        v.tensor_copy(xT[:, 1, :], bank[1]).then_inc(s_xTv, 1)
                        v.wait_ge(s_atr, past(f, 1, 1))
                        v.tensor_copy(attrT, bank[2][0:EA, :]).then_inc(s_atT, 1)
                    if kind == "turn2":
                        v.wait_ge(s_tr, past(f, 2, 2))
                        v.tensor_copy(xT[:, 1, :], bank[1]).then_inc(s_xTv, 1)
                    if kind in OUTS:
                        added(kind, e)
                    if kind == "mlp2":
                        v.wait_ge(s_yr, y(outs) + FREE)
                        norm(fx, xln, s_xln)
                    if kind == "logits":
                        v.wait_ge(s_lg, past(f, 1, 1))
                        lg = bank[3][:, 0:TG * NX].rearrange("p (t e) -> p t e", e=NX)
                        d.add(v.tensor_reduce(gmx[:], lg, AX, ALU.max))
                        own()
                        v.tensor_tensor(gate_next[:], lg, gmx[:].unsqueeze(2).broadcast_to([P, TG, NX]), ALU.subtract).then_inc(s_sh, 1)
                        v.wait_ge(s_ex, past(f, 1, 1))
                        d.add(v.tensor_reduce(gsm[:], gate_next[:], AX, ALU.add))
                        own()
                        d.add(v.reciprocal(gsm[:], gsm[:]))
                        own()
                        v.tensor_tensor(gate_next[:], gate_next[:], gsm[:].unsqueeze(2).broadcast_to([P, TG, NX]), ALU.mult).then_inc(s_gt, 1)
                    if kind == "gates":
                        v.wait_ge(s_gtp, past(f, 1, 1))
                        v.tensor_copy(gateT, bank[3][0:NX, :]).then_inc(s_gT, 1)
                    hidden += HIDDEN.get(kind, 0)
                    if kind == "hand":
                        if g:
                            v.wait_ge(s_hp, hid(hidden))
                        v.wait_ge(s_xTa, past(f, 2, 2))
                        v.wait_ge(s_xTv, past(f, 2, 2))
                        v.tensor_copy(flat(xTb), flat(xT)).then_inc(s_xTb, 1)
                if g:
                    v.wait_ge(s_yr, y(outs) + FREE)
                    v.wait_ge(s_xst, past(g, 16, 16))
                    norm(gx, xl3, s_xl3)
                if f:
                    v.wait_ge(s_gt, past(f, 1, 1))
                    d.add(v.tensor_copy(gate[:], gate_next[:]))
                    own()

            def dense_counted(part, f, g, hid, y):
                if part == "both":
                    d.enter(f[0], 3 * NORM + 2 + TG + 3 + 1)
                if part == "back":
                    d.leave(GROUPS - 1)
                dense(part, f, g, hid, y)
            dense_turns(v, dense_counted)
            own()

            d.add(v.memset(big, 0.0))
            with v.Fori(0, C1) as i:
                d.enter(i, 2 * SC)
                for s in range(2):
                    v.wait_ge(s_m1[s], i * 16 + 16)
                    v.wait_ge(s_mm1[s], i * SC + FREE)
                    record = mring[:, s, :].bitcast(F32)
                    for c in range(SC):
                        v.tensor_scalar(oh[:, s * SC + c, :], iota[:], record[:, c * R1 + 1:c * R1 + 2], record[:, c * R1 + 2:c * R1 + 3], ALU.is_equal, ALU.mult).then_inc(s_oh1[s], 1)
                for s in range(2):
                    _, at = nc.values_load_multi_w_load_instructions(off1[:, bass.ds(i * (2 * SC) + s * SC, SC)], engines=DVE_ONLY, min_val=0, max_val=(TILES - 1) * P, skip_runtime_bounds_check_because=CLAMPED)
                    for c in range(SC):
                        if c % 2 == 0:
                            v.wait_ge(s_mm1[s], i * SC + (c + 2) + FREE)
                        own()
                        a = big[:, :, bass.ds(at[c], P)]
                        sums_ = bank[4 * s + c // 2][:, (c % 2) * KD * P:(c % 2 + 1) * KD * P].rearrange("p (k n) -> p k n", k=KD)
                        d.add(v.tensor_tensor(a, a, sums_, ALU.add))
                    signal(s_ad1[s])
            d.leave(C1)

            with v.Fori(0, GROUPS - 1) as i:
                for m in range(KD):
                    v.wait_ge(s_hc, i * KD + (m + 1) + FREE_PAIR)
                    v.sem_inc(s_vpass, 1)
                    v.bn_stats(bst[:, m, bass.ds(i, 1), :].rearrange("p a w -> p (a w)"), big[:, m, bass.ds(i * W, W)]).then_inc(s_hb, 1)
            for m in range(KD):
                v.wait_ge(s_hc, (GROUPS - 1) * KD + m + 1 + FREE_PAIR)
                v.bn_stats(bst[:, m, GROUPS - 1, :], big[:, m, (GROUPS - 1) * W:N]).then_inc(s_hb, 1)
            v.wait_ge(s_hb, GROUPS * KD)
            for m in range(KD):
                d.add(v.bn_aggr(bmv[:, m, :], bst[:, m, :, :].rearrange("p g w -> p (g w)")))
            own()
            gamma, beta = pcol[:, 2, KG + 1:KG + 1 + KD], pcol[:, 2, KG + 1 + KD:KG + 1 + 2 * KD]
            d.add(v.tensor_scalar(root_in[:, 0:KD], bmv[:, :, 1], BN_EPS_GRAPH, None, ALU.add))
            own()
            inverse_root(root_in[:, KD:2 * KD], root_in[:, 0:KD], root_part[:, 0:KD])
            d.add(v.tensor_copy(bsc[:, :, 0], root_in[:, KD:2 * KD]))
            own()
            d.add(v.tensor_tensor(bsc[:, :, 0], bsc[:, :, 0], gamma, ALU.mult))
            own()
            d.add(v.tensor_tensor(bsc[:, :, 1], bmv[:, :, 0], bsc[:, :, 0], ALU.mult))
            own()
            d.add(v.tensor_tensor(bsc[:, :, 1], beta, bsc[:, :, 1], ALU.subtract))
            signal(s_bn)

            d.add(v.memset(nd, 0.0))
            def add_tanh(g):
                v.wait_ge(s_nt, past(g, 1, 1) + FREE)
                for b in range(2):
                    x_ = X[:, bass.ds(past(g, TG, 2 * b), 2), :]
                    v.tensor_tensor(x_, x_, bank[2 + b].rearrange("p (t d) -> p t d", d=D), ALU.add).then_inc(s_ta, 1)
                v.wait_ge(s_ta, past(g, 2, 2))
                if g[0] is not None:
                    v.wait_ge(s_nr, past(g, 1, 0))
                norm(lambda j: tile_at(X, g, j), xln, s_nx)

            def take_projection(g):
                v.wait_ge(s_nh, past(g, 1, 1))
                h = bank[6][:, 0:TG * HK].rearrange("p (t q) -> p t q", q=HK)
                v.tensor_copy(G[:, bass.ds(past(g, TG, 0), TG), HEADS:GW], h).then_inc(s_nhr, 1)

            add_tanh((None, 0))
            with v.Fori(0, GROUPS - 1) as i:
                d.enter(i, NORM)
                add_tanh((i, 1))
                take_projection((i, 0))
            d.leave(GROUPS - 1)
            take_projection((None, GROUPS - 1))
            v.wait_ge(s_nhr, GROUPS + FREE)
            for a, scores in ((0, G), (1, nd)):
                own()
                d.add(v.tensor_tensor(hat, G[:, :, HEADS:GW], att[:, a, :].unsqueeze(1).broadcast_to([P, TPAD, HK]), ALU.mult))
                own()
                d.add(v.tensor_reduce(scores[:, :, 0:HEADS], hat.rearrange("p t (h k) -> p t h k", h=HEADS), AX, ALU.add))
                if a == 0:
                    signal(s_gs)
            d.add(v.tensor_reduce(gmax[:], G[:, 0:TILES - 1, 0:HEADS].rearrange("p t h -> p h t"), AX, ALU.max))
            own()
            d.add(v.tensor_tensor(gmax[0:TAIL, :], gmax[0:TAIL, :], G[0:TAIL, TILES - 1, 0:HEADS], ALU.max))
            signal(s_mxa)
            v.wait_ge(s_mxp, 1)
            d.add(v.tensor_reduce(gm4[:, 0:1], bank[0][0:HEADS, 0:P], AX, ALU.max))
            own()
            d.add(v.tensor_scalar(gm4[:, 1:1 + HEADS], ident[0:HEADS, 0:HEADS], gm4[:, 0:1], None, ALU.mult))
            signal(s_mxa)
            v.wait_ge(s_mxp, 2)
            d.add(v.tensor_copy(gmax[:], bank[0][:, P:P + HEADS]))
            own()
            score, shift = nd[:, 0:TPAD, 0:HEADS], nd[:, 0:TPAD, HEADS:2 * HEADS]
            d.add(v.tensor_tensor(es, score, G[:, :, 0:HEADS], ALU.add))
            d.add(v.tensor_tensor(shift, score, gmax[:].unsqueeze(1).broadcast_to([P, TPAD, HEADS]), ALU.add))
            own()
            d.add(v.scalar_tensor_tensor(out=es, in0=es, scalar=0.2, in1=es, op0=ALU.mult, op1=ALU.max))
            d.add(v.scalar_tensor_tensor(out=shift, in0=shift, scalar=0.2, in1=shift, op0=ALU.mult, op1=ALU.max))
            own()
            d.add(v.tensor_scalar(tmp[0], es, SELF_REACH, None, ALU.add))
            own()
            d.add(v.tensor_tensor(shift, shift, tmp[0], ALU.min))
            own()
            d.add(v.tensor_tensor(es, es, shift, ALU.subtract))
            d.add(v.memset(zero, 0.0))
            signal(s_nd)
            v.wait_ge(s_z2, 2)
            d.add(v.memset(nd3, 0.0))
            for b in range(2):
                z = min(TPAD - b * PB, PB)
                at_place = nd3[:, :, b * 512:b * 512 + z * GW].rearrange("p n (t w) -> p n t w", w=GW)
                three_parts([at_place[:, n, :, 0:2 * HEADS] for n in range(3)], nd[:, b * PB:b * PB + z, :], ndrest[:, 0:z, :])
            d.add(v.tensor_copy(identb[:], ident[:]))
            own()

            def stage_outputs(g, piece):
                for kind, e, b in piece:
                    if kind == "o":
                        v.wait_ge(s_fyp, past(g, 2 * NE, e * 2 + b + 1))
                        v.wait_ge(s_yst[b], past(g, 16 * NE, 16 * e) + FREE)
                        v.tensor_tensor(ystage[b].rearrange("p (t d) -> p t d", d=D), bank[5].rearrange("p (t d) -> p t d", d=D),
                                        fb2[:, e, :].unsqueeze(1).broadcast_to([P, 2, D]), ALU.add).then_inc(s_fyr, 1)

            def edges(i, g, parts):
                for s in range(2):
                    v.wait_ge(s_m2[s], past(i, 16, 16))
                    v.wait_ge(s_a2[s], past(i, SC, 0) + FREE)
                    record = mring[:, s, :].bitcast(F32)
                    for c in range(SC):
                        v.tensor_scalar(ohb[:, s * SC + c, :], iota[:], record[:, c * R2 + 1:c * R2 + 2], None, ALU.is_equal).then_inc(s_oh2[s], 1)
                for s in range(2):
                    stage_outputs(g, parts[s])
                    parts3 = bank[2][:, s * 256:s * 256 + SC * 6 * HEADS].rearrange("p (c n w) -> p c w n", n=3, w=2 * HEADS)
                    row = r2[:, s, :].rearrange("p (c w) -> p c w", w=GW)
                    msg = v2[:, s, :].rearrange("p (c w) -> p c w", w=GW)
                    e = ev[:, s, :].rearrange("p (c h) -> p c h", h=HEADS)
                    v.wait_ge(s_g2[s], past(i, 16 * SC, 16 * SC))
                    v.wait_ge(s_d2[s], past(i, 1, 1))
                    d.add(v.tensor_reduce(at_dst, parts3, AX, ALU.add))
                    own()
                    d.add(v.tensor_tensor(e, row[:, :, 0:HEADS], at_dst[:, :, 0:HEADS], ALU.add))
                    own()
                    d.add(v.scalar_tensor_tensor(out=e, in0=e, scalar=0.2, in1=e, op0=ALU.mult, op1=ALU.max))
                    own()
                    d.add(v.tensor_tensor(e, e, at_dst[:, :, HEADS:2 * HEADS], ALU.subtract))
                    own()
                    d.add(v.tensor_scalar(e, e, SELF_REACH, None, ALU.min))
                    signal(s_e2[s])
                    v.wait_ge(s_x2[s], past(i, 1, 1))
                    d.add(v.tensor_tensor(msg[:, :, HEADS:GW].rearrange("p c (h k) -> p c h k", h=HEADS), row[:, :, HEADS:GW].rearrange("p c (h k) -> p c h k", h=HEADS),
                                          msg[:, :, 0:HEADS].unsqueeze(3).broadcast_to([P, SC, HEADS, HK // HEADS]), ALU.mult))
                    three_parts([v3[:, s, n, :] for n in range(3)], v2[:, s, :], vrest)
                    signal(s_v2[s])
                stage_outputs(g, parts[2])

            EDGES = 2 * (5 + 1 + 4)
            with v.Fori(0, GROUPS) as i:
                d.enter(i, EPG * EDGES)
                for q in range(EPG):
                    edges((i, q, EPG), (i, 0), pieces[q])
            d.leave(GROUPS)
            with v.Fori(0, REST) as i:
                d.enter(i, EDGES)
                edges((i, EPG * GROUPS), None, nothing)
            d.leave(REST)

            for s in range(2):
                v.wait_ge(s_a2[s], C2 * SC + FREE)
            v.wait_ge(s_fx, 1)
            for b in range(-(-TILES // PB)):
                a, z = b * PB, min((b + 1) * PB, TILES)
                d.add(v.tensor_copy(sums[:, a:z, :], sumbank[:, 512 * b:512 * b + (z - a) * GW].rearrange("p (t w) -> p t w", w=GW)))
            den, num = sums[:, :, 0:HEADS], sums[:, :, HEADS:GW]
            by_head = lambda a: a.rearrange("p t (h k) -> p t h k", h=HEADS)
            wide = lambda a: a.unsqueeze(3).broadcast_to([P, TILES, HEADS, HK // HEADS])
            vec = lambda a: att[:, a, :].unsqueeze(1).broadcast_to([P, TILES, HK])
            over16 = lambda a: a.broadcast_to([P, TILES, HK])
            own_e = es[:, 0:TILES, :]
            d.add(v.tensor_tensor(by_head(t16), by_head(G[:, 0:TILES, HEADS:GW]), wide(own_e), ALU.mult))
            own()
            d.add(v.tensor_tensor(den, den, own_e, ALU.add))
            d.add(v.tensor_tensor(num, num, t16, ALU.add))
            own()
            d.add(v.reciprocal(den, den))
            own()
            d.add(v.tensor_tensor(by_head(num), by_head(num), wide(den), ALU.mult))
            own()
            d.add(v.tensor_tensor(num, num, vec(2), ALU.add))
            own()
            m1, m2 = tmp[0][:, 0:TILES, 0:1], tmp[1][:, 0:TILES, 0:1]
            m1s, m2s = tmp[0][:, 0:TILES, 0], tmp[1][:, 0:TILES, 0]
            d.add(v.tensor_reduce(m1s, num, AX, ALU.add))
            own()
            d.add(v.tensor_scalar(m1s, m1s, 1.0 / HK, None, ALU.mult))
            own()
            d.add(v.tensor_tensor(num, num, over16(m1), ALU.subtract))
            own()
            d.add(v.tensor_tensor(t16, num, num, ALU.mult))
            own()
            d.add(v.tensor_reduce(m2s, t16, AX, ALU.add))
            own()
            d.add(v.tensor_scalar(m2s, m2s, 1.0 / HK, LN_EPS, ALU.mult, ALU.add))
            own()
            d.add(v.tensor_copy(roots[:, 0, 0:TILES], m2s))
            own()
            inverse_root(roots[:, 1, 0:TILES], roots[:, 0, 0:TILES], roots[:, 2, 0:TILES])
            d.add(v.tensor_tensor(num, num, roots[:, 1, 0:TILES].unsqueeze(2).broadcast_to([P, TILES, HK]), ALU.mult))
            own()
            d.add(v.tensor_tensor(num, num, vec(3), ALU.mult))
            own()
            d.add(v.tensor_tensor(num, num, vec(4), ALU.add))
            own()
            score, rank, ahead = es[:, 0:TILES, :], tmp[0][:, 0:TILES, :], tmp[1][:, 0:TILES, :]
            d.add(v.tensor_reduce(score, num.rearrange("p t (h k) -> p t k h", h=HEADS), AX, ALU.add))
            own()
            d.add(v.tensor_scalar(score, score, 1.0 / HEADS, None, ALU.mult))
            d.add(v.memset(rank, 0.0))
            own()
            best = tmp[2][:, 0:TILES, 0:1]
            d.add(v.tensor_reduce(tmp[2][:, 0:TILES, 0], score, AX, ALU.max))
            for f in range(NE):
                for a, z, op in ((0, f + 1, ALU.is_gt), (f + 1, NE, ALU.is_ge)):
                    if a < z:
                        d.add(v.tensor_tensor(ahead[:, :, a:z], score[:, :, f:f + 1].broadcast_to([P, TILES, z - a]), score[:, :, a:z], op))
                own()
                d.add(v.tensor_tensor(rank, rank, ahead, ALU.add))
                own()
            d.add(v.tensor_scalar(rank, rank, 1.5, None, ALU.is_lt))
            d.add(v.tensor_tensor(score, score, best.broadcast_to([P, TILES, NE]), ALU.subtract))
            signal(s_fe)
            v.wait_ge(s_fx, 2)
            d.add(v.tensor_tensor(score, score, rank, ALU.mult))
            d.add(v.memset(gates, 0.0))
            own()
            d.add(v.tensor_reduce(tmp[2][:, 0:TILES, 0], score, AX, ALU.add))
            own()
            d.add(v.reciprocal(tmp[2][:, 0:TILES, 0], tmp[2][:, 0:TILES, 0]))
            own()
            d.add(v.tensor_tensor(gates[:, 0:TILES, :], score, best.broadcast_to([P, TILES, NE]), ALU.mult))
            own()
            def combine(g, k, slot):
                v.wait_ge(s_yin[slot], k)
                for e in range(NE):
                    for j in range(TG):
                        v.wait_ge(s_dve, d.value - (TG - 1))
                        x_ = tile_at(X, g, j)
                        gate_ = gates[:, bass.ds(past(g, TG, j), 1), e:e + 1].rearrange("p a e -> p (a e)")
                        d.add(v.scalar_tensor_tensor(out=x_, in0=yring[slot][:, e, j, :], scalar=gate_, in1=x_, op0=ALU.mult, op1=ALU.add))
                signal(s_comb)

            with v.Fori(0, ring_turns) as i:
                d.enter(i, YR * NE * TG)
                for slot in range(YR):
                    combine((i, slot, YR), i * 16 + 16, slot)
            d.leave(ring_turns)
            combine((None, GROUPS - 1), 16 * ring_turns + 16, 0)

        @block.scalar
        def _(a):
            load = lambda dst, src: a.dma_start(dst, src).then_inc(s_w, 16)
            for dst, src in weights:
                load(dst, src)
            a.wait_ge(s_fillv, 3)
            for dst, src in param_rows:
                load(dst, src)
            a.wait_ge(s_fill[0], 16 * FILLS[0])
            for dst, src in late_weights:
                load(dst, src)
            a.wait_ge(s_slot, 1)
            for s in range(2):
                a.activation(aring[0:g0.parts, s, :, EA], lo0[0:g0.parts, s * SS:(s + 1) * SS], ACT.Copy).then_inc(s_loc[s], 1)
            with a.Fori(0, ITERS[0] - 1) as i:
                for s in range(2):
                    a.wait_ge(s_sc[s], i * (16 * SS) + 16 * SS)
                    a.activation(aring[0:g0.parts, s, :, EA], lo0[0:g0.parts, bass.ds(i * (2 * SS) + (2 + s) * SS, SS)], ACT.Copy).then_inc(s_loc[s], 1)
            for s in range(2):
                a.wait_ge(s_sc[s], 16 * SS * ITERS[0])
            a.wait_ge(s_sd, 16 * 5)
            with a.Fori(0, C0) as i:
                for s in range(2):
                    a.wait_ge(s_mm[s], i * SC + FREE)
                    a.dma_start(flat(oring[:, s * SC:(s + 1) * SC, :]), r0v[:, bass.ds((i * 2 + s) * (SC * A0), SC * A0)]).then_inc(s_bld[s], 16)
            a.wait_ge(s_par, 2)
            def dense(part, f, g, hid, y):
                hidden = 0

                def take(into, func, bias, scale=1.0):
                    nonlocal hidden
                    a.wait_ge(s_hp, hid(hidden + 1))
                    a.activation(into, bank[4 + hidden % 2], func, bias=bias, scale=scale).then_inc(s_hr, 1)
                    hidden += 1

                for kind, e in steps(part):
                    if kind in ("turn1", "turn2"):
                        a.wait_ge(s_tr, past(f, 2, int(kind[-1])))
                        a.activation(xT[:, 0, :], bank[0], ACT.Copy).then_inc(s_xTa, 1)
                    if kind == "mlp1":
                        for m in range(KG):
                            take(HG[:, m, :], ACT.Relu, gb1[:, m:m + 1])
                    if (kind, e) == ("third", 1) and g:
                        store_tokens(g)
                    if kind in ("first", "second"):
                        c = BACK.index(kind)
                        for m in range(KD):
                            q = e * KD + m
                            take(HB[:, 4 * c + (e % 2) * KD + m, :], ACT.Relu, bnf[:, c, 1, q:q + 1], bnf[:, c, 0, q:q + 1])
                    if kind == "logits":
                        a.wait_ge(s_sh, past(f, 1, 1))
                        a.activation(gate_next[:], gate_next[:], ACT.Exp).then_inc(s_ex, 1)

            def store_tokens(g):
                a.wait_ge(s_xl3, past(g, 1, 1))
                a.dma_start(xl_d[bass.ds(past(g, W, 0), W), :].rearrange("(t p) d -> p t d", p=P), xl3).then_inc(s_xst, 16)

            dense_turns(a, dense)
            store_tokens((None, GROUPS))
            assert GROUPS % 2 == 1

            def take_octonion(g, pair):
                a.wait_ge(s_hm, past(g, KD, KD))
                for m in range(KD):
                    a.activation(big[:, m, bass.ds(past(g, W, 0), W)], bank[pair * KD + m], ACT.Copy).then_inc(s_hc, 1)

            with a.Fori(0, GROUPS // 2) as i:
                for pair in range(2):
                    take_octonion((i, pair, 2), pair)
            take_octonion((None, GROUPS - 1), 0)
            a.wait_ge(s_bn, 1)
            a.wait_ge(s_hc, GROUPS * KD + FREE_PAIR)

            def tanh(g):
                a.wait_ge(s_nt, past(g, 1, 0) + FREE)
                for k in range(KD):
                    a.activation(HB[:, k, :], big[:, k, bass.ds(past(g, W, 0), W)], ACT.Tanh, bias=bsc[:, k, 1:2], scale=bsc[:, k, 0:1]).then_inc(s_th, 1)

            def copy_tokens(g):
                a.wait_ge(s_nr, past(g, 1, 1))
                for k in range(KD):
                    a.activation(xT[:, k, :], bank[4 + k], ACT.Copy).then_inc(s_nca, 1)
                for k in range(KD):
                    a.activation(big[:, k, bass.ds(past(g, W, 0), W)], bank[4 + k], ACT.Copy).then_inc(s_nb, 1)

            tanh((None, 0))
            with a.Fori(0, GROUPS - 1) as i:
                tanh((i, 1))
                copy_tokens((i, 0))
            copy_tokens((None, GROUPS - 1))
            a.wait_ge(s_nd, 1)
            a.activation(es, es, ACT.Exp).then_inc(s_fx, 1)
            bias4 = pcol[:, 2, KG + 1 + 2 * KD:KG + 1 + 2 * KD + NE * KF]

            def take_piece(g, piece, pending):
                for kind, e, m in piece:
                    if kind == "h":
                        u = e * KF + m
                        a.wait_ge(s_fhp, past(g, NE * KF, u + 1))
                        a.activation(HB[:, (e % 2) * KF + m, :], bank[3 + u % 2], ACT.Gelu, bias=bias4[:, u:u + 1]).then_inc(s_fhr, 1)
                    else:
                        store_outputs(g, pending)
                        pending.append((e, m))

            def store_outputs(g, pending):
                for e, b in pending:
                    a.wait_ge(s_fyr, past(g, 2 * NE, e * 2 + b + 1) + FREE)
                    a.dma_start(y_d[bass.ds(past(g, P, 0), P), (e * 2 + b) * 2 * D:(e * 2 + b + 1) * 2 * D], ystage[b]).then_inc(s_yst[b], 16)
                pending.clear()

            def edges(i, g, parts):
                pending = []
                take_piece(g, parts[0][:1], pending)
                for s in range(2):
                    a.wait_ge(s_t2[s], past(i, 1, 1))
                    a.activation(flat(ohT[:, s * SC:(s + 1) * SC, :]), bank[s].bitcast(BF16), ACT.Copy).then_inc(s_c2[s], 1)
                    if s == 1:
                        exp(i, 0)
                    take_piece(g, parts[s][1 - s:], pending)
                exp(i, 1)
                take_piece(g, parts[2], pending)
                if pending:
                    store_outputs(g, pending)

            def exp(i, s):
                a.wait_ge(s_e2[s], past(i, 1, 1))
                a.wait_ge(s_a2[s], past(i, SC, 0) + FREE)
                a.activation(v2[:, s, :].rearrange("p (c w) -> p c w", w=GW)[:, :, 0:HEADS], ev[:, s, :].rearrange("p (c h) -> p c h", h=HEADS), ACT.Exp).then_inc(s_x2[s], 1)

            edge_turns(a, edges)
            a.wait_ge(s_fe, 1)
            a.activation(es[:, 0:TILES, :], es[:, 0:TILES, :], ACT.Exp).then_inc(s_fx, 1)

        @block.tensor
        def _(pe):
            pe.wait_ge(s_const, 9)
            for n, g in enumerate(graphs):
                pp, NB = g.parts, g.buckets
                pe.wait_ge(s_cnt, n + 1)
                pe.matmul(bank[0][0:NB, 0:1], cnt[0:pp, 0:NB], ones[0:pp, 0:1], start=True, stop=True).then_inc(s_tot, 1)
                pe.wait_ge(s_nch, n + 1)
                pe.matmul(bank[1][0:pp, 0:NB], before[0:pp, 0:pp], cnt[0:pp, 0:NB], start=True, stop=False)
                pe.matmul(bank[1][0:pp, 0:NB], nrep[0:NB, 0:pp], before[0:NB, 0:NB], start=False, stop=True)
                pe.matmul(bank[2][0:NB, 0:1], upto[0:NB, 0:NB], nch[0:NB, 1:2], start=True, stop=True).then_inc(s_base, 1)
                pe.wait_ge(s_cmp, n + 1)
                for c in range(0, g.chunks, 512):
                    z = min(c + 512, g.chunks)
                    mm = pe.matmul(bank[3 + c // 512][0:1, 0:z - c], ones[0:NB, 0:1], ends[0:NB, c:z], start=True, stop=True)
                mm.then_inc(s_brow, 1)
            pe.wait_ge(s_w, 16 * weight_loads)
            for c in range(3):
                mm = pe.transpose(bank[6][:, c * P:(c + 1) * P], prow[:, c, :], ident[:])
            mm.then_inc(s_pT, 1)
            pe.wait_ge(s_par, 1)
            for m in range(KG):
                mm = pe.matmul(bank[7][:, m:m + 1], gw1u[:, m * P:(m + 1) * P], pcol[:, 2, KG:KG + 1], start=True, stop=True)
            mm.then_inc(s_ub, 1)

            pe.wait_ge(s_par, 2)
            for b in range(1, 8):
                pe.matmul(bank[b], zero_l0, zero_r0, start=True, stop=False, skip_group_check=True)
            with pe.Fori(0, C0) as i:
                for s in range(2):
                    _, at = nc.values_load_multi_w_load_instructions(off0[:, bass.ds(i * (2 * SC) + s * SC, SC)], engines=PE_ONLY, min_val=0, max_val=7 * 512 - A0, skip_runtime_bounds_check_because=CLAMPED)
                    pe.wait_ge(s_bld[s], i * 16 + 16)
                    for c in range(SC):
                        pe.wait_ge(s_oh[s], i * SC + (c + 1))
                        pe.matmul(sumbank0[:, bass.ds(at[c], A0)], oh[:, s * SC + c, :], oring[:, s * SC + c, :], start=False, stop=False, skip_group_check=True).then_inc(s_mm[s], 1)

            def turn(source, banks, j0=0):
                for k in range(KD):
                    for j in range(TG):
                        mm = pe.transpose(banks[k][:, j * P:(j + 1) * P], source[:, j, k * P:(k + 1) * P], ident[:])
                return mm

            pe.wait_ge(s_add, 1)
            cols = lambda j: slice(j * P, (j + 1) * P)

            def dense(part, f, g, hid, y):
                hidden, outs = 0, 0
                after = {("first", 0): 0}

                def into_hidden(products):
                    nonlocal hidden
                    if part != "front" or hidden >= 2:
                        pe.wait_ge(s_hr, hid(hidden - 1) + FREE)
                    for n, (w_, x_) in enumerate(products):
                        mm = pe.matmul(bank[4 + hidden % 2], w_, x_, start=(n == 0), stop=(n == len(products) - 1))
                    mm.then_inc(s_hp, 1)
                    hidden += 1

                def into_outputs(products):
                    nonlocal outs
                    for b in range(2):
                        if part != "front" or outs >= 2:
                            pe.wait_ge(s_yr, y(outs - 1) + FREE)
                        for j in range(2):
                            ps = products(2 * b + j)
                            for n, (x_, w_) in enumerate(ps):
                                mm = pe.matmul(bank[6 + b][:, j * D:(j + 1) * D], x_, w_, start=(n == 0), stop=(n == len(ps) - 1))
                        mm.then_inc(s_yp, 1)
                        outs += 1

                for kind, e in steps(part):
                    if kind == "turn1":
                        pe.wait_ge(s_xln, past(f, 2, 1))
                        turn(xln, bank[0:2]).then_inc(s_tr, 1)
                        pe.wait_ge(s_at, past(f, 1, 1))
                        pe.sem_inc(s_ppass, 1)
                        for j in range(TG):
                            mm = pe.transpose(bank[2][0:EA, cols(j)], attr[:, j, :], ident[:])
                        mm.then_inc(s_atr, 1)
                    if kind == "mlp1":
                        pe.wait_ge(s_xTa, past(f, 2, 1))
                        pe.wait_ge(s_xTv, past(f, 2, 1))
                        pe.wait_ge(s_atT, past(f, 1, 1))
                        for m in range(KG):
                            into_hidden([(gw1[:, k, cols(m)], xT[:, k, :]) for k in range(KD)] + [(gw1e[:, cols(m)], attrT)])
                    if kind == "mlp2":
                        pe.wait_ge(s_hr, hid(after["mlp1", 0]) + FREE)
                        into_outputs(lambda j: [(ones[0:1, :], gb2r)] + [(HG[:, m, cols(j)], gw2[:, m, :]) for m in range(KG)])
                    if kind == "turn2":
                        pe.wait_ge(s_xln, past(f, 2, 2))
                        turn(xln, bank[0:2]).then_inc(s_tr, 1)
                    if kind == "logits":
                        pe.wait_ge(s_xTa, past(f, 2, 2))
                        pe.wait_ge(s_xTv, past(f, 2, 2))
                        for j in range(TG):
                            for k in range(KD):
                                pe.matmul(bank[3][:, j * NX:(j + 1) * NX], xT[:, k, cols(j)], wr[:, k, :], start=(k == 0), stop=False)
                            mm = pe.matmul(bank[3][:, j * NX:(j + 1) * NX], ones[0:1, :], brr, start=False, stop=True)
                        mm.then_inc(s_lg, 1)
                    if kind == "gates":
                        pe.wait_ge(s_gt, past(f, 1, 1))
                        for j in range(TG):
                            mm = pe.transpose(bank[3][0:NX, cols(j)], gate_next[:, j, :], ident[:])
                        mm.then_inc(s_gtp, 1)
                    if kind == "bias":
                        pe.wait_ge(s_gT, past(f, 1, 1))
                        into_outputs(lambda j: [(gateT[:, cols(j)], bo)])
                    if kind == "first":
                        if e == 0:
                            pe.wait_ge(s_xTb, past(f, 1, 1))
                        for m in range(KD):
                            into_hidden([(EW1[:, e, k, cols(m)], xTb[:, k, :]) for k in range(KD)])
                    if kind == "second":
                        pe.wait_ge(s_hr, hid(after["first", e]) + FREE)
                        for m in range(KD):
                            into_hidden([(EW2[:, e, k, cols(m)], HB[:, (e % 2) * KD + k, :]) for k in range(KD)])
                    if kind == "third":
                        pe.wait_ge(s_hr, hid(after["second", e]) + FREE)
                        into_outputs(lambda j: [(HB[:, 4 + (e % 2) * KD + k, cols(j)], EWo[:, e, k, :]) for k in range(KD)])
                    after[kind, e] = hidden
                assert part != "both" or (hidden, outs) == (HP, YP)

            dense_turns(pe, dense)

            pe.wait_ge(s_yr, GROUPS * YP + FREE)
            with pe.Fori(0, C1) as i:
                for s in range(2):
                    pe.wait_ge(s_g1[s], i * (16 * SC) + 16 * SC)
                    pe.wait_ge(s_ad1[s], i + FREE)
                    for c in range(SC):
                        pe.wait_ge(s_oh1[s], i * SC + (c + 1))
                        for k in range(KD):
                            at = (c % 2) * KD * P + k * P
                            mm = pe.matmul(bank[4 * s + c // 2][:, at:at + P], rows1[:, s * SC + c, k * P:(k + 1) * P], oh[:, s * SC + c, :], start=True, stop=True)
                        mm.then_inc(s_mm1[s], 1)
            for s in range(2):
                pe.wait_ge(s_ad1[s], C1 + FREE)
            def octonion(g, pair):
                pe.wait_ge(s_hc, past(g, KD, 0) + FREE)
                for m in range(KD):
                    for k in range(KD):
                        mm = pe.matmul(bank[pair * KD + m], ham[:, k, m * P:(m + 1) * P], big[:, k, bass.ds(past(g, W, 0), W)], start=(k == 0), stop=(k == KD - 1))
                    mm.then_inc(s_hm, 1)

            with pe.Fori(0, GROUPS // 2) as i:
                for pair in range(2):
                    octonion((i, pair, 2), pair)
            octonion((None, GROUPS - 1), 0)
            def tanh_back(g):
                pe.wait_ge(s_th, past(g, KD, KD))
                for j in range(TG):
                    for k in range(KD):
                        mm = pe.transpose(bank[2 + j // 2][:, (j % 2) * D + k * P:(j % 2) * D + (k + 1) * P], HB[:, k, j * P:(j + 1) * P], ident[:])
                mm.then_inc(s_nt, 1)

            def project(g, next_group):
                if next_group:
                    pe.wait_ge(s_ta, past(g, 2, 2))
                    tanh_back(next_group)
                pe.wait_ge(s_nx, past(g, 1, 1))
                pe.wait_ge(s_nb, past(g, KD, 0) + FREE)
                turn(xln, bank[4:6]).then_inc(s_nr, 1)
                pe.wait_ge(s_nca, past(g, KD, KD))
                pe.wait_ge(s_nhr, past(g, 1, 0) + FREE)
                for j in range(TG):
                    for k in range(KD):
                        mm = pe.matmul(bank[6][:, j * HK:(j + 1) * HK], xT[:, k, j * P:(j + 1) * P], wg[:, k, :], start=(k == 0), stop=(k == KD - 1))
                mm.then_inc(s_nh, 1)

            tanh_back((None, 0))
            with pe.Fori(0, GROUPS - 1) as i:
                project((i, 0), (i, 1))
            project((None, GROUPS - 1), None)
            pe.wait_ge(s_nb, GROUPS * KD + FREE)
            pe.wait_ge(s_mxa, 1)
            pe.transpose(bank[0][0:HEADS, 0:P], gmax[:], ident[:]).then_inc(s_mxp, 1)
            pe.wait_ge(s_mxa, 2)
            pe.matmul(bank[0][:, P:P + HEADS], ones[0:HEADS, :], gm4[:, 1:1 + HEADS], start=True, stop=True).then_inc(s_mxp, 1)

            pe.wait_ge(s_nd, 1)
            for b in range(2):
                pe.matmul(bank[6 + b], zero_l, zero_r, start=True, stop=False, skip_group_check=True).then_inc(s_z2, 1)
            pe.wait_ge(s_w4, 48)


            def experts4(g, piece):
                for kind, e, m in piece:
                    if kind == "h":
                        u = e * KF + m
                        pe.wait_ge(s_fhr, past(g, NE * KF, max(u - 1, 0)) + FREE)
                        for k in range(KD):
                            mm = pe.matmul(bank[3 + u % 2], FW1[:, e, k, m * P:(m + 1) * P], big[:, k, bass.ds(past(g, W, 0), W)], start=(k == 0), stop=(k == KD - 1))
                        mm.then_inc(s_fhp, 1)
                    else:
                        pe.wait_ge(s_fhr, past(g, NE * KF, (e + 1) * KF) + FREE)
                        pe.wait_ge(s_fyr, past(g, 2 * NE, e * 2 + m) + FREE)
                        for j in range(2):
                            for k in range(KF):
                                mm = pe.matmul(bank[5][:, j * D:(j + 1) * D], HB[:, (e % 2) * KF + k, (2 * m + j) * P:(2 * m + j + 1) * P], FW2[:, e, k, :], start=(k == 0), stop=(k == KF - 1))
                        mm.then_inc(s_fyp, 1)

            def transposes(i, s):
                pe.wait_ge(s_c2[s], past(i, 1, 0) + FREE)
                for c in range(SC):
                    pe.wait_ge(s_oh2[s], past(i, SC, c + 1))
                    mm = pe.transpose(bank[s].bitcast(BF16)[:, c * P:(c + 1) * P], ohb[:, s * SC + c, :], identb[:])
                mm.then_inc(s_t2[s], 1)

            def places(i, s):
                _, at = nc.values_load_multi_w_load_instructions(off2[:, bass.ds(past(i, 2 * SC, s * SC), SC)], engines=PE_ONLY, min_val=0, max_val=2 * 512 - GW, skip_runtime_bounds_check_because=CLAMPED)
                return at

            def destinations(i, s, at):
                pe.wait_ge(s_c2[s], past(i, 1, 1) + FREE)
                pe.wait_ge(s_v2[s], past(i, 1, 0) + FREE)
                for c in range(SC):
                    mm = pe.matmul(bank[2][:, s * 256 + c * 6 * HEADS:s * 256 + (c + 1) * 6 * HEADS], ohT[:, s * SC + c, :], nd3[:, :, bass.ds(at[c], 2 * HEADS)], start=True, stop=True)
                mm.then_inc(s_d2[s], 1)

            def add_messages(i, s, at):
                pe.wait_ge(s_v2[s], past(i, 1, 1) + FREE)
                for c in range(SC):
                    for n in range(3):
                        mm = pe.matmul(sumbank[:, bass.ds(at[c], GW)], ohb[:, s * SC + c, :], v3[:, s, n, c * GW:(c + 1) * GW], start=False, stop=False, skip_group_check=True)
                    mm.then_inc(s_a2[s], 1)

            def edges(i, g, parts):
                experts4(g, parts[0][:1])
                transposes(i, 0)
                experts4(g, parts[0][1:])
                places0 = places(i, 0)
                destinations(i, 0, places0)
                transposes(i, 1)
                experts4(g, parts[1])
                places1 = places(i, 1)
                add_messages(i, 0, places0)
                destinations(i, 1, places1)
                experts4(g, parts[2])
                add_messages(i, 1, places1)

            edge_turns(pe, edges)


def kernel(**inputs):
    import numpy as _np
    import concourse.bacc as _bacc
    from concourse.bass_utils import run_bass_kernel_spmd as _run

    nc = _bacc.Bacc("TRN2", target_bir_lowering=False, num_devices=1)
    arrays, args = {}, {}
    for name, value in inputs.items():
        a = _np.ascontiguousarray(value)
        arrays[f"in_{name}"] = a
        args[name] = nc.dram_tensor(f"in_{name}", a.shape, mybir.dt.from_np(a.dtype), kind="ExternalInput").ap()
    shape = args["x"].shape
    result = nc.dram_tensor("out_x", shape, F32, kind="ExternalOutput").ap()
    build(nc, args, result)
    r = _run(nc, [arrays], core_ids=[0])
    return r.results[0]["out_x"]
```
